# Optimizing a Trainium2 kernel written in Bass

```python
import numpy as np
import jax
import jax.numpy as jnp

def _softmax(x, axis=-1):
    return jax.nn.softmax(x, axis=axis)

def _gelu(x):
    return jax.nn.gelu(x, approximate=True)

def _silu(x):
    return jax.nn.silu(x)

def _sigmoid(x):
    return jax.nn.sigmoid(x)

def _layernorm(x, axis=-1, eps=1e-05):
    m = jnp.mean(x, axis=axis, keepdims=True)
    v = jnp.var(x, axis=axis, keepdims=True)
    return (x - m) / jnp.sqrt(v + eps)

def _scatter_add(tgt, idx, src, axis=0):
    return tgt.at[idx].add(src)

def _segment_sum(src, seg, n):
    return jax.ops.segment_sum(src, seg, n)
kernel_name = 'mk_seq_preln_d2_jaxref_r8_eeae5a'

def setup_inputs(seed: int=0):
    np.random.seed(seed)
    _w = jnp.asarray

    def _L0_attn_setup():
        import jax, jax.numpy as jnp
        import numpy as np
        B, T, D_DENSE = (4, 256, 128)
        SPARSE = 128
        NH = 8
        HD = SPARSE // NH
        K = 32
        WIN = 64
        RANK = HD // 4
        key = jax.random.key(seed)
        ks = jax.random.split(key, 8)
        n = lambda k, shape, scale=1.0: jax.random.normal(k, shape, dtype=jnp.float32) * scale
        return {'x': n(ks[0], (B, T, D_DENSE)), 'encoder_query': n(ks[1], (NH, D_DENSE, HD), 0.02), 'encoder_value': n(ks[2], (NH, D_DENSE, HD), 0.02), 'mn_w1': n(ks[3], (SPARSE, SPARSE // 2), 1.0 / np.sqrt(SPARSE)), 'mn_b1': jnp.zeros((SPARSE // 2,), jnp.float32), 'mn_w2': n(ks[4], (SPARSE // 2, NH * HD), 1.0 / np.sqrt(SPARSE // 2)), 'mn_b2': jnp.zeros((NH * HD,), jnp.float32), 'base_metric': jnp.ones((NH, HD), jnp.float32) * 0.1, 'decoder': n(ks[5], (NH * HD, D_DENSE), 0.02), 'hebbian_U': n(ks[6], (NH, HD, RANK), 0.01), 'hebbian_V': n(ks[7], (NH, RANK, HD), 0.01)}
    _L0_attn_in = _L0_attn_setup()

    def _L0_ffn_setup():
        import jax, jax.numpy as jnp
        import numpy as np
        S, B, H = (256, 1, 128)
        N_HEADS = 16
        HEAD_DIM = H // N_HEADS
        E, K, F = (8, 2, 256)
        EPS = 1e-05

        def layernorm(x, w, b):
            mu = jnp.mean(x, axis=-1, keepdims=True)
            var = jnp.mean(jnp.square(x - mu), axis=-1, keepdims=True)
            return (x - mu) * jax.lax.rsqrt(var + EPS) * w + b
        key = jax.random.key(seed)
        ks = jax.random.split(key, 8)
        std = 0.02
        return {'x': jax.random.normal(ks[0], (S, B, H), dtype=jnp.float32), 'ln1_w': jnp.ones((H,), jnp.float32), 'ln1_b': jnp.zeros((H,), jnp.float32), 'in_proj_w': jax.random.normal(ks[1], (3 * H, H), jnp.float32) * std, 'in_proj_b': jnp.zeros((3 * H,), jnp.float32), 'out_proj_w': jax.random.normal(ks[2], (H, H), jnp.float32) * std, 'out_proj_b': jnp.zeros((H,), jnp.float32), 'ln2_w': jnp.ones((H,), jnp.float32), 'ln2_b': jnp.zeros((H,), jnp.float32), 'router_w': jax.random.normal(ks[3], (E, H), jnp.float32) * std, 'w1': jax.random.normal(ks[4], (E, H, F), jnp.float32) * std, 'w2': jax.random.normal(ks[5], (E, F, H), jnp.float32) * std}
    _L0_ffn_in = _L0_ffn_setup()

    def _L1_attn_setup():
        import jax, jax.numpy as jnp
        import numpy as np
        B, N, D, H = (2, 256, 128, 8)
        HD = D // H
        EPS = 1e-06

        def _interleave(a, b):
            return jnp.stack([a, b], axis=2).reshape(a.shape[0], 2 * a.shape[1], a.shape[2], a.shape[3])

        def _l2norm(x):
            return x / jnp.sqrt(jnp.sum(x * x, axis=-1, keepdims=True) + EPS)

        def _dense_rnn(x, Wq, Wk, Wv, Wf1, Wf2, Wbeta, Wog1, Wog2, norm_w, Wo):
            b, n, d = x.shape
            q = jax.nn.silu(x @ Wq)
            k = jax.nn.silu(x @ Wk)
            v = jax.nn.silu(x @ Wv)
            f = x @ Wf1 @ Wf2
            log_f = jax.nn.log_sigmoid(f)
            beta = jax.nn.sigmoid(x @ Wbeta) * 2.0
            shp = (b, n, H, HD)
            q, k, v, log_f = (t.reshape(shp) for t in (q, k, v, log_f))
            k = _l2norm(k)
            k_ = -beta[..., None] * k
            zero = jnp.zeros(shp, x.dtype)
            gk = _interleave(log_f, zero)
            a = _interleave(k_ * jnp.exp(log_f), k_)
            bb = _interleave(k, k)
            kk = _interleave(zero, k)
            vv = _interleave(zero, v)
            qq = _interleave(zero, q)
            seq = tuple((jnp.moveaxis(t, 1, 0) for t in (gk, a, bb, kk, vv, qq)))
            S0 = jnp.zeros((b, H, HD, HD), x.dtype)

            def step(S, inp):
                g, a_t, b_t, k_t, v_t, q_t = inp
                bS = jnp.einsum('bhk,bhkv->bhv', b_t, S)
                S = jnp.exp(g)[..., None] * S + a_t[..., None] * bS[:, :, None, :] + k_t[..., None] * v_t[:, :, None, :]
                o = jnp.einsum('bhk,bhkv->bhv', q_t, S)
                return (S, o)
            _, o = jax.lax.scan(step, S0, seq)
            o = jnp.moveaxis(o, 0, 1)[:, 1::2]
            out = o.reshape(b, n, d)
            gate = x @ Wog1 @ Wog2
            y = out * jax.nn.sigmoid(gate)
            yh = y.reshape(b, n, H, HD)
            yh = yh / jnp.sqrt(jnp.mean(yh * yh, axis=-1, keepdims=True) + EPS)
            y = yh.reshape(b, n, d) * norm_w
            return y @ Wo
        key = jax.random.key(seed)
        ks = jax.random.split(key, 11)
        std = 0.02
        w = lambda k, shape: jax.random.normal(k, shape, dtype=jnp.float32) * std
        return {'x': jax.random.normal(ks[0], (B, N, D), dtype=jnp.float32), 'Wq': w(ks[1], (D, D)), 'Wk': w(ks[2], (D, D)), 'Wv': w(ks[3], (D, D)), 'Wf1': w(ks[4], (D, HD)), 'Wf2': w(ks[5], (HD, D)), 'Wbeta': w(ks[6], (D, H)), 'Wog1': w(ks[7], (D, HD)), 'Wog2': w(ks[8], (HD, D)), 'norm_w': jnp.ones((D,), dtype=jnp.float32), 'Wo': w(ks[9], (D, D))}
    _L1_attn_in = _L1_attn_setup()

    def _L1_ffn_setup():
        import jax, jax.numpy as jnp
        import numpy as np
        TOP_K = 2
        SHARED_SCALE = 0.5

        def _swiglu(x, wg, wu, wd):
            return jax.nn.silu(x @ wg) * (x @ wu) @ wd
        key = jax.random.key(seed)
        ks = jax.random.split(key, 8)
        B, S, H, I, E = (4, 256, 128, 512, 8)
        s = 0.02
        return {'hidden_states': jax.random.normal(ks[0], (B, S, H), jnp.float32), 'Wr': jax.random.normal(ks[1], (H, E), jnp.float32) * s, 'Wg': jax.random.normal(ks[2], (E, H, I), jnp.float32) * s, 'Wu': jax.random.normal(ks[3], (E, H, I), jnp.float32) * s, 'Wd': jax.random.normal(ks[4], (E, I, H), jnp.float32) * s, 'Sg': jax.random.normal(ks[5], (H, I // 2), jnp.float32) * s, 'Su': jax.random.normal(ks[6], (H, I // 2), jnp.float32) * s, 'Sd': jax.random.normal(ks[7], (I // 2, H), jnp.float32) * s}
    _L1_ffn_in = _L1_ffn_setup()
    _d = {'L0_attn_x': _L0_attn_in['x'], 'L0_attn_encoder_query': _L0_attn_in['encoder_query'], 'L0_attn_encoder_value': _L0_attn_in['encoder_value'], 'L0_attn_mn_w1': _L0_attn_in['mn_w1'], 'L0_attn_mn_b1': _L0_attn_in['mn_b1'], 'L0_attn_mn_w2': _L0_attn_in['mn_w2'], 'L0_attn_mn_b2': _L0_attn_in['mn_b2'], 'L0_attn_base_metric': _L0_attn_in['base_metric'], 'L0_attn_decoder': _L0_attn_in['decoder'], 'L0_attn_hebbian_U': _L0_attn_in['hebbian_U'], 'L0_attn_hebbian_V': _L0_attn_in['hebbian_V'], 'L0_ffn_ln1_w': _L0_ffn_in['ln1_w'], 'L0_ffn_ln1_b': _L0_ffn_in['ln1_b'], 'L0_ffn_in_proj_w': _L0_ffn_in['in_proj_w'], 'L0_ffn_in_proj_b': _L0_ffn_in['in_proj_b'], 'L0_ffn_out_proj_w': _L0_ffn_in['out_proj_w'], 'L0_ffn_out_proj_b': _L0_ffn_in['out_proj_b'], 'L0_ffn_ln2_w': _L0_ffn_in['ln2_w'], 'L0_ffn_ln2_b': _L0_ffn_in['ln2_b'], 'L0_ffn_router_w': _L0_ffn_in['router_w'], 'L0_ffn_w1': _L0_ffn_in['w1'], 'L0_ffn_w2': _L0_ffn_in['w2'], 'L1_attn_Wq': _L1_attn_in['Wq'], 'L1_attn_Wk': _L1_attn_in['Wk'], 'L1_attn_Wv': _L1_attn_in['Wv'], 'L1_attn_Wf1': _L1_attn_in['Wf1'], 'L1_attn_Wf2': _L1_attn_in['Wf2'], 'L1_attn_Wbeta': _L1_attn_in['Wbeta'], 'L1_attn_Wog1': _L1_attn_in['Wog1'], 'L1_attn_Wog2': _L1_attn_in['Wog2'], 'L1_attn_norm_w': _L1_attn_in['norm_w'], 'L1_attn_Wo': _L1_attn_in['Wo'], 'L1_ffn_Wr': _L1_ffn_in['Wr'], 'L1_ffn_Wg': _L1_ffn_in['Wg'], 'L1_ffn_Wu': _L1_ffn_in['Wu'], 'L1_ffn_Wd': _L1_ffn_in['Wd'], 'L1_ffn_Sg': _L1_ffn_in['Sg'], 'L1_ffn_Su': _L1_ffn_in['Su'], 'L1_ffn_Sd': _L1_ffn_in['Sd']}
    _x0 = _d['L0_attn_x']
    _d['L0_attn_x'] = jax.random.normal(jax.random.fold_in(jax.random.key(seed), 1), (8, 256, 128), dtype=_x0.dtype)
    del _x0
    return _d

def reference(L0_attn_x, L0_attn_encoder_query, L0_attn_encoder_value, L0_attn_mn_w1, L0_attn_mn_b1, L0_attn_mn_w2, L0_attn_mn_b2, L0_attn_base_metric, L0_attn_decoder, L0_attn_hebbian_U, L0_attn_hebbian_V, L0_ffn_ln1_w, L0_ffn_ln1_b, L0_ffn_in_proj_w, L0_ffn_in_proj_b, L0_ffn_out_proj_w, L0_ffn_out_proj_b, L0_ffn_ln2_w, L0_ffn_ln2_b, L0_ffn_router_w, L0_ffn_w1, L0_ffn_w2, L1_attn_Wq, L1_attn_Wk, L1_attn_Wv, L1_attn_Wf1, L1_attn_Wf2, L1_attn_Wbeta, L1_attn_Wog1, L1_attn_Wog2, L1_attn_norm_w, L1_attn_Wo, L1_ffn_Wr, L1_ffn_Wg, L1_ffn_Wu, L1_ffn_Wd, L1_ffn_Sg, L1_ffn_Su, L1_ffn_Sd):

    def _L0_attn_ref(x, encoder_query, encoder_value, mn_w1, mn_b1, mn_w2, mn_b2, base_metric, decoder, hebbian_U, hebbian_V):
        import jax, jax.numpy as jnp
        import numpy as np
        B, T, D_DENSE = (4, 256, 128)
        SPARSE = 128
        NH = 8
        HD = SPARSE // NH
        K = 32
        WIN = 64
        RANK = HD // 4
        Bv, Tv, _ = x.shape
        q = jax.nn.relu(jnp.einsum('btd,nde->btne', x, encoder_query))
        v = jax.nn.relu(jnp.einsum('btd,nde->btne', x, encoder_value))
        qflat = q.reshape(Bv, Tv, -1)
        sig = qflat.mean(axis=1)
        if Tv >= 8:
            sig = sig + qflat[:, ::8].mean(axis=1) * 0.5
        hidden = jax.nn.gelu(sig @ mn_w1 + mn_b1, approximate=False)
        mod = (hidden @ mn_w2 + mn_b2).reshape(Bv, NH, HD)
        metric = jax.nn.softplus(base_metric[None] + 0.1 * mod)
        pos = jnp.arange(Tv)
        offs = jnp.arange(0, -WIN, -1)
        idx = jnp.clip(pos[:, None] + offs[None, :], 0, Tv - 1)
        mask = idx <= pos[:, None]
        k_act = min(K, WIN)
        batch_ix = jnp.arange(Bv)[:, None, None]
        outs = []
        for h in range(NH):
            q_h = q[:, :, h, :]
            v_h = v[:, :, h, :]
            kw = q_h[:, idx, :]
            diff = kw - q_h[:, :, None, :]
            wsq = diff * diff * metric[:, h][:, None, None, :]
            dist = jnp.sqrt(wsq.sum(-1) + 1e-08)
            dist = jnp.where(mask[None], dist, jnp.inf)
            neg, loc = jax.lax.top_k(-dist, k_act)
            topd = -neg
            topi = jnp.take_along_axis(jnp.broadcast_to(idx[None], (Bv, Tv, WIN)), loc, axis=2)
            infl = jnp.exp(-topd)
            infl = infl / (infl.sum(-1, keepdims=True) + 1e-08)
            nv = v_h[batch_ix, topi]
            context = jnp.einsum('btk,btkd->btd', infl, nv)
            q_norm = jnp.linalg.norm(q_h, axis=-1, keepdims=True)
            gate = (q_norm > 0.2).astype(q_h.dtype)
            Hm = hebbian_U[h] @ hebbian_V[h]
            qhat = q_h / jnp.maximum(q_norm, 1e-12)
            context = context + gate * 0.1 * (qhat @ Hm)
            outs.append(q_h * context)
        out_sparse = jnp.stack(outs, axis=2).reshape(Bv, Tv, -1)
        return out_sparse @ decoder

    def _L0_ffn_ref(x, ln1_w, ln1_b, in_proj_w, in_proj_b, out_proj_w, out_proj_b, ln2_w, ln2_b, router_w, w1, w2):
        import jax, jax.numpy as jnp
        import numpy as np
        S, B, H = (256, 1, 128)
        N_HEADS = 16
        HEAD_DIM = H // N_HEADS
        E, K, F = (8, 2, 256)
        EPS = 1e-05

        def layernorm(x, w, b):
            mu = jnp.mean(x, axis=-1, keepdims=True)
            var = jnp.mean(jnp.square(x - mu), axis=-1, keepdims=True)
            return (x - mu) * jax.lax.rsqrt(var + EPS) * w + b
        s, b, h = x.shape
        hn = layernorm(x, ln1_w, ln1_b)
        qkv = hn @ in_proj_w.T + in_proj_b
        q, k, v = jnp.split(qkv, 3, axis=-1)
        q = q.reshape(s, b, N_HEADS, HEAD_DIM)
        k = k.reshape(s, b, N_HEADS, HEAD_DIM)
        v = v.reshape(s, b, N_HEADS, HEAD_DIM)
        scores = jnp.einsum('sbnd,tbnd->bnst', q, k) / np.sqrt(HEAD_DIM)
        causal = jnp.tril(jnp.ones((s, s), bool))
        scores = jnp.where(causal[None, None], scores, -jnp.inf)
        probs = jax.nn.softmax(scores, axis=-1)
        attn = jnp.einsum('bnst,tbnd->sbnd', probs, v).reshape(s, b, h)
        attn = attn @ out_proj_w.T + out_proj_b
        x1 = x + attn
        hn2 = layernorm(x1, ln2_w, ln2_b).reshape(s * b, h)
        logits = hn2 @ router_w.T
        rp = jax.nn.softmax(logits, axis=-1)
        topw, topi = jax.lax.top_k(rp, K)
        gates = jnp.sum(jax.nn.one_hot(topi, E, dtype=hn2.dtype) * topw[..., None], axis=1)
        hmid = jax.nn.gelu(jnp.einsum('th,ehf->tef', hn2, w1), approximate=False)
        y = jnp.einsum('tef,efh->th', hmid * gates[:, :, None], w2)
        return x1 + y.reshape(s, b, h)

    def _L1_attn_ref(x, Wq, Wk, Wv, Wf1, Wf2, Wbeta, Wog1, Wog2, norm_w, Wo):
        import jax, jax.numpy as jnp
        import numpy as np
        B, N, D, H = (2, 256, 128, 8)
        HD = D // H
        EPS = 1e-06

        def _interleave(a, b):
            return jnp.stack([a, b], axis=2).reshape(a.shape[0], 2 * a.shape[1], a.shape[2], a.shape[3])

        def _l2norm(x):
            return x / jnp.sqrt(jnp.sum(x * x, axis=-1, keepdims=True) + EPS)

        def _dense_rnn(x, Wq, Wk, Wv, Wf1, Wf2, Wbeta, Wog1, Wog2, norm_w, Wo):
            b, n, d = x.shape
            q = jax.nn.silu(x @ Wq)
            k = jax.nn.silu(x @ Wk)
            v = jax.nn.silu(x @ Wv)
            f = x @ Wf1 @ Wf2
            log_f = jax.nn.log_sigmoid(f)
            beta = jax.nn.sigmoid(x @ Wbeta) * 2.0
            shp = (b, n, H, HD)
            q, k, v, log_f = (t.reshape(shp) for t in (q, k, v, log_f))
            k = _l2norm(k)
            k_ = -beta[..., None] * k
            zero = jnp.zeros(shp, x.dtype)
            gk = _interleave(log_f, zero)
            a = _interleave(k_ * jnp.exp(log_f), k_)
            bb = _interleave(k, k)
            kk = _interleave(zero, k)
            vv = _interleave(zero, v)
            qq = _interleave(zero, q)
            seq = tuple((jnp.moveaxis(t, 1, 0) for t in (gk, a, bb, kk, vv, qq)))
            S0 = jnp.zeros((b, H, HD, HD), x.dtype)

            def step(S, inp):
                g, a_t, b_t, k_t, v_t, q_t = inp
                bS = jnp.einsum('bhk,bhkv->bhv', b_t, S)
                S = jnp.exp(g)[..., None] * S + a_t[..., None] * bS[:, :, None, :] + k_t[..., None] * v_t[:, :, None, :]
                o = jnp.einsum('bhk,bhkv->bhv', q_t, S)
                return (S, o)
            _, o = jax.lax.scan(step, S0, seq)
            o = jnp.moveaxis(o, 0, 1)[:, 1::2]
            out = o.reshape(b, n, d)
            gate = x @ Wog1 @ Wog2
            y = out * jax.nn.sigmoid(gate)
            yh = y.reshape(b, n, H, HD)
            yh = yh / jnp.sqrt(jnp.mean(yh * yh, axis=-1, keepdims=True) + EPS)
            y = yh.reshape(b, n, d) * norm_w
            return y @ Wo
        return _dense_rnn(x, Wq, Wk, Wv, Wf1, Wf2, Wbeta, Wog1, Wog2, norm_w, Wo)

    def _L1_ffn_ref(hidden_states, Wr, Wg, Wu, Wd, Sg, Su, Sd):
        import jax, jax.numpy as jnp
        import numpy as np
        TOP_K = 2
        SHARED_SCALE = 0.5

        def _swiglu(x, wg, wu, wd):
            return jax.nn.silu(x @ wg) * (x @ wu) @ wd
        B, S, H = hidden_states.shape
        E = Wr.shape[1]
        flat = hidden_states.reshape(-1, H)
        logits = flat @ Wr
        probs = jax.nn.softmax(logits, axis=-1)
        top_vals, top_idx = jax.lax.top_k(probs, TOP_K)
        combine = (jax.nn.one_hot(top_idx, E, dtype=probs.dtype) * top_vals[..., None]).sum(axis=1)
        out = jnp.zeros_like(flat)
        for e in range(E):
            out = out + _swiglu(flat, Wg[e], Wu[e], Wd[e]) * combine[:, e:e + 1]
        out = out + SHARED_SCALE * _swiglu(flat, Sg, Su, Sd)
        return out.reshape(B, S, H)
    x = L0_attn_x
    x = x + _L0_attn_ref(_layernorm(x, axis=-1), L0_attn_encoder_query, L0_attn_encoder_value, L0_attn_mn_w1, L0_attn_mn_b1, L0_attn_mn_w2, L0_attn_mn_b2, L0_attn_base_metric, L0_attn_decoder, L0_attn_hebbian_U, L0_attn_hebbian_V)
    x = x + _L0_ffn_ref(_layernorm(x, axis=-1), L0_ffn_ln1_w, L0_ffn_ln1_b, L0_ffn_in_proj_w, L0_ffn_in_proj_b, L0_ffn_out_proj_w, L0_ffn_out_proj_b, L0_ffn_ln2_w, L0_ffn_ln2_b, L0_ffn_router_w, L0_ffn_w1, L0_ffn_w2)
    x = x + _L1_attn_ref(_layernorm(x, axis=-1), L1_attn_Wq, L1_attn_Wk, L1_attn_Wv, L1_attn_Wf1, L1_attn_Wf2, L1_attn_Wbeta, L1_attn_Wog1, L1_attn_Wog2, L1_attn_norm_w, L1_attn_Wo)
    x = x + _L1_ffn_ref(_layernorm(x, axis=-1), L1_ffn_Wr, L1_ffn_Wg, L1_ffn_Wu, L1_ffn_Wd, L1_ffn_Sg, L1_ffn_Su, L1_ffn_Sd)
    return x

_drawn_inputs = setup_inputs


def setup_inputs(seed=0):
    import zlib

    import numpy as np

    out = dict(_drawn_inputs(seed))
    spreads = {'L0_attn_mn_b1': (0.0, 0.8),
     'L0_attn_mn_b2': (0.0, 2.0),
     'L0_attn_base_metric': (0.10000000149011612, 0.6),
     'L0_ffn_ln1_w': (1.0, 0.6),
     'L0_ffn_ln1_b': (0.0, 0.8),
     'L0_ffn_in_proj_b': (0.0, 0.611),
     'L0_ffn_out_proj_b': (0.0, 0.1),
     'L0_ffn_ln2_w': (1.0, 0.6),
     'L0_ffn_ln2_b': (0.0, 0.8),
     'L1_attn_norm_w': (1.0, 0.6)}
    factors = {'L0_attn_encoder_query': 8.0,
     'L0_attn_encoder_value': 8.0,
     'L0_attn_mn_w1': 8.0,
     'L0_attn_mn_w2': 8.0,
     'L0_attn_decoder': 8.0,
     'L0_attn_hebbian_U': 27.029,
     'L0_attn_hebbian_V': 29.065,
     'L0_ffn_in_proj_w': 3.283,
     'L0_ffn_router_w': 8.0,
     'L0_ffn_w1': 8.0,
     'L0_ffn_w2': 8.0,
     'L1_attn_Wf1': 8.0,
     'L1_attn_Wf2': 8.0,
     'L1_attn_Wbeta': 23.59,
     'L1_attn_Wog1': 8.0,
     'L1_attn_Wog2': 8.0,
     'L1_ffn_Wr': 8.0,
     'L1_ffn_Wg': 8.0,
     'L1_ffn_Wu': 8.0,
     'L1_ffn_Wd': 8.0,
     'L1_ffn_Sg': 8.0,
     'L1_ffn_Su': 8.0,
     'L1_ffn_Sd': 8.0}
    for name, (base, spread) in spreads.items():
        noise = np.random.default_rng([zlib.crc32(name.encode()), seed]).standard_normal(out[name].shape)
        drawn = base * np.exp(spread * noise) if base else spread * noise
        out[name] = jnp.asarray(drawn.astype(out[name].dtype))
    for name, factor in factors.items():
        out[name] = (out[name] * factor).astype(out[name].dtype)
    return out
```

```python
import math
from contextlib import ExitStack

import concourse.bass as bass
import numpy as np
from concourse import mybir

F32 = mybir.dt.float32
BF16 = mybir.dt.bfloat16
ALU = mybir.AluOpType
ACT = mybir.ActivationFunctionType
AX = mybir.AxisListType

P = 128
B, T = 8, 256
NT = B * T
BLK = 512
NBLK = NT // BLK
BB = BLK // T
HD = 16
NHEAD = P // HD
LN_EPS = 1e-5


class Mem:

    def __init__(self, nc):
        self.nc, self.semaphores = nc, []

    def sem(self, name):
        self.semaphores.append(self.nc.alloc_semaphore(name))
        return self.semaphores[-1]

    def release(self):
        self.nc.clear_and_free_semaphores(self.semaphores)
        self.nc.all_engine_barrier()
        self.semaphores = []


def cols(n, width=BLK):
    return slice(n * width, (n + 1) * width)


def load_all(nc, m, name, loads):
    w_loaded = m.sem(name + "_loaded")
    with nc.Block() as block:
        @block.sync
        def _(sp):
            for dst, src in loads:
                sp.dma_start(dst, src).then_inc(w_loaded, 16)
            sp.wait_ge(w_loaded, 16 * len(loads))


def layernorm(nc, m, name, src, dst, weight=None, bias=None):
    with ExitStack() as ctx:
        xc = ctx.enter_context(nc.sbuf_tensor(f"{name}_centred", [P, NT], F32))
        sq = ctx.enter_context(nc.sbuf_tensor(f"{name}_squares", [P, NT], F32))
        rstd = ctx.enter_context(nc.sbuf_tensor(f"{name}_rstd", [P, NT], F32))
        mean_done, centred, squared, var_done, logged, rstd_done, normed, scaled = (
            m.sem(f"{name}_{s}")
            for s in ("mean", "centred", "squared", "var", "log", "rstd", "normed", "scaled"))
        block = ctx.enter_context(nc.Block())

        @block.tensor
        def _(pe):
            for n in range(NBLK):
                nc.tensor.matmul(m.ps[n][:, :], m.avg[:, :], src[:, cols(n)],
                                 start=True, stop=True).then_inc(mean_done, 1)
            for n in range(NBLK):
                pe.wait_ge(squared, n + 1)
                nc.tensor.matmul(m.ps[NBLK + n][:, :], m.avg[:, :], sq[:, cols(n)],
                                 start=True, stop=True).then_inc(var_done, 1)

        @block.scalar
        def _(act):
            for n in range(NBLK):
                act.wait_ge(centred, n + 1)
                nc.scalar.activation(sq[:, cols(n)], xc[:, cols(n)], ACT.Square).then_inc(squared, 1)
            for n in range(NBLK):
                act.wait_ge(var_done, n + 1)
                nc.scalar.activation(rstd[:, cols(n)], m.ps[NBLK + n][:, :], ACT.Ln,
                                     bias=m.eps[:, 0:1]).then_inc(logged, 1)
                act.wait_ge(logged, n + 1)
                nc.scalar.activation(rstd[:, cols(n)], rstd[:, cols(n)], ACT.Exp, scale=-0.5).then_inc(rstd_done, 1)

        @block.vector
        def _(dve):
            for n in range(NBLK):
                dve.wait_ge(mean_done, n + 1)
                nc.vector.tensor_tensor(xc[:, cols(n)], src[:, cols(n)], m.ps[n][:, :],
                                        ALU.subtract).then_inc(centred, 1)
            for n in range(NBLK):
                dve.wait_ge(centred, n + 1)
                dve.wait_ge(rstd_done, n + 1)
                nc.vector.tensor_tensor(dst[:, cols(n)], xc[:, cols(n)], rstd[:, cols(n)],
                                        ALU.mult).then_inc(normed, 1)
                if weight is not None:
                    dve.wait_ge(normed, n + 1)
                    nc.vector.tensor_scalar(dst[:, cols(n)], dst[:, cols(n)], weight, bias,
                                            ALU.mult, ALU.add).then_inc(scaled, 1)


PAD = 64
WIN = 64
TOPK = 32
QT = 32
KT = QT + WIN
HG = 4
NQT = T // QT
GT = 4
NG = NQT * (NHEAD // HG) // GT
HALF = HG * HD
ROUNDS = TOPK // 8
TAKEN = -3.0e38
OUTSIDE = -1.0e15
GATE2 = float(0.2) ** 2
NORM_SCALE = 2.0 ** 30


class Tally:

    def __init__(self, m, name, units, per=1, credit=0):
        self.sem = m.sem(name)
        self.units, self.per, self.credit = units, per, credit * per

    def done(self, step, unit, j=None):
        j = self.per - 1 if j is None else j
        return step * (self.units * self.per) + (unit * self.per + self.credit + j + 1)


def give_credit(pool, tallies):
    for t in tallies:
        if t.credit:
            pool.sem_inc(t.sem, t.credit)


def distance_queries(nc, m, w, z, qpad, metric):
    with ExitStack() as ctx:
        def sb(name, shape):
            return ctx.enter_context(nc.sbuf_tensor(name, shape, F32))

        def sem(name):
            return m.sem(name)

        total, every8, sig = sb("a_total", [P, B]), sb("a_every8", [P, B]), sb("a_sig", [P, B])
        hidden, arg, size, tail = sb("a_hidden", [P // 2, B]), sb("a_arg", [P, B]), sb("a_size", [P, B]), sb("a_tail", [P, B])
        base01 = sb("a_base01", [P, 1])
        q_done, relu_done, sums, sig_done, hid_done, gelu_done, mod_done, arg_done, size_done, act_done, based = map(
            sem, ("a_q", "a_relu", "a_sums", "a_sigd", "a_hid", "a_gelu", "a_mod", "a_argd", "a_sized", "a_act", "a_based"))
        hm_done, hm_copied = sem("a_hm"), sem("a_hmc")
        block = ctx.enter_context(nc.Block())

        @block.tensor
        def _(pe):
            for n in range(NBLK):
                nc.tensor.matmul(m.ps[n][:, :], w["encoder_query"], z[:, cols(n)], start=True, stop=True).then_inc(q_done, 1)
            nc.tensor.matmul(m.ps[5][:, 0:P], w["hebbian_U"], w["hebbian_V"], start=True, stop=True).then_inc(hm_done, 1)
            pe.wait_ge(sig_done, 1)
            nc.tensor.matmul(m.ps[4][0:P // 2, 0:B], w["mn_w1"], sig[:, :], start=True, stop=True).then_inc(hid_done, 1)
            pe.wait_ge(gelu_done, 1)
            nc.tensor.matmul(m.ps[6][:, 0:B], w["mn_w2"], hidden[:, :], start=True, stop=True).then_inc(mod_done, 1)

        @block.scalar
        def _(act):
            for n in range(NBLK):
                act.wait_ge(q_done, n + 1)
                nc.scalar.activation(qpad[:, n * BB:(n + 1) * BB, PAD:], m.ps[n][:, :].rearrange("p (b t) -> p b t", b=BB),
                                     ACT.Relu).then_inc(relu_done, 1)
            act.wait_ge(hm_done, 1)
            nc.scalar.copy(w["hebbian"], m.ps[5][:, 0:P]).then_inc(hm_copied, 1)
            act.wait_ge(hid_done, 1)
            nc.scalar.activation(hidden[:, :], m.ps[4][0:P // 2, 0:B], ACT.Gelu, bias=w["mn_b1"]).then_inc(gelu_done, 1)
            act.wait_ge(size_done, 1)
            nc.scalar.activation(tail[:, :], size[:, :], ACT.Exp, scale=-1.0).then_inc(act_done, 1)
            act.wait_ge(act_done, 1)
            nc.scalar.activation(tail[:, :], tail[:, :], ACT.Ln, bias=m.eps[:, 4:5]).then_inc(act_done, 1)

        @block.gpsimd
        def _(pool):
            for n in range(NBLK):
                pool.wait_ge(relu_done, n + 1)
                for b in range(n * BB, (n + 1) * BB):
                    nc.gpsimd.tensor_copy(qpad[:, b, 0:PAD], qpad[:, b, PAD:PAD + 1].to_broadcast([P, PAD]))

        @block.vector
        def _(dve):
            for n in range(NBLK):
                bs = slice(n * BB, (n + 1) * BB)
                dve.wait_ge(relu_done, n + 1)
                nc.vector.tensor_reduce(total[:, bs], qpad[:, bs, PAD:], AX.X, ALU.add).then_inc(sums, 1)
                nc.vector.tensor_reduce(every8[:, bs], qpad[:, bs, PAD:PAD + T:8], AX.X, ALU.add).then_inc(sums, 1)
            dve.wait_ge(sums, 2 * NBLK)
            nc.vector.tensor_scalar(every8[:, :], every8[:, :], 0.5 * 8 / T, None, ALU.mult).then_inc(sums, 1)
            dve.wait_ge(sums, 2 * NBLK + 1)
            nc.vector.scalar_tensor_tensor(sig[:, :], total[:, :], 1.0 / T, every8[:, :], ALU.mult, ALU.add).then_inc(sig_done, 1)
            nc.vector.scalar_tensor_tensor(base01[:, :], w["mn_b2"], 0.1, w["base_metric"], ALU.mult, ALU.add).then_inc(based, 1)
            dve.wait_ge(mod_done, 1)
            dve.wait_ge(based, 1)
            nc.vector.tensor_scalar(arg[:, :], m.ps[6][:, 0:B], 0.1, base01[:, :], ALU.mult, ALU.add).then_inc(arg_done, 1)
            dve.wait_ge(arg_done, 1)
            nc.vector.scalar_tensor_tensor(size[:, :], arg[:, :], -1.0, arg[:, :], ALU.mult, ALU.max).then_inc(size_done, 1)
            dve.wait_ge(act_done, 2)
            nc.vector.scalar_tensor_tensor(metric[:, :], arg[:, :], 0.0, tail[:, :], ALU.max, ALU.add).then_inc(arg_done, 1)
            dve.wait_ge(arg_done, 2)


def distance_attention(nc, m, w, z, qpad, metric):
    with ExitStack() as ctx:
        def sb(name, shape, n=2):
            return [ctx.enter_context(nc.sbuf_tensor(f"{name}{i}", shape, F32)) for i in range(n)]

        def tally(name, per=1, credit=0):
            return Tally(m.sem("b_" + name), per, credit)

        xp = sb("b_xp", [P, PAD + T])
        q2m, mk2 = sb("b_q2m", [P, T]), sb("b_mk2", [P, PAD + T])
        keys = [sb(f"b_keys{i}", [P, PAD + T]) for i in range(2)]
        lhs = [sb(f"b_lhs{i}", [P, NQT, HG, QT]) for i in range(2)]
        vwin = sb("b_vwin", [KT, NQT, NHEAD // HG, HALF + 1])
        qsq, n2c, inv, gate, heb, ctxt, outb = (sb("b_" + s, [P, T], 1)[0] for s in (
            "qsq", "n2c", "inv", "gate", "heb", "ctxt", "outb"))
        metric2 = sb("b_metric2", [P, B], 1)[0]
        top = [sb(f"b_top{r}_", [P, GT, 8]) for r in range(ROUNDS)]
        left, weight, dist = sb("b_left", [P, GT, KT]), sb("b_weight", [P, GT, KT]), sb("b_dist", [P, GT, KT])
        value, (spare, spare_act) = sb("b_value", [P, GT, KT]), sb("b_spare", [P, 12])
        weightT = sb("b_weightT", [KT, GT * P])
        rden, chead = sb("b_rden", [P, GT]), sb("b_chead", [P, GT, HALF])

        tallies = []

        def tally(name, units, per=1, credit=0):
            tallies.append(Tally(m, "b_" + name, units, per, credit))
            return tallies[-1]

        S, G = 2, 2 * NG
        t_xp, t_q2m, t_mk2 = tally("xp", S, 2), tally("q2m", S), tally("mk2", S)
        t_keys, t_lhs, t_vps, t_vw = tally("keys", S, 4, 2), tally("lhs", S, 2, 2), tally("vps", S, 2, 2), tally("vw", S, 2, 1)
        t_qsq, t_nh, t_n2c, t_inv = tally("qsq", S), tally("nh", S, 1, 1), tally("n2c", S, 2), tally("inv", S, 2)
        t_heb, t_ctx, t_out, t_dec, t_x = (tally("heb", S, 2, 1), tally("ctx", S, 1, 1), tally("out", S),
                                           tally("dec", S, 1, 1), tally("x", S, 1, 1))
        t_score, t_top, t_taken, t_self = (tally("score", G, 1, 4), tally("top", G, GT),
                                           tally("taken", G, GT), tally("self", G, GT))
        t_value, t_step = tally("value", G, 1, 2), m.sem("b_step")
        t_log, t_dist, t_infl, t_weight = tally("log", G), tally("dist", G), tally("infl", G), tally("weight", G, 1, 2)
        t_tr, t_wT, t_cx, t_rden, t_chead, t_cxT = (tally("tr", G, 1, 2), tally("wT", G, 1, 1), tally("cx", G, 1, 8),
                                                    tally("rden", G, 2), tally("chead", G, GT, 1), tally("cxT", G, 1, 2))
        b_score, b_v, b_tr, b_cx, b_cxT, b_nh, b_dec = [m.ps[0], m.ps[1]], m.ps[2], m.ps[3], m.ps[4], m.ps[5], m.ps[6], m.ps[7]

        preset = m.sem("b_preset")
        with nc.Block() as block:
            @block.gpsimd
            def _(pool):
                for i in range(2):
                    nc.gpsimd.memset(vwin[i][:, :, :, HALF:HALF + 1], 1.0).then_inc(preset, 1)
                pool.wait_ge(preset, 2)
                for i in range(2):
                    for hg in range(2):
                        sq = slice(HALF * (1 - hg), HALF * (2 - hg))
                        nc.gpsimd.tensor_scalar(lhs[hg][i][sq, :, :, :],
                                                m.hmask[sq, :].unsqueeze(1).unsqueeze(3).to_broadcast([HALF, NQT, HG, QT]),
                                                -1.0, None, ALU.mult).then_inc(preset, 1)
                        pool.wait_ge(preset, 2 * i + hg + 3)
                give_credit(pool, tallies)

            @block.vector
            def _(dve):
                nc.vector.tensor_scalar(metric2[:, :], metric[:, :], 2.0, None, ALU.mult)

        block = ctx.enter_context(nc.Block())

        def wait(eng, t, step, unit, j=None):
            eng.wait_ge(t.sem, t.done(step, unit, j))

        def column(a, b):
            return a[:, bass.ds(b, 1)]

        def queries(b, start=PAD, n=T):
            return qpad[:, bass.ds(b, 1), start:start + n].rearrange("p o t -> p (o t)")

        @block.gpsimd
        def _(pool):
            with pool.Fori(0, B // 2) as step:
                for i in range(2):
                    b = step * 2 + i
                    wait(pool, t_vps, step, i - 2)
                    nc.gpsimd.tensor_copy(xp[i][:, PAD:], z[:, bass.ds(b * T, T)]).then_inc(t_xp.sem, 1)
                    nc.gpsimd.tensor_copy(xp[i][:, 0:PAD], z[:, bass.ds(b * T, 1)].to_broadcast([P, PAD])).then_inc(t_xp.sem, 1)
                    wait(pool, t_q2m, step, i)
                    wait(pool, t_score, step, NG * (i - 1) - 1)
                    wait(pool, t_xp, step, i)
                    for hg in range(2):
                        own = slice(HALF * hg, HALF * (hg + 1))
                        nc.gpsimd.tensor_tensor(
                            lhs[hg][i][own, :, :, :],
                            q2m[i][own, :].rearrange("p (w q) -> p w q", q=QT).unsqueeze(2).to_broadcast([HALF, NQT, HG, QT]),
                            m.hmask[own, :].unsqueeze(1).unsqueeze(3).to_broadcast([HALF, NQT, HG, QT]),
                            ALU.mult).then_inc(t_lhs.sem, 1)
                    wait(pool, t_lhs, step, i)

        @block.tensor
        def _(pe):
            def scores(step, i, g):
                hg, w0 = g // (NG // 2), g % (NG // 2) * GT
                bank = b_score[g % 2]
                wait(pe, t_value, step, i * NG + g - 2)
                if g == 0:
                    wait(pe, t_keys, step, i)
                    wait(pe, t_lhs, step, i)
                for t in range(GT):
                    q0 = (w0 + t) * QT
                    nc.tensor.matmul(bank[:, t * KT:(t + 1) * KT], m.identb[:, :], m.band[:, :], start=True, stop=False)
                    mm = nc.tensor.matmul(bank[:, t * KT:(t + 1) * KT],
                                          lhs[hg][i][:, w0 + t, :, :].rearrange("p h q -> p (h q)"),
                                          keys[hg][i][:, q0:q0 + KT], start=False, stop=True)
                mm.then_inc(t_score.sem, 1)

            def values(step, i):
                wait(pe, t_xp, step, i)
                for half in range(2):
                    wait(pe, t_vw, step, i, half - 1)
                    for t in range(NQT // 2):
                        q0 = (half * (NQT // 2) + t) * QT
                        mm = nc.tensor.matmul(b_v[0:KT, t * P:(t + 1) * P], xp[i][:, q0:q0 + KT],
                                              w["encoder_value"], start=True, stop=True)
                    mm.then_inc(t_vps.sem, 1)

            def context(step, i, g):
                unit = i * NG + g
                hg, w0 = g // (NG // 2), g % (NG // 2) * GT
                wait(pe, t_weight, step, unit)
                wait(pe, t_wT, step, unit - 1)
                for t in range(GT):
                    mm = nc.tensor.transpose(b_tr[0:KT, t * P:(t + 1) * P], weight[g % 2][:, t, :], m.ident[:, :])
                mm.then_inc(t_tr.sem, 1)
                wait(pe, t_wT, step, unit)
                wait(pe, t_chead, step, unit - 1)
                if g == 0:
                    wait(pe, t_vw, step, i)
                for t in range(GT):
                    mm = nc.tensor.matmul(b_cx[:, t * P:t * P + HALF + 1], weightT[g % 2][:, t * P:(t + 1) * P],
                                          vwin[i][:, w0 + t, hg, :], start=True, stop=True)
                mm.then_inc(t_cx.sem, 1)
                wait(pe, t_chead, step, unit)
                if g == 0:
                    wait(pe, t_ctx, step, i - 1)
                for t in range(GT):
                    q0 = (w0 + t) * QT
                    mm = nc.tensor.matmul(b_cxT[HALF * hg:HALF * (hg + 1), q0:q0 + QT], chead[g % 2][:, t, :],
                                          m.qsel[:, :], start=True, stop=True)
                mm.then_inc(t_cxT.sem, 1)

            with pe.Fori(0, B // 2) as step:
                for i in range(2):
                    if i == 0:
                        scores(step, i, 0)
                    values(step, i)
                    wait(pe, t_qsq, step, i)
                    wait(pe, t_heb, step, i - 1)
                    nc.tensor.matmul(b_nh[:, 0:T], m.headsum[:, :], qsq[:, :], start=True, stop=True)
                    nc.tensor.matmul(b_nh[:, T:2 * T], w["hebbian"], queries(step * 2 + i),
                                     start=True, stop=True).then_inc(t_nh.sem, 1)
                    for g in range(NG):
                        if g < NG - 1:
                            scores(step, i, g + 1)
                        elif i == 0:
                            scores(step, 1, 0)
                        context(step, i, g)
                    wait(pe, t_out, step, i)
                    wait(pe, t_x, step, i - 1)
                    nc.tensor.matmul(b_dec[:, 0:T], w["decoder"], outb[:, :], start=True, stop=True).then_inc(t_dec.sem, 1)

        @block.scalar
        def _(act):
            def sequence_inputs(step, i):
                b = step * 2 + i
                wait(act, t_lhs, step, i - 2)
                nc.scalar.copy(spare_act[:, 2 * i:2 * i + 1], m.eps[:, 0:1])
                nc.scalar.activation(q2m[i][:, :], queries(b), ACT.Copy, scale=column(metric2, b)).then_inc(t_q2m.sem, 1)
                wait(act, t_score, step, NG * (i - 1) - 1)
                wait(act, t_mk2, step, i)
                for hg in range(2):
                    own, sq = slice(HALF * hg, HALF * (hg + 1)), slice(HALF * (1 - hg), HALF * (2 - hg))
                    nc.scalar.copy(keys[hg][i][own, :], qpad[own, bass.ds(b, 1), :].rearrange("p o t -> p (o t)")
                                   ).then_inc(t_keys.sem, 1)
                    nc.scalar.copy(keys[hg][i][sq, :], mk2[i][own, :]).then_inc(t_keys.sem, 1)
                wait(act, t_nh, step, i - 1)
                nc.scalar.copy(spare_act[:, 2 * i + 1:2 * i + 2], m.eps[:, 0:1])
                nc.scalar.activation(qsq[:, :], queries(b), ACT.Square).then_inc(t_qsq.sem, 1)

            def value_windows(step, i, half):
                wait(act, t_vps, step, i, half)
                wait(act, t_cx, step, i * NG - NG - 1)
                w0 = half * (NQT // 2)
                nc.scalar.activation(vwin[i][:, w0:w0 + NQT // 2, :, 0:HALF],
                                     b_v[0:KT, :].rearrange("k (w g e) -> k w g e", w=NQT // 2, g=2),
                                     ACT.Relu).then_inc(t_vw.sem, 1)

            def distances(step, i, g):
                unit, d = i * NG + g, dist[g % 2]
                wait(act, t_score, step, unit)
                wait(act, t_weight, step, unit - 2)
                nc.scalar.copy(value[g % 2][:, :, :], b_score[g % 2][:, 0:GT * KT].rearrange("p (t k) -> p t k", t=GT)
                               ).then_inc(t_value.sem, 1)
                wait(act, t_value, step, unit)
                for t in range(GT):
                    wait(act, t_top, step, unit, t)
                    nc.scalar.activation(d[:, t, :], value[g % 2][:, t, :], ACT.Identity,
                                         scale=-1.0, bias=top[0][g % 2][:, t, 0:1]).then_inc(t_self.sem, 1)
                wait(act, t_self, step, unit)
                nc.scalar.activation(d[:, :, :], d[:, :, :], ACT.Ln, bias=m.eps[:, 2:3]).then_inc(t_log.sem, 1)
                wait(act, t_log, step, unit)
                nc.scalar.activation(d[:, :, :], d[:, :, :], ACT.Exp, scale=0.5).then_inc(t_dist.sem, 1)
                wait(act, t_dist, step, unit)
                nc.scalar.activation(d[:, :, :], d[:, :, :], ACT.Exp, scale=-1.0).then_inc(t_infl.sem, 1)

            def transposed(step, i, g):
                wait(act, t_tr, step, i * NG + g)
                wait(act, t_cx, step, i * NG + g - 2)
                nc.scalar.copy(weightT[g % 2][:, :], b_tr[0:KT, :]).then_inc(t_wT.sem, 1)

            with act.Fori(0, B // 2) as step:
                for i in range(2):
                    if i == 0:
                        sequence_inputs(step, 0)
                        distances(step, 0, 0)
                    value_windows(step, i, 0)
                    value_windows(step, i, 1)
                    wait(act, t_n2c, step, i, 0)
                    nc.scalar.activation(inv[:, :], n2c[:, :], ACT.Ln, scale=NORM_SCALE).then_inc(t_inv.sem, 1)
                    wait(act, t_inv, step, i, 0)
                    nc.scalar.activation(inv[:, :], inv[:, :], ACT.Exp, scale=-0.5, bias=m.eps[:, 3:4]).then_inc(t_inv.sem, 1)
                    for g in range(NG):
                        if i == 0 and g == 2:
                            sequence_inputs(step, 1)
                        if g < NG - 1:
                            distances(step, i, g + 1)
                        elif i == 0:
                            distances(step, 1, 0)
                        transposed(step, i, g)

        @block.vector
        def _(dve):
            def squares(step, i):
                b = step * 2 + i
                wait(dve, t_keys, step, i - 2)
                all_q = qpad[:, bass.ds(b, 1), :].rearrange("p o t -> p (o t)")
                nc.vector.scalar_tensor_tensor(mk2[i][:, :], all_q, column(metric, b), all_q,
                                               ALU.mult, ALU.mult).then_inc(t_mk2.sem, 1)

            def carry(j):
                nc.vector.memset(spare[:, j:j + 1], 0.0)

            def select(step, i, g):
                unit, k = i * NG + g, g % 2
                base = unit * 2 * GT * (ROUNDS - 1)
                for r in range(ROUNDS):
                    src = value[k] if r == 0 else left[k]
                    if r == 0:
                        wait(dve, t_value, step, unit)
                        carry(3 * (g % 4) + 0)
                    for t in range(GT):
                        if r == 1 and t == 0:
                            wait(dve, t_taken, step, unit)
                            carry(3 * (g % 4) + 1)
                        elif r > 1:
                            dve.wait_ge(t_step, base + (2 * r - 3) * GT + t + 1)
                        ins = nc.vector.max(top[r][k][:, t, :], src[:, t, :])
                        ins.then_inc(t_top.sem, 1) if r == 0 else ins.then_inc(t_step, 1)
                    for t in range(GT):
                        if r == 0 and t == 0:
                            wait(dve, t_top, step, unit)
                            carry(3 * (g % 4) + 2)
                        elif r:
                            dve.wait_ge(t_step, base + (2 * r - 2) * GT + t + 1)
                        ins = nc.vector.match_replace(left[k][:, t, :], top[r][k][:, t, :], src[:, t, :], TAKEN)
                        ins.then_inc(t_taken.sem, 1) if r == 0 else ins.then_inc(t_step, 1)
                dve.wait_ge(t_step, base + 2 * GT * (ROUNDS - 1))
                wait(dve, t_infl, step, unit)
                wait(dve, t_tr, step, unit - 2)
                nc.vector.scalar_tensor_tensor(weight[k][:, :, :], left[k][:, :, :], TAKEN, dist[k][:, :, :],
                                               ALU.is_equal, ALU.mult).then_inc(t_weight.sem, 1)

            def normalise(step, i, g):
                unit, k = i * NG + g, g % 2
                cx = b_cx[:, :].rearrange("p (t e) -> p t e", t=GT)
                wait(dve, t_cx, step, unit)
                nc.vector.tensor_scalar(rden[k][:, :], cx[:, :, HALF], 1e-8, None, ALU.add).then_inc(t_rden.sem, 1)
                wait(dve, t_rden, step, unit, 0)
                nc.vector.reciprocal(rden[k][:, :], rden[k][:, :]).then_inc(t_rden.sem, 1)
                wait(dve, t_rden, step, unit)
                wait(dve, t_cxT, step, unit - 2)
                for t in range(GT):
                    nc.vector.scalar_tensor_tensor(chead[k][:, t, :], cx[:, t, 0:HALF], rden[k][:, t:t + 1], m.omask[:, :],
                                                   ALU.mult, ALU.mult).then_inc(t_chead.sem, 1)

            def hebbian(step, i):
                wait(dve, t_nh, step, i)
                nc.vector.tensor_scalar(n2c[:, :], b_nh[:, 0:T], 1e-24, None, ALU.max).then_inc(t_n2c.sem, 1)
                nc.vector.tensor_scalar(gate[:, :], b_nh[:, 0:T], GATE2, 0.1, ALU.is_gt, ALU.mult).then_inc(t_n2c.sem, 1)
                wait(dve, t_n2c, step, i)
                wait(dve, t_inv, step, i)
                nc.vector.tensor_tensor(gate[:, :], gate[:, :], inv[:, :], ALU.mult).then_inc(t_heb.sem, 1)
                wait(dve, t_heb, step, i, 0)
                nc.vector.tensor_tensor(heb[:, :], b_nh[:, T:2 * T], gate[:, :], ALU.mult).then_inc(t_heb.sem, 1)

            def finish(step, i):
                b = step * 2 + i
                wait(dve, t_cxT, step, i * NG + NG - 1)
                wait(dve, t_heb, step, i)
                nc.vector.tensor_tensor(ctxt[:, :], b_cxT[:, 0:T], heb[:, :], ALU.add).then_inc(t_ctx.sem, 1)
                wait(dve, t_ctx, step, i)
                wait(dve, t_dec, step, i - 1)
                nc.vector.tensor_tensor(outb[:, :], ctxt[:, :], queries(b), ALU.mult).then_inc(t_out.sem, 1)

            def residual(step, i):
                here = m.x[:, bass.ds((step * 2 + i) * T, T)]
                wait(dve, t_dec, step, i)
                nc.vector.tensor_tensor(here, here, b_dec[:, 0:T], ALU.add).then_inc(t_x.sem, 1)

            with dve.Fori(0, B // 2) as step:
                squares(step, 0)
                for i in range(2):
                    for g in range(NG):
                        select(step, i, g)
                        if i == 0 and g == 0:
                            squares(step, 1)
                        if g >= 1:
                            normalise(step, i, g - 1)
                        elif i == 1:
                            normalise(step, 0, NG - 1)
                            finish(step, 0)
                        if g == 0:
                            hebbian(step, i)
                    if i == 1:
                        residual(step, 0)
                normalise(step, 1, NG - 1)
                finish(step, 1)
                residual(step, 1)
                dve.wait_ge(t_step, G * 2 * GT * (ROUNDS - 1))
                dve.sem_clear(t_step)


def distance_layer(nc, m, dram):
    names = ("encoder_query", "encoder_value", "mn_w1", "mn_b1", "mn_w2", "mn_b2", "base_metric", "decoder",
             "hebbian_U", "hebbian_V")
    with ExitStack() as ctx:
        def sb(name, shape):
            return ctx.enter_context(nc.sbuf_tensor(name, shape, F32))

        w, loads = {"hebbian": sb("w_hebbian", [P, P])[:, :]}, []
        for name in names:
            a = dram["L0_attn_" + name]
            w[name] = sb("w_" + name, list(a.shape))[:, :]
            loads.append((w[name], a))
        z, qpad, metric = sb("a_z", [P, NT]), sb("a_qpad", [P, B, PAD + T]), sb("a_metric", [P, B])
        load_all(nc, m, "distance_layer", loads)
        layernorm(nc, m, "ln0", m.x, z)
        distance_queries(nc, m, w, z, qpad, metric)
        distance_attention(nc, m, w, z, qpad, metric)



UNROLL = 16
OGRP = 8


def delta_inputs(nc, m, w, z, kk, fT, qT, vT):
    with ExitStack() as ctx:
        def sb(name, shape):
            return ctx.enter_context(nc.sbuf_tensor(name, shape, F32))

        def sem(name):
            return m.sem(name)

        kraw, beta, f = sb("d_kraw", [P, NT]), sb("d_beta", [P, NT]), sb("d_f", [P, NT])
        f1 = sb("d_f1", [HD, NT])
        ksq, rk, kn = sb("d_ksq", [P, NT]), sb("d_rk", [P, NT]), sb("d_kn", [P, NT])
        kf, kkf, bk = sb("d_kf", [P, NT]), sb("d_kkf", [P, NT]), sb("d_bk", [P, NT])
        qkv_done, silu_done, f1_done, f1_copied, f2_done, beta_done, sig_done = map(
            sem, ("d_qkv", "d_silu", "d_f1d", "d_f1c", "d_f2", "d_bd", "d_sig"))
        ksq_done, knorm_done, s_done, dch, kkf_done, rk_log, rk_done = map(
            sem, ("d_sq", "d_kno", "d_s", "d_ch", "d_kkfd", "d_rklog", "d_rkd"))
        block = ctx.enter_context(nc.Block())

        def tb(a, n):
            return a[:, cols(n)].rearrange("p (b t) -> p b t", b=BB)

        def bt(a, n):
            return a[:, 0:T, n * BB:(n + 1) * BB].rearrange("p t b -> p b t")

        @block.tensor
        def _(pe):
            for n in range(NBLK):
                for j, name in enumerate(("Wq", "Wk", "Wv")):
                    if 3 * n + j >= 6:
                        pe.wait_ge(silu_done, 3 * n + j - 5)
                    nc.tensor.matmul(m.ps[(3 * n + j) % 6][:, :], w[name], z[:, cols(n)],
                                     start=True, stop=True).then_inc(qkv_done, 1)
            for n in range(NBLK):
                if n >= 2:
                    pe.wait_ge(f1_copied, n - 1)
                nc.tensor.matmul(m.ps[6 + n % 2][0:HD, :], w["Wf1"], z[:, cols(n)],
                                 start=True, stop=True).then_inc(f1_done, 1)
            for n in range(NBLK):
                pe.wait_ge(silu_done, 3 * NBLK)
                pe.wait_ge(f1_copied, n + 1)
                if n >= 2:
                    pe.wait_ge(sig_done, 2 * (n - 1))
                nc.tensor.matmul(m.ps[n % 2][:, :], w["Wf2"], f1[:, cols(n)],
                                 start=True, stop=True).then_inc(f2_done, 1)
                nc.tensor.matmul(m.ps[2 + n % 2][:, :], w["Wbeta"], z[:, cols(n)],
                                 start=True, stop=True).then_inc(beta_done, 1)
            for n in range(NBLK):
                pe.wait_ge(ksq_done, n + 1)
                if n >= 1:
                    pe.wait_ge(dch, 7 * n)
                nc.tensor.matmul(m.ps[4][:, :], m.headsum[:, :], ksq[:, cols(n)],
                                 start=True, stop=True).then_inc(knorm_done, 1)
                pe.wait_ge(kkf_done, n + 1)
                nc.tensor.matmul(m.ps[5][:, :], m.headsum[:, :], kkf[:, cols(n)],
                                 start=True, stop=True).then_inc(s_done, 1)

        @block.scalar
        def _(act):
            for n in range(NBLK):
                for j, out in enumerate((bt(qT, n), tb(kraw, n), bt(vT, n))):
                    act.wait_ge(qkv_done, 3 * n + j + 1)
                    nc.scalar.activation(out, m.ps[(3 * n + j) % 6][:, :].rearrange(
                        "p (b t) -> p b t", b=BB), ACT.Silu).then_inc(silu_done, 1)
                act.wait_ge(silu_done, 3 * n + 2)
                nc.scalar.activation(ksq[:, cols(n)], kraw[:, cols(n)], ACT.Square).then_inc(ksq_done, 1)
            for n in range(NBLK):
                act.wait_ge(f1_done, n + 1)
                nc.scalar.copy(f1[:, cols(n)], m.ps[6 + n % 2][0:HD, :]).then_inc(f1_copied, 1)
            for n in range(NBLK):
                act.wait_ge(f2_done, n + 1)
                nc.scalar.activation(f[:, cols(n)], m.ps[n % 2][:, :], ACT.Sigmoid).then_inc(sig_done, 1)
                act.wait_ge(beta_done, n + 1)
                nc.scalar.activation(beta[:, cols(n)], m.ps[2 + n % 2][:, :], ACT.Sigmoid).then_inc(sig_done, 1)
            for n in range(NBLK):
                act.wait_ge(knorm_done, n + 1)
                nc.scalar.activation(rk[:, cols(n)], m.ps[4][:, :], ACT.Ln, bias=m.eps[:, 1:2]).then_inc(rk_log, 1)
                act.wait_ge(rk_log, n + 1)
                nc.scalar.activation(rk[:, cols(n)], rk[:, cols(n)], ACT.Exp, scale=-0.5).then_inc(rk_done, 1)

        @block.vector
        def _(dve):
            for n in range(NBLK):
                c, base = cols(n), 7 * n
                dve.wait_ge(rk_done, n + 1)
                nc.vector.tensor_tensor(kn[:, c], kraw[:, c], rk[:, c], ALU.mult).then_inc(dch, 1)
                dve.wait_ge(sig_done, 2 * (n + 1))
                dve.wait_ge(dch, base + 1)
                nc.vector.tensor_tensor(kf[:, c], kn[:, c], f[:, c], ALU.mult).then_inc(dch, 1)
                nc.vector.tensor_scalar(beta[:, c], beta[:, c], 2.0, None, ALU.mult).then_inc(dch, 1)
                dve.wait_ge(dch, base + 3)
                nc.vector.tensor_tensor(kkf[:, c], kn[:, c], kf[:, c], ALU.mult).then_inc(kkf_done, 1)
                nc.vector.scalar_tensor_tensor(bt(kk[:, :, 2, :], n), tb(kf, n), -1.0, tb(beta, n),
                                               ALU.mult, ALU.mult).then_inc(dch, 1)
                nc.vector.tensor_tensor(bk[:, c], kn[:, c], beta[:, c], ALU.mult).then_inc(dch, 1)
                dve.wait_ge(s_done, n + 1)
                dve.wait_ge(dch, base + 5)
                nc.vector.tensor_tensor(bk[:, c], m.ps[5][:, :], bk[:, c], ALU.mult).then_inc(dch, 1)
                dve.wait_ge(dch, base + 6)
                nc.vector.tensor_tensor(bk[:, c], bk[:, c], kf[:, c], ALU.subtract).then_inc(dch, 1)
                dve.wait_ge(dch, base + 7)
                nc.vector.tensor_tensor(bt(kk[:, :, 0, :], n), tb(bk, n), tb(beta, n), ALU.mult)
                nc.vector.tensor_copy(bt(kk[:, :, 1, :], n), tb(kn, n))

        @block.gpsimd
        def _(pool):
            for n in range(NBLK):
                pool.wait_ge(sig_done, 2 * n + 1)
                nc.gpsimd.tensor_copy(bt(fT, n), tb(f, n))


def delta_scan(nc, m, kk, fT, qT, vT, ost):
    W = B * HD
    with ExitStack() as ctx:
        def sb(name, shape):
            return ctx.enter_context(nc.sbuf_tensor(name, shape, F32))

        def sem(name):
            return m.sem(name)

        state = [sb(f"r_state{i}", [P, B, HD]) for i in range(2)]
        k_state = [sb(f"r_kstate{i}", [P, B, HD]) for i in range(2)]
        p_state = [sb(f"r_pstate{i}", [P, B, HD]) for i in range(2)]
        q_state = [sb(f"r_qstate{i}", [P, B, HD]) for i in range(2)]
        decayed = [sb(f"r_decayed{i}", [P, B, HD]) for i in range(2)]
        v_spread = [sb(f"r_vspread{i}", [P, B, HD]) for i in range(2)]
        g_part = [sb(f"r_gpart{i}", [P, B, HD]) for i in range(2)]
        rest = [sb(f"r_rest{i}", [P, B, HD]) for i in range(2)]
        k_part = [sb(f"r_kpart{i}", [P, B, HD]) for i in range(2)]
        (s_state, s_kstate, s_pstate, s_qstate, s_decayed, s_vspread, s_gpart, s_rest, s_kpart,
         s_ysum_k, s_ysum_p, s_out, s_outcopied) = map(sem, (
            "r_state", "r_kstate", "r_pstate", "r_qstate", "r_decayed", "r_vspread", "r_gpart", "r_rest",
            "r_kpart", "r_ysum_k", "r_ysum_p", "r_out", "r_outcopied"))
        y_k, y_p = [m.ps[0], m.ps[1]], [m.ps[2], m.ps[3]]
        o_ps = [m.ps[4], m.ps[5]]
        block = ctx.enter_context(nc.Block())

        def flat(a):
            return a[:, :, :].rearrange("p b j -> p (b j)")

        def bj(a):
            return a[:, 0:W].rearrange("p (b j) -> p b j", b=B)

        def spread(a):
            return a.unsqueeze(2).to_broadcast([P, B, HD])

        def at(a, t):
            return a[:, bass.ds(t, 1), :].rearrange("p o b -> p (o b)")

        def at3(a, t, j):
            return a[:, bass.ds(t, 1), j, :].rearrange("p o b -> p (o b)")

        vmask = m.vmask[:, :].unsqueeze(1).to_broadcast([P, B, HD])

        @block.vector
        def _(dve):
            nc.vector.memset(state[0][:, :, :], 0.0).then_inc(s_state, 1)
            with dve.Fori(0, T // UNROLL) as step:
                t0 = step * UNROLL
                for u in range(UNROLL):
                    i, t = u % 2, t0 + u
                    dve.wait_ge(s_state, t0 + (u + 1))
                    nc.vector.tensor_tensor(k_state[i][:, :, :], state[i][:, :, :], spread(at3(kk, t, 1)),
                                            ALU.mult).then_inc(s_kstate, 1)
                    nc.vector.tensor_tensor(p_state[i][:, :, :], state[i][:, :, :], spread(at3(kk, t, 0)),
                                            ALU.mult).then_inc(s_pstate, 1)
                    dve.wait_ge(s_ysum_k, t0 + (u + 1))
                    nc.vector.tensor_tensor(g_part[i][:, :, :], bj(y_k[i]), spread(at3(kk, t, 2)),
                                            ALU.mult).then_inc(s_gpart, 1)
                    dve.wait_ge(s_gpart, t0 + (u + 1))
                    dve.wait_ge(s_decayed, t0 + (u + 1))
                    nc.vector.tensor_tensor(rest[i][:, :, :], g_part[i][:, :, :], decayed[i][:, :, :],
                                            ALU.add).then_inc(s_rest, 1)
                    dve.wait_ge(s_ysum_p, t0 + (u + 1))
                    nc.vector.tensor_tensor(k_part[i][:, :, :], bj(y_p[i]), spread(at3(kk, t, 1)),
                                            ALU.mult).then_inc(s_kpart, 1)
                    dve.wait_ge(s_rest, t0 + (u + 1))
                    dve.wait_ge(s_kpart, t0 + (u + 1))
                    nc.vector.tensor_tensor(state[1 - i][:, :, :], k_part[i][:, :, :], rest[i][:, :, :],
                                            ALU.add).then_inc(s_state, 1)

        @block.gpsimd
        def _(pool):
            nc.gpsimd.tensor_tensor(v_spread[0][:, :, :], vmask, spread(vT[:, 0, :]), ALU.mult).then_inc(s_vspread, 1)
            pool.wait_ge(s_state, 1)
            nc.gpsimd.tensor_tensor(decayed[0][:, :, :], state[0][:, :, :], spread(fT[:, 0, :]),
                                    ALU.mult).then_inc(s_decayed, 1)
            nc.gpsimd.tensor_tensor(v_spread[1][:, :, :], vmask, spread(vT[:, 1, :]), ALU.mult).then_inc(s_vspread, 1)
            with pool.Fori(0, T // UNROLL) as step:
                t0 = step * UNROLL
                for u in range(UNROLL):
                    i, t = u % 2, t0 + u
                    pool.wait_ge(s_state, t0 + (u + 2))
                    nc.gpsimd.tensor_tensor(decayed[1 - i][:, :, :], state[1 - i][:, :, :],
                                            spread(at(fT, t + 1)), ALU.mult).then_inc(s_decayed, 1)
                    nc.gpsimd.tensor_tensor(q_state[i][:, :, :], state[1 - i][:, :, :],
                                            spread(at(qT, t)), ALU.mult).then_inc(s_qstate, 1)
                    nc.gpsimd.tensor_tensor(v_spread[i][:, :, :], vmask,
                                            spread(at(vT, t + 2)), ALU.mult).then_inc(s_vspread, 1)

        @block.tensor
        def _(pe):
            def output(u_prev):
                slot = u_prev % UNROLL
                half, col = slot // OGRP, slot % OGRP * NHEAD
                return nc.tensor.matmul(o_ps[half][:, col:col + NHEAD], flat(q_state[slot % 2]),
                                        m.headsel[:, :], start=True, stop=True)

            with pe.Fori(0, T // UNROLL) as step:
                t0 = step * UNROLL
                for u in range(UNROLL):
                    i = u % 2
                    pe.wait_ge(s_vspread, t0 + (u + 1))
                    nc.tensor.matmul(y_p[i][:, 0:W], m.headsum[:, :], flat(v_spread[i]), start=True, stop=False)
                    pe.wait_ge(s_kstate, t0 + (u + 1))
                    nc.tensor.matmul(y_k[i][:, 0:W], m.headsum[:, :], flat(k_state[i]),
                                     start=True, stop=True).then_inc(s_ysum_k, 1)
                    pe.wait_ge(s_pstate, t0 + (u + 1))
                    nc.tensor.matmul(y_p[i][:, 0:W], m.headsum[:, :], flat(p_state[i]),
                                     start=False, stop=True).then_inc(s_ysum_p, 1)
                    if u >= 1:
                        pe.wait_ge(s_qstate, t0 + u)
                        if u - 1 in (0, OGRP):
                            pe.wait_ge(s_outcopied, step * (UNROLL // OGRP) + ((u - 1) // OGRP + 1))
                        output(u - 1).then_inc(s_out, 1)
                pe.wait_ge(s_qstate, t0 + UNROLL)
                output(UNROLL - 1).then_inc(s_out, 1)

        @block.scalar
        def _(act):
            nc.scalar.copy(m.scratch[:, 0:1], m.vmask[:, 0:1]).then_inc(s_outcopied, 1)
            nc.scalar.copy(m.scratch[:, 1:2], m.vmask[:, 0:1]).then_inc(s_outcopied, 1)
            with act.Fori(0, T // UNROLL) as step:
                t0 = step * UNROLL
                for half in range(UNROLL // OGRP):
                    act.wait_ge(s_out, t0 + (half + 1) * OGRP)
                    nc.scalar.copy(ost[:, :, bass.ds(t0 + half * OGRP, OGRP)],
                                   o_ps[half][:, 0:OGRP * NHEAD].rearrange("p (t h) -> p h t", t=OGRP)
                                   ).then_inc(s_outcopied, 1)


def delta_outputs(nc, m, w, z, ost, o_dram):
    with ExitStack() as ctx:
        def sb(name, shape):
            return ctx.enter_context(nc.sbuf_tensor(name, shape, F32))

        def sem(name):
            return m.sem(name)

        oT, sg, g1 = sb("e_oT", [P, NT]), sb("e_sg", [P, NT]), sb("e_g1", [HD, NT])
        ysq, ry = sb("e_ysq", [P, NT]), sb("e_ry", [P, NT])
        stored, loaded, g1_done, g1_copied, g2_done, sig_done, gated, squared, ms_done, dch, wo_done, ry_log, ry_done = map(
            sem, ("e_stored", "e_loaded", "e_g1d", "e_g1c", "e_g2", "e_sig", "e_gated", "e_sq", "e_ms", "e_dch",
                  "e_wo", "e_rylog", "e_ryd"))
        block = ctx.enter_context(nc.Block())

        @block.sync
        def _(sp):
            sp.dma_start(o_dram.rearrange("b j h t -> (b j) h t"), ost[:, :, :]).then_inc(stored, 16)
            sp.wait_ge(stored, 16)
            for h in range(NHEAD):
                sp.dma_start(oT[h * HD:(h + 1) * HD, :].rearrange("j (b t) -> j b t", b=B),
                             o_dram[:, :, h, :].rearrange("b j t -> j b t")).then_inc(loaded, 16)

        @block.tensor
        def _(pe):
            for n in range(NBLK):
                nc.tensor.matmul(m.ps[n][0:HD, :], w["Wog1"], z[:, cols(n)], start=True, stop=True).then_inc(g1_done, 1)
            for n in range(NBLK):
                pe.wait_ge(g1_copied, n + 1)
                nc.tensor.matmul(m.ps[4 + n][:, :], w["Wog2"], g1[:, cols(n)], start=True, stop=True).then_inc(g2_done, 1)
            for n in range(NBLK):
                pe.wait_ge(squared, n + 1)
                nc.tensor.matmul(m.ps[n][:, :], m.headavg[:, :], ysq[:, cols(n)], start=True, stop=True).then_inc(ms_done, 1)
            for n in range(NBLK):
                pe.wait_ge(dch, 2 * (n + 1))
                nc.tensor.matmul(m.ps[4 + n][:, :], w["Wo"], oT[:, cols(n)], start=True, stop=True).then_inc(wo_done, 1)

        @block.scalar
        def _(act):
            for n in range(NBLK):
                act.wait_ge(g1_done, n + 1)
                nc.scalar.copy(g1[:, cols(n)], m.ps[n][0:HD, :]).then_inc(g1_copied, 1)
            for n in range(NBLK):
                act.wait_ge(g2_done, n + 1)
                nc.scalar.activation(sg[:, cols(n)], m.ps[4 + n][:, :], ACT.Sigmoid).then_inc(sig_done, 1)
            for n in range(NBLK):
                act.wait_ge(gated, n + 1)
                nc.scalar.activation(ysq[:, cols(n)], oT[:, cols(n)], ACT.Square).then_inc(squared, 1)
            for n in range(NBLK):
                act.wait_ge(ms_done, n + 1)
                nc.scalar.activation(ry[:, cols(n)], m.ps[n][:, :], ACT.Ln, bias=m.eps[:, 1:2]).then_inc(ry_log, 1)
                act.wait_ge(ry_log, n + 1)
                nc.scalar.activation(ry[:, cols(n)], ry[:, cols(n)], ACT.Exp, scale=-0.5).then_inc(ry_done, 1)

        @block.vector
        def _(dve):
            dve.wait_ge(loaded, 16 * NHEAD)
            for n in range(NBLK):
                dve.wait_ge(sig_done, n + 1)
                nc.vector.tensor_tensor(oT[:, cols(n)], oT[:, cols(n)], sg[:, cols(n)], ALU.mult).then_inc(gated, 1)
            for n in range(NBLK):
                dve.wait_ge(gated, n + 1)
                dve.wait_ge(squared, n + 1)
                dve.wait_ge(ry_done, n + 1)
                nc.vector.tensor_tensor(oT[:, cols(n)], oT[:, cols(n)], ry[:, cols(n)], ALU.mult).then_inc(dch, 1)
                dve.wait_ge(dch, 2 * n + 1)
                nc.vector.tensor_scalar(oT[:, cols(n)], oT[:, cols(n)], w["norm_w"], None, ALU.mult).then_inc(dch, 1)
            for n in range(NBLK):
                dve.wait_ge(wo_done, n + 1)
                nc.vector.tensor_tensor(m.x[:, cols(n)], m.x[:, cols(n)], m.ps[4 + n][:, :], ALU.add)


def recurrence_layer(nc, m, dram):
    names = ("Wq", "Wk", "Wv", "Wf1", "Wf2", "Wbeta", "Wog1", "Wog2", "Wo", "norm_w")
    with ExitStack() as ctx:
        w, loads = {}, []
        for name in names:
            a = dram["L1_attn_" + name]
            buf = ctx.enter_context(nc.sbuf_tensor("w_" + name, list(a.shape), F32))
            w[name] = buf[:, :]
            loads.append((buf[:, :], a))
        z = ctx.enter_context(nc.sbuf_tensor("d_z", [P, NT], F32))
        qT = ctx.enter_context(nc.sbuf_tensor("d_qT", [P, T, B], F32))
        kk = ctx.enter_context(nc.sbuf_tensor("d_kk", [P, T, 3, B], F32))
        fT = ctx.enter_context(nc.sbuf_tensor("d_fT", [P, T + 2, B], F32))
        vT = ctx.enter_context(nc.sbuf_tensor("d_vT", [P, T + 2, B], F32))
        ost = ctx.enter_context(nc.sbuf_tensor("d_ost", [P, NHEAD, T], F32))
        load_all(nc, m, "recurrence_layer", loads)
        with nc.Block() as block:
            @block.gpsimd
            def _(pool):
                nc.gpsimd.memset(fT[:, T:T + 2, :], 0.0)
                nc.gpsimd.memset(vT[:, T:T + 2, :], 0.0)
        layernorm(nc, m, "ln5", m.x, z)
        delta_inputs(nc, m, w, z, kk, fT, qT, vT)
        delta_scan(nc, m, kk, fT, qT, vT, ost)
        delta_outputs(nc, m, w, z, ost, dram["o_scratch"])


NEXP = 8
TILES = NT // P


def route(nc, m, name, z, router, gates):
    with ExitStack() as ctx:
        def sb(s, shape):
            return ctx.enter_context(nc.sbuf_tensor(f"{name}_{s}", shape, F32))

        prob, order, best = sb("prob", [P, TILES, NEXP]), sb("order", [P, TILES, NEXP]), sb("best", [P, TILES, NEXP])
        pick1, pick2, rest = sb("pick1", [P, TILES, NEXP]), sb("pick2", [P, TILES, NEXP]), sb("rest", [P, TILES, NEXP])
        top, total, first = sb("top", [P, TILES]), sb("total", [P, TILES]), sb("first", [P, TILES])
        logits_done, shifted, exped, chain = (m.sem(f"{name}_{s}")
                                              for s in ("logits", "shifted", "exped", "chain"))
        block = ctx.enter_context(nc.Block())

        def wide(a):
            return a[:, :].unsqueeze(2).to_broadcast([P, TILES, NEXP])

        @block.tensor
        def _(pe):
            for t in range(TILES):
                mm = nc.tensor.matmul(m.ps[0][:, t * NEXP:(t + 1) * NEXP], z[:, cols(t, P)], router, start=True, stop=True)
            mm.then_inc(logits_done, 1)

        @block.scalar
        def _(act):
            act.wait_ge(shifted, 1)
            nc.scalar.activation(prob[:, :, :], prob[:, :, :], ACT.Exp).then_inc(exped, 1)

        @block.vector
        def _(dve):
            steps = [0]

            def then(ins):
                steps[0] += 1
                ins.then_inc(chain, 1)
                dve.wait_ge(chain, steps[0])

            logits = m.ps[0][:, 0:TILES * NEXP].rearrange("p (t e) -> p t e", t=TILES)
            weight = m.order[:, :].unsqueeze(1).to_broadcast([P, TILES, NEXP])
            dve.wait_ge(logits_done, 1)
            then(nc.vector.tensor_reduce(top[:, :], logits, AX.X, ALU.max))
            nc.vector.tensor_tensor(prob[:, :, :], logits, wide(top), ALU.subtract).then_inc(shifted, 1)
            dve.wait_ge(exped, 1)
            then(nc.vector.tensor_reduce(total[:, :], prob[:, :, :], AX.X, ALU.add))
            then(nc.vector.reciprocal(total[:, :], total[:, :]))
            then(nc.vector.tensor_tensor(prob[:, :, :], prob[:, :, :], wide(total), ALU.mult))

            def pick(source, out):
                then(nc.vector.tensor_reduce(top[:, :], source[:, :, :], AX.X, ALU.max))
                then(nc.vector.tensor_tensor(best[:, :, :], source[:, :, :], wide(top), ALU.is_equal))
                then(nc.vector.tensor_tensor(order[:, :, :], best[:, :, :], weight, ALU.mult))
                then(nc.vector.tensor_reduce(first[:, :], order[:, :, :], AX.X, ALU.max))
                then(nc.vector.tensor_tensor(out[:, :, :], order[:, :, :], wide(first), ALU.is_equal))

            pick(prob, pick1)
            then(nc.vector.scalar_tensor_tensor(rest[:, :, :], pick1[:, :, :], -2.0, prob[:, :, :], ALU.mult, ALU.add))
            pick(rest, pick2)
            then(nc.vector.tensor_tensor(pick1[:, :, :], pick1[:, :, :], pick2[:, :, :], ALU.add))
            then(nc.vector.tensor_tensor(gates[:, :, :], pick1[:, :, :], prob[:, :, :], ALU.mult))


def experts(nc, m, name, z, gates, up_dram, gate_dram, down_dram, width, gelu, shared=None):
    C = width // P
    S = 2 * NBLK * C
    with ExitStack() as ctx:
        def sb(s, shape, n=2):
            return [ctx.enter_context(nc.sbuf_tensor(f"{name}_{s}{i}", shape, F32)) for i in range(n)]

        tallies = []

        def tally(s, units, per=1, credit=0):
            tallies.append(Tally(m, f"{name}_{s}", units, per, credit))
            return tallies[-1]

        up, down = sb("up", [P, width]), sb("down", [P, C, P])
        first = sb("first", [P, width]) if not gelu else up
        gcol = sb("gcol", [P, TILES])
        silu, hidden, gate, gated = sb("silu", [P, BLK]), sb("hidden", [P, BLK]), sb("gate", [P, BLK]), sb("gated", [P, BLK])
        loads = 2 if gelu else 3
        t_w = [tally(f"w{i}", 1, 16 * loads) for i in range(2)]
        t_col = tally("col", 2)
        t_first, t_second, t_silu, t_hidden, t_down = (tally("first_ps", S), tally("second_ps", S), tally("silu_done", S, 1, 2),
                                                       tally("hidden_done", S, 1, 2), tally("down_done", S, 1, 2))
        t_gps, t_gate, t_gated, t_acc = (tally("gate_ps", 2 * NBLK, 1, 1), tally("gate_done", 2 * NBLK, 1, 2),
                                         tally("gated_done", 2 * NBLK, 1, 2), tally("acc", 2 * NBLK, 1, 2))
        b_first, b_second, b_y, b_gate = m.ps[0:2], m.ps[2:4], m.ps[4:6], m.ps[6:8]
        NPASS = NEXP // 2
        if shared:
            s_first, s_up, s_down = (sb(f"s_{j}", shape, 1)[0] for j, shape in
                                     (("first", [P, width // 2]), ("up", [P, width // 2]), ("down", [P, C // 2, P])))
            s_loaded = m.sem(name + "_sloaded")
        with nc.Block() as block:
            @block.gpsimd
            def _(pool):
                give_credit(pool, tallies)

        block = ctx.enter_context(nc.Block())

        def wait(eng, t, step, unit, j=None):
            eng.wait_ge(t.sem, t.done(step, unit, j))

        def load(sp, i, e):
            pick = (lambda a: a[e]) if isinstance(e, int) else (lambda a: a[bass.ds(e, 1)].rearrange("o a b -> (o a) b"))
            sp.dma_start(up[i][:, :], pick(up_dram)).then_inc(t_w[i].sem, 16)
            sp.dma_start(down[i][:, :, :], pick(down_dram).rearrange("(c p) h -> p c h", p=P)).then_inc(t_w[i].sem, 16)
            if not gelu:
                sp.dma_start(first[i][:, :], pick(gate_dram)).then_inc(t_w[i].sem, 16)

        @block.sync
        def _(sp):
            if shared:
                for dst, src in ((s_first[:, :], shared[0]), (s_up[:, :], shared[1]),
                                 (s_down[:, :, :], shared[2].rearrange("(c p) h -> p c h", p=P))):
                    sp.dma_start(dst, src).then_inc(s_loaded, 16)
            for i in range(2):
                load(sp, i, i)
            with sp.Fori(0, NPASS - 1) as step:
                for i in range(2):
                    wait(sp, t_down, step, (i + 1) * NBLK * C - 1)
                    load(sp, i, step * 2 + (i + 2))

        def steps(experts_of_pass, chunks):
            return [(i, n, c) for i in experts_of_pass for n in range(NBLK) for c in range(chunks)]

        def pe_pass(pe, step, chunks, weights, gated_by):
            seq = steps(range(len(weights)), chunks)

            def down_product(k):
                i, n, c = seq[k]
                wait(pe, t_hidden, step, k)
                if c == 0:
                    wait(pe, t_gated, step, i * NBLK + n - 2)
                nc.tensor.matmul(b_y[n % 2][:, :], weights[i][2][:, c, :], hidden[k % 2][:, :],
                                 start=(c == 0), stop=(c == chunks - 1)).then_inc(t_down.sem, 1)

            for k, (i, n, c) in enumerate(seq):
                w_first, w_up, _ = weights[i]
                if c == 0 and gated_by:
                    if n == 0:
                        wait(pe, t_col, step, i)
                        wait(pe, t_w[i], step, 0)
                    wait(pe, t_gate, step, i * NBLK + n - 2)
                    for t in range(BLK // P):
                        tile = n * (BLK // P) + t
                        mm = nc.tensor.matmul(b_gate[n % 2][:, cols(t, P)],
                                              gcol[i][:, tile:tile + 1].to_broadcast([P, P]), m.ident[:, :],
                                              start=True, stop=True)
                    mm.then_inc(t_gps.sem, 1)
                wait(pe, t_silu if not gelu else t_hidden, step, k - 2)
                nc.tensor.matmul(b_first[k % 2][:, :], w_first[:, cols(c, P)], z[:, cols(n)],
                                 start=True, stop=True).then_inc(t_first.sem, 1)
                if not gelu:
                    wait(pe, t_hidden, step, k - 2)
                    nc.tensor.matmul(b_second[k % 2][:, :], w_up[:, cols(c, P)], z[:, cols(n)],
                                     start=True, stop=True).then_inc(t_second.sem, 1)
                if k:
                    down_product(k - 1)
            down_product(len(seq) - 1)

        def act_pass(act, step, chunks, n_experts, gated_by):
            for k, (i, n, c) in enumerate(steps(range(n_experts), chunks)):
                if c == 0 and gated_by:
                    unit = i * NBLK + n
                    wait(act, t_gps, step, unit)
                    wait(act, t_gated, step, unit - 2)
                    nc.scalar.copy(gate[n % 2][:, :], b_gate[n % 2][:, :]).then_inc(t_gate.sem, 1)
                wait(act, t_first, step, k)
                if gelu:
                    wait(act, t_down, step, k - 2)
                    nc.scalar.activation(hidden[k % 2][:, :], b_first[k % 2][:, :], ACT.Gelu).then_inc(t_hidden.sem, 1)
                else:
                    wait(act, t_hidden, step, k - 2)
                    nc.scalar.activation(silu[k % 2][:, :], b_first[k % 2][:, :], ACT.Silu).then_inc(t_silu.sem, 1)

        def dve_pass(dve, step, chunks, n_experts, gated_by):
            seq = steps(range(n_experts), chunks)

            def gated_block(i, n):
                unit = i * NBLK + n
                wait(dve, t_down, step, unit * chunks + chunks - 1)
                wait(dve, t_acc, step, unit - 2)
                if gated_by:
                    wait(dve, t_gate, step, unit)
                    nc.vector.tensor_tensor(gated[n % 2][:, :], b_y[n % 2][:, :], gate[n % 2][:, :],
                                            ALU.mult).then_inc(t_gated.sem, 1)
                else:
                    nc.vector.tensor_scalar(gated[n % 2][:, :], b_y[n % 2][:, :], SHARED_SCALE, None,
                                            ALU.mult).then_inc(t_gated.sem, 1)

            for k, (i, n, c) in enumerate(seq):
                if not gelu:
                    wait(dve, t_second, step, k)
                    wait(dve, t_silu, step, k)
                    wait(dve, t_down, step, k - 2)
                    nc.vector.tensor_tensor(hidden[k % 2][:, :], b_second[k % 2][:, :], silu[k % 2][:, :],
                                            ALU.mult).then_inc(t_hidden.sem, 1)
                if k >= chunks + 1 and (k - 1) % chunks == 0:
                    gated_block(*seq[k - chunks - 1][:2])
            gated_block(*seq[-1][:2])

        def pool_pass(pool, step, n_experts, columns):
            if columns:
                wait(pool, t_gps, step, -1)
                for i in range(n_experts):
                    nc.gpsimd.tensor_copy(gcol[i][:, :], gates[:, :, bass.ds(step * 2 + i, 1)].rearrange("p t o -> p (t o)")
                                          ).then_inc(t_col.sem, 1)
            for i in range(n_experts):
                for n in range(NBLK):
                    unit = i * NBLK + n
                    wait(pool, t_gated, step, unit)
                    wait(pool, t_acc, step, unit - 1)
                    nc.gpsimd.tensor_tensor(m.x[:, cols(n)], m.x[:, cols(n)], gated[n % 2][:, :],
                                            ALU.add).then_inc(t_acc.sem, 1)

        pair = [(first[i], up[i], down[i]) for i in range(2)]

        @block.tensor
        def _(pe):
            with pe.Fori(0, NPASS) as step:
                pe_pass(pe, step, C, pair, True)
            if shared:
                pe.wait_ge(s_loaded, 48)
                pe_pass(pe, NPASS, C // 2, [(s_first, s_up, s_down)], False)

        @block.scalar
        def _(act):
            with act.Fori(0, NPASS) as step:
                act_pass(act, step, C, 2, True)
            if shared:
                act_pass(act, NPASS, C // 2, 1, False)

        @block.vector
        def _(dve):
            with dve.Fori(0, NPASS) as step:
                dve_pass(dve, step, C, 2, True)
            if shared:
                dve_pass(dve, NPASS, C // 2, 1, False)

        @block.gpsimd
        def _(pool):
            with pool.Fori(0, NPASS) as step:
                pool_pass(pool, step, 2, True)
            if shared:
                pool_pass(pool, NPASS, 1, False)


SHARED_SCALE = 0.5


def mixture_layer(nc, m, dram):
    d = {k: dram["L1_ffn_" + k] for k in ("Wr", "Wg", "Wu", "Wd", "Sg", "Su", "Sd")}
    with ExitStack() as ctx:
        z = ctx.enter_context(nc.sbuf_tensor("f_z", [P, NT], F32))
        router = ctx.enter_context(nc.sbuf_tensor("f_router", [P, NEXP], F32))
        gates = ctx.enter_context(nc.sbuf_tensor("f_gates", [P, TILES, NEXP], F32))
        load_all(nc, m, "mixture_layer", [(router[:, :], d["Wr"])])
        layernorm(nc, m, "ln6", m.x, z)
        route(nc, m, "f_route", z, router[:, :], gates)
        experts(nc, m, "f", z, gates, d["Wu"], d["Wg"], d["Wd"], d["Wg"].shape[2], False, (d["Sg"], d["Su"], d["Sd"]))


AHD = 8


def sequence_attention(nc, m, w, z):
    with ExitStack() as ctx:
        def sb(s, shape):
            return ctx.enter_context(nc.sbuf_tensor("g_" + s, shape, F32))

        def sem(s):
            return m.sem("g_" + s)

        hn = sb("hn", [P, NT])
        q, k, v, attended = sb("q", [P, B, T]), sb("k", [P, B, T]), sb("v", [P, B, T]), sb("attended", [P, B, T])
        prod = [sb(f"prod{i}", [P, B, T]) for i in range(2)]
        prob = [sb(f"prob{i}", [P, B, T]) for i in range(2)]
        top, total = sb("top", [P, T]), sb("total", [P, T])
        layernorm(nc, m, "ln2", z, hn, w["ln1_w"], w["ln1_b"])
        qkv_done, qkv_copied, prods, scored, shifted, exped, weighted, chain, added, attn_done, proj_done = map(
            sem, ("qkv", "qkvc", "prods", "scored", "shifted", "exped", "weighted", "chain", "added", "attn", "proj"))
        block = ctx.enter_context(nc.Block())

        def flat(a):
            return a[:, :, :].rearrange("p b t -> p (b t)")

        def banks(s, n):
            half = 4 * (s % 2)
            return m.psum[:, half * BLK:half * BLK + n * T].rearrange("p (b t) -> p b t", b=n)

        @block.tensor
        def _(pe):
            for j in range(3):
                for n in range(NBLK):
                    u = j * NBLK + n
                    if u >= 8:
                        pe.wait_ge(qkv_copied, u - 7)
                    nc.tensor.matmul(m.ps[u % 8][:, :], w["in_proj_w"][:, cols(j, P)], hn[:, cols(n)],
                                     start=True, stop=True).then_inc(qkv_done, 1)
            for s in range(B):
                pe.wait_ge(prods, s + 1)
                if s < 2:
                    pe.wait_ge(qkv_copied, 3 * NBLK)
                else:
                    pe.wait_ge(shifted, s - 1)
                for c in range(0, s + 1, BB):
                    n = min(BB, s + 1 - c) * T
                    mm = nc.tensor.matmul(m.psum[:, (4 * (s % 2)) * BLK + c * T:(4 * (s % 2)) * BLK + c * T + n],
                                          m.headscale[:, :], flat(prod[s % 2])[:, c * T:c * T + n], start=True, stop=True)
                mm.then_inc(scored, 1)
            for n in range(NBLK):
                pe.wait_ge(attn_done, (n + 1) * BB)
                if n == 0:
                    pe.wait_ge(shifted, B)
                nc.tensor.matmul(m.ps[n][:, :], w["out_proj_w"], flat(attended)[:, cols(n)],
                                 start=True, stop=True).then_inc(proj_done, 1)

        @block.scalar
        def _(act):
            for j, out in enumerate((q, k, v)):
                for n in range(NBLK):
                    u = j * NBLK + n
                    act.wait_ge(qkv_done, u + 1)
                    nc.scalar.activation(flat(out)[:, cols(n)], m.ps[u % 8][:, :], ACT.Identity,
                                         bias=w["in_proj_b"][:, j:j + 1]).then_inc(qkv_copied, 1)
            for s in range(B):
                act.wait_ge(shifted, s + 1)
                nc.scalar.activation(prob[s % 2][:, 0:s + 1, :], prob[s % 2][:, 0:s + 1, :], ACT.Exp).then_inc(exped, 1)

        @block.gpsimd
        def _(pool):
            for s in range(B):
                pool.wait_ge(exped, s + 1)
                pool.wait_ge(scored, s + 1)
                nc.gpsimd.tensor_tensor(prod[s % 2][:, 0:s + 1, :], prob[s % 2][:, 0:s + 1, :], v[:, 0:s + 1, :],
                                        ALU.mult).then_inc(weighted, 1)

        @block.vector
        def _(dve):
            steps = [0]

            def then(ins):
                steps[0] += 1
                ins.then_inc(chain, 1)
                dve.wait_ge(chain, steps[0])

            def products(s):
                if s >= 2:
                    dve.wait_ge(weighted, s - 1)
                    dve.wait_ge(attn_done, s - 1)
                nc.vector.tensor_tensor(prod[s % 2][:, 0:s + 1, :], k[:, 0:s + 1, :],
                                        q[:, s:s + 1, :].to_broadcast([P, s + 1, T]), ALU.mult).then_inc(prods, 1)

            dve.wait_ge(qkv_copied, 3 * NBLK)
            products(0)
            for s in range(B):
                n = s + 1
                dve.wait_ge(scored, n)
                then(nc.vector.tensor_reduce(top[:, :], banks(s, n).rearrange("p b t -> p t b"), AX.X, ALU.max))
                nc.vector.tensor_tensor(prob[s % 2][:, 0:n, :], banks(s, n),
                                        top[:, :].unsqueeze(1).to_broadcast([P, n, T]), ALU.subtract).then_inc(shifted, 1)
                if s + 1 < B:
                    products(s + 1)
                dve.wait_ge(exped, n)
                then(nc.vector.tensor_reduce(total[:, :], prob[s % 2][:, 0:n, :].rearrange("p b t -> p t b"), AX.X, ALU.add))
                then(nc.vector.reciprocal(total[:, :], total[:, :]))
                dve.wait_ge(weighted, n)
                then(nc.vector.tensor_reduce(attended[:, s, :], prod[s % 2][:, 0:n, :].rearrange("p b t -> p t b"),
                                             AX.X, ALU.add))
                nc.vector.tensor_tensor(attended[:, s, :], attended[:, s, :], total[:, :], ALU.mult).then_inc(attn_done, 1)
            for n in range(NBLK):
                dve.wait_ge(proj_done, n + 1)
                nc.vector.scalar_tensor_tensor(z[:, cols(n)], m.ps[n][:, :], w["out_proj_b"], z[:, cols(n)],
                                               ALU.add, ALU.add).then_inc(added, 1)
            dve.wait_ge(added, NBLK)


def sequence_layer(nc, m, dram):
    names = ("ln1_w", "ln1_b", "in_proj_w", "in_proj_b", "out_proj_w", "out_proj_b", "ln2_w", "ln2_b", "router_w")
    with ExitStack() as ctx:
        w, loads = {}, []
        for name in names:
            a = dram["L0_ffn_" + name]
            w[name] = ctx.enter_context(nc.sbuf_tensor("w_" + name, list(a.shape), F32))[:, :]
            loads.append((w[name], a))
        z = ctx.enter_context(nc.sbuf_tensor("g_z", [P, NT], F32))
        gates = ctx.enter_context(nc.sbuf_tensor("g_gates", [P, TILES, NEXP], F32))
        load_all(nc, m, "sequence_layer", loads)
        layernorm(nc, m, "ln1", m.x, z)
        sequence_attention(nc, m, w, z)
        with nc.Block() as block:
            @block.gpsimd
            def _(pool):
                nc.gpsimd.tensor_tensor(m.x[:, :], m.x[:, :], z[:, :], ALU.add)
        with nc.sbuf_tensor("g_hn2", [P, NT], F32) as hn2:
            layernorm(nc, m, "ln3", z, hn2, w["ln2_w"], w["ln2_b"])
            route(nc, m, "g_route", hn2, w["router_w"], gates)
            experts(nc, m, "h", hn2, gates, dram["L0_ffn_w1"], None, dram["L0_ffn_w2"], dram["L0_ffn_w1"].shape[2], True)


LAYERS = (distance_layer, sequence_layer, recurrence_layer, mixture_layer)

CONSTS = ("avg", "headsum", "headavg", "headsel", "vmask", "ident", "band", "hmask", "omask", "qsel", "headscale", "order")


def program(nc, dram, stages):
    with ExitStack() as ctx:
        m = Mem(nc)
        m.x = ctx.enter_context(nc.sbuf_tensor("x", [P, NT], F32))
        m.scratch = ctx.enter_context(nc.sbuf_tensor("scratch", [P, 2], F32))
        m.psum = ctx.enter_context(nc.psum_tensor("banks", [P, 8 * BLK], F32))
        m.ps = [m.psum[:, cols(i)] for i in range(8)]
        loads, bufs = [(m.x, dram["x"])], []
        for name in CONSTS:
            a = dram[name]
            bufs.append(ctx.enter_context(nc.sbuf_tensor("c_" + name, list(a.shape), a.dtype)))
            loads.append((bufs[-1], a))
        (m.avg, m.headsum, m.headavg, m.headsel, m.vmask, m.ident, m.band32, m.hmask, m.omask, m.qsel, m.headscale,
         m.order) = bufs
        m.identb = ctx.enter_context(nc.sbuf_tensor("identb", [P, P], BF16))
        m.band = ctx.enter_context(nc.sbuf_tensor("band", [P, KT], BF16))
        m.eps = ctx.enter_context(nc.sbuf_tensor("eps", [P, 5], F32))
        loaded = m.sem("loaded")
        with nc.Block() as block:
            @block.gpsimd
            def _(pool):
                for i, eps in enumerate((1e-5, 1e-6, 1e-8, 0.5 * math.log(NORM_SCALE), 1.0)):
                    nc.gpsimd.memset(m.eps[:, i:i + 1], eps)

            @block.sync
            def _(sp):
                for buf, a in loads:
                    sp.dma_start(buf[:, :], a).then_inc(loaded, 16)
                sp.wait_ge(loaded, 16 * len(loads))
        with nc.Block() as block:
            @block.vector
            def _(dve):
                nc.vector.tensor_copy(m.identb[:, :], m.ident[:, :])
                nc.vector.tensor_copy(m.band[:, :], m.band32[:, :])
        for stage in stages:
            stage(nc, m, dram)
            m.release()
        stored = m.sem("stored")
        with nc.Block() as block:
            @block.sync
            def _(sp):
                sp.dma_start(dram["out"], m.x[:, :]).then_inc(stored, 16)
                sp.wait_ge(stored, 16)




def constants():
    part = np.arange(P)
    head = part // HD
    same = head[:, None] == head[None, :]
    key, query = np.arange(KT), part % QT
    inside = (key[None, :] > query[:, None]) & (key[None, :] <= query[:, None] + WIN)
    f = np.float32
    return {
        "avg": np.full((P, P), 1.0 / P, f),
        "headsum": same.astype(f),
        "headavg": same.astype(f) / f(HD),
        "headsel": (head[:, None] == np.arange(NHEAD)[None, :]).astype(f),
        "vmask": (part[:, None] % HD == np.arange(HD)[None, :]).astype(f),
        "ident": np.eye(P, dtype=f),
        "band": np.where(inside, 0.0, OUTSIDE).astype(f),
        "hmask": (head[:, None] % HG == np.arange(HG)[None, :]).astype(f),
        "omask": (part[:, None] // QT == np.arange(HALF)[None, :] // HD).astype(f),
        "headscale": ((part[:, None] // AHD == part[None, :] // AHD) / np.sqrt(AHD)).astype(f),
        "order": np.tile(np.arange(NEXP, 0, -1), (P, 1)).astype(f),
        "qsel": (query[:, None] == np.arange(QT)[None, :]).astype(f),
    }


def host_layout(inputs):
    a = {k: np.asarray(v) for k, v in inputs.items()}
    out = {"x": a["L0_attn_x"].reshape(NT, P).T}
    for name in ("encoder_query", "encoder_value"):
        out["L0_attn_" + name] = a["L0_attn_" + name].transpose(1, 0, 2).reshape(P, P)
    for name in ("mn_w1", "mn_w2", "decoder"):
        out["L0_attn_" + name] = a["L0_attn_" + name]
    for name in ("mn_b1", "mn_b2", "base_metric"):
        out["L0_attn_" + name] = a["L0_attn_" + name].reshape(-1, 1)
    u, v = a["L0_attn_hebbian_U"], a["L0_attn_hebbian_V"]
    rank = u.shape[2]
    for name in ("hebbian_U", "hebbian_V"):
        out["L0_attn_" + name] = np.zeros((NHEAD * rank, P), u.dtype)
    for h in range(NHEAD):
        rows, channels = slice(h * rank, (h + 1) * rank), slice(h * HD, (h + 1) * HD)
        out["L0_attn_hebbian_U"][rows, channels] = u[h].T
        out["L0_attn_hebbian_V"][rows, channels] = v[h]
    for name in ("ln1_w", "ln1_b", "out_proj_b", "ln2_w", "ln2_b"):
        out["L0_ffn_" + name] = a["L0_ffn_" + name].reshape(P, 1)
    out["L0_ffn_in_proj_b"] = a["L0_ffn_in_proj_b"].reshape(3, P).T
    for name in ("in_proj_w", "out_proj_w", "router_w"):
        out["L0_ffn_" + name] = a["L0_ffn_" + name].T
    for name in ("w1", "w2"):
        out["L0_ffn_" + name] = a["L0_ffn_" + name]
    for name in ("Wq", "Wk", "Wv", "Wf1", "Wf2", "Wog1", "Wog2", "Wo"):
        out["L1_attn_" + name] = a["L1_attn_" + name]
    out["L1_attn_Wbeta"] = np.repeat(a["L1_attn_Wbeta"], HD, axis=1)
    out["L1_attn_norm_w"] = a["L1_attn_norm_w"].reshape(P, 1)
    for name in ("Wr", "Wg", "Wu", "Wd", "Sg", "Su", "Sd"):
        out["L1_ffn_" + name] = a["L1_ffn_" + name]
    return {k: np.ascontiguousarray(v) for k, v in out.items()}


def kernel(**inputs):
    from concourse import bacc
    from concourse.bass_utils import run_bass_kernel_spmd

    nc = bacc.Bacc("TRN2", target_bir_lowering=False, num_devices=1)
    arrays = {**host_layout(inputs), **constants()}
    dram = {name: nc.dram_tensor("in_" + name, a.shape, mybir.dt.from_np(a.dtype), kind="ExternalInput").ap()
            for name, a in arrays.items()}
    dram["out"] = nc.dram_tensor("out", [P, NT], F32, kind="ExternalOutput").ap()
    dram["o_scratch"] = nc.dram_tensor("o_scratch", [B, HD, NHEAD, T], F32, kind="Internal").ap()
    program(nc, dram, LAYERS)
    r = run_bass_kernel_spmd(nc, [{"in_" + name: a for name, a in arrays.items()}], core_ids=[0])
    return np.ascontiguousarray(r.results[0]["out"].T).reshape(B, T, P)
```

```python
import math
from contextlib import ExitStack

import concourse.bass as bass
import numpy as np
from concourse import mybir

F32 = mybir.dt.float32
BF16 = mybir.dt.bfloat16
ALU = mybir.AluOpType
ACT = mybir.ActivationFunctionType
AX = mybir.AxisListType

P = 128
B, T = 8, 256
NT = B * T
BLK = 512
NBLK = NT // BLK
BB = BLK // T
HD = 16
NHEAD = P // HD
LN_EPS = 1e-5


LOG_EXP = "natural_log_exp_and_others"


class Mem:

    def __init__(self, nc):
        self.nc, self.semaphores = nc, []

    def sem(self, name):
        self.semaphores.append(self.nc.alloc_semaphore(name))
        return self.semaphores[-1]

    def release(self):
        self.nc.clear_and_free_semaphores(self.semaphores)
        self.nc.all_engine_barrier()
        self.semaphores = []


def cols(n, width=BLK):
    return slice(n * width, (n + 1) * width)


def load_all(nc, m, name, loads):
    w_loaded = m.sem(name + "_loaded")
    with nc.Block() as block:
        @block.sync
        def _(sp):
            for dst, src in loads:
                sp.dma_start(dst, src).then_inc(w_loaded, 16)
            sp.wait_ge(w_loaded, 16 * len(loads))


def layernorm(nc, m, name, src, dst, weight=None, bias=None):
    with ExitStack() as ctx:
        xc = ctx.enter_context(nc.sbuf_tensor(f"{name}_centred", [P, NT], F32))
        sq = ctx.enter_context(nc.sbuf_tensor(f"{name}_squares", [P, NT], F32))
        rstd = ctx.enter_context(nc.sbuf_tensor(f"{name}_rstd", [P, NT], F32))
        mean_done, centred, squared, var_done, logged, rstd_done, normed, scaled = (
            m.sem(f"{name}_{s}")
            for s in ("mean", "centred", "squared", "var", "log", "rstd", "normed", "scaled"))
        block = ctx.enter_context(nc.Block())

        @block.tensor
        def _(pe):
            for n in range(NBLK):
                nc.tensor.matmul(m.ps[n][:, :], m.avg[:, :], src[:, cols(n)],
                                 start=True, stop=True).then_inc(mean_done, 1)
            for n in range(NBLK):
                pe.wait_ge(squared, n + 1)
                nc.tensor.matmul(m.ps[NBLK + n][:, :], m.avg[:, :], sq[:, cols(n)],
                                 start=True, stop=True).then_inc(var_done, 1)

        @block.scalar
        def _(act):
            nc.scalar.preload_act_table_set(LOG_EXP)
            for n in range(NBLK):
                act.wait_ge(centred, n + 1)
                nc.scalar.activation(sq[:, cols(n)], xc[:, cols(n)], ACT.Square).then_inc(squared, 1)
            for n in range(NBLK):
                act.wait_ge(var_done, n + 1)
                nc.scalar.activation(rstd[:, cols(n)], m.ps[NBLK + n][:, :], ACT.Ln,
                                     bias=m.eps[:, 0:1]).then_inc(logged, 1)
                act.wait_ge(logged, n + 1)
                nc.scalar.activation(rstd[:, cols(n)], rstd[:, cols(n)], ACT.Exp, scale=-0.5).then_inc(rstd_done, 1)

        @block.vector
        def _(dve):
            for n in range(NBLK):
                dve.wait_ge(mean_done, n + 1)
                nc.vector.tensor_tensor(xc[:, cols(n)], src[:, cols(n)], m.ps[n][:, :],
                                        ALU.subtract).then_inc(centred, 1)
            for n in range(NBLK):
                dve.wait_ge(centred, n + 1)
                dve.wait_ge(rstd_done, n + 1)
                nc.vector.tensor_tensor(dst[:, cols(n)], xc[:, cols(n)], rstd[:, cols(n)],
                                        ALU.mult).then_inc(normed, 1)
                if weight is not None:
                    dve.wait_ge(normed, n + 1)
                    nc.vector.tensor_scalar(dst[:, cols(n)], dst[:, cols(n)], weight, bias,
                                            ALU.mult, ALU.add).then_inc(scaled, 1)


PAD = 64
WIN = 64
TOPK = 32
QT = 32
KT = QT + WIN
HG = 4
NQT = T // QT
GT = 4
NG = NQT * (NHEAD // HG) // GT
HALF = HG * HD
ROUNDS = TOPK // 8
TAKEN = -3.0e38
OUTSIDE = -1.0e15
GATE2 = float(0.2) ** 2
NORM_SCALE = 2.0 ** 30


class Tally:

    def __init__(self, m, name, units, per=1, credit=0):
        self.sem = m.sem(name)
        self.units, self.per, self.credit = units, per, credit * per

    def done(self, step, unit, j=None):
        j = self.per - 1 if j is None else j
        return step * (self.units * self.per) + (unit * self.per + self.credit + j + 1)


def give_credit(pool, tallies):
    for t in tallies:
        if t.credit:
            pool.sem_inc(t.sem, t.credit)


def distance_queries(nc, m, w, z, qpad, metric):
    with ExitStack() as ctx:
        def sb(name, shape):
            return ctx.enter_context(nc.sbuf_tensor(name, shape, F32))

        def sem(name):
            return m.sem(name)

        total, every8, sig = sb("a_total", [P, B]), sb("a_every8", [P, B]), sb("a_sig", [P, B])
        hidden, arg, size, tail = sb("a_hidden", [P // 2, B]), sb("a_arg", [P, B]), sb("a_size", [P, B]), sb("a_tail", [P, B])
        base01 = sb("a_base01", [P, 1])
        q_done, relu_done, sums, sig_done, hid_done, gelu_done, mod_done, arg_done, size_done, act_done, based = map(
            sem, ("a_q", "a_relu", "a_sums", "a_sigd", "a_hid", "a_gelu", "a_mod", "a_argd", "a_sized", "a_act", "a_based"))
        hm_done, hm_copied = sem("a_hm"), sem("a_hmc")
        block = ctx.enter_context(nc.Block())

        @block.tensor
        def _(pe):
            for n in range(NBLK):
                nc.tensor.matmul(m.ps[n][:, :], w["encoder_query"], z[:, cols(n)], start=True, stop=True).then_inc(q_done, 1)
            nc.tensor.matmul(m.ps[5][:, 0:P], w["hebbian_U"], w["hebbian_V"], start=True, stop=True).then_inc(hm_done, 1)
            pe.wait_ge(sig_done, 1)
            nc.tensor.matmul(m.ps[4][0:P // 2, 0:B], w["mn_w1"], sig[:, :], start=True, stop=True).then_inc(hid_done, 1)
            pe.wait_ge(gelu_done, 1)
            nc.tensor.matmul(m.ps[6][:, 0:B], w["mn_w2"], hidden[:, :], start=True, stop=True).then_inc(mod_done, 1)

        @block.scalar
        def _(act):
            for n in range(NBLK):
                act.wait_ge(q_done, n + 1)
                nc.scalar.activation(qpad[:, n * BB:(n + 1) * BB, PAD:], m.ps[n][:, :].rearrange("p (b t) -> p b t", b=BB),
                                     ACT.Relu).then_inc(relu_done, 1)
            act.wait_ge(hm_done, 1)
            nc.scalar.copy(w["hebbian"], m.ps[5][:, 0:P]).then_inc(hm_copied, 1)
            act.wait_ge(hid_done, 1)
            nc.scalar.activation(hidden[:, :], m.ps[4][0:P // 2, 0:B], ACT.Gelu, bias=w["mn_b1"]).then_inc(gelu_done, 1)
            nc.scalar.preload_act_table_set(LOG_EXP)
            act.wait_ge(size_done, 1)
            nc.scalar.activation(tail[:, :], size[:, :], ACT.Exp, scale=-1.0).then_inc(act_done, 1)
            act.wait_ge(act_done, 1)
            nc.scalar.activation(tail[:, :], tail[:, :], ACT.Ln, bias=m.eps[:, 4:5]).then_inc(act_done, 1)

        @block.gpsimd
        def _(pool):
            for n in range(NBLK):
                pool.wait_ge(relu_done, n + 1)
                for b in range(n * BB, (n + 1) * BB):
                    nc.gpsimd.tensor_copy(qpad[:, b, 0:PAD], qpad[:, b, PAD:PAD + 1].to_broadcast([P, PAD]))

        @block.vector
        def _(dve):
            for n in range(NBLK):
                bs = slice(n * BB, (n + 1) * BB)
                dve.wait_ge(relu_done, n + 1)
                nc.vector.tensor_reduce(total[:, bs], qpad[:, bs, PAD:], AX.X, ALU.add).then_inc(sums, 1)
                nc.vector.tensor_reduce(every8[:, bs], qpad[:, bs, PAD:PAD + T:8], AX.X, ALU.add).then_inc(sums, 1)
            dve.wait_ge(sums, 2 * NBLK)
            nc.vector.tensor_scalar(every8[:, :], every8[:, :], 0.5 * 8 / T, None, ALU.mult).then_inc(sums, 1)
            dve.wait_ge(sums, 2 * NBLK + 1)
            nc.vector.scalar_tensor_tensor(sig[:, :], total[:, :], 1.0 / T, every8[:, :], ALU.mult, ALU.add).then_inc(sig_done, 1)
            nc.vector.scalar_tensor_tensor(base01[:, :], w["mn_b2"], 0.1, w["base_metric"], ALU.mult, ALU.add).then_inc(based, 1)
            dve.wait_ge(mod_done, 1)
            dve.wait_ge(based, 1)
            nc.vector.tensor_scalar(arg[:, :], m.ps[6][:, 0:B], 0.1, base01[:, :], ALU.mult, ALU.add).then_inc(arg_done, 1)
            dve.wait_ge(arg_done, 1)
            nc.vector.scalar_tensor_tensor(size[:, :], arg[:, :], -1.0, arg[:, :], ALU.mult, ALU.max).then_inc(size_done, 1)
            dve.wait_ge(act_done, 2)
            nc.vector.scalar_tensor_tensor(metric[:, :], arg[:, :], 0.0, tail[:, :], ALU.max, ALU.add).then_inc(arg_done, 1)
            dve.wait_ge(arg_done, 2)


def distance_attention(nc, m, w, z, qpad, metric):
    with ExitStack() as ctx:
        def sb(name, shape, n=2):
            return [ctx.enter_context(nc.sbuf_tensor(f"{name}{i}", shape, F32)) for i in range(n)]

        def tally(name, per=1, credit=0):
            return Tally(m.sem("b_" + name), per, credit)

        xp = sb("b_xp", [P, PAD + T])
        q2m, mk2 = sb("b_q2m", [P, T]), sb("b_mk2", [P, PAD + T])
        keys = [sb(f"b_keys{i}", [P, PAD + T]) for i in range(2)]
        lhs = [sb(f"b_lhs{i}", [P, NQT, HG, QT]) for i in range(2)]
        vwin = sb("b_vwin", [KT, NQT, NHEAD // HG, HALF + 1])
        qsq, n2c, inv, gate, heb, ctxt, outb = (sb("b_" + s, [P, T], 1)[0] for s in (
            "qsq", "n2c", "inv", "gate", "heb", "ctxt", "outb"))
        metric2 = sb("b_metric2", [P, B], 1)[0]
        top = [sb(f"b_top{r}_", [P, GT, 8]) for r in range(ROUNDS)]
        left, weight, dist = sb("b_left", [P, GT, KT]), sb("b_weight", [P, GT, KT]), sb("b_dist", [P, GT, KT])
        value, (spare, spare_act) = sb("b_value", [P, GT, KT]), sb("b_spare", [P, 12])
        weightT = sb("b_weightT", [KT, GT * P])
        rden, chead = sb("b_rden", [P, GT]), sb("b_chead", [P, GT, HALF])

        tallies = []

        def tally(name, units, per=1, credit=0):
            tallies.append(Tally(m, "b_" + name, units, per, credit))
            return tallies[-1]

        S, G = 2, 2 * NG
        t_xp, t_q2m, t_mk2 = tally("xp", S, 2), tally("q2m", S), tally("mk2", S)
        t_keys, t_lhs, t_vps, t_vw = tally("keys", S, 4, 2), tally("lhs", S, 2, 2), tally("vps", S, 2, 2), tally("vw", S, 2, 1)
        t_qsq, t_nh, t_n2c, t_inv = tally("qsq", S), tally("nh", S, 1, 1), tally("n2c", S, 2), tally("inv", S, 2)
        t_heb, t_ctx, t_out, t_dec, t_x = (tally("heb", S, 2, 1), tally("ctx", S, 1, 1), tally("out", S),
                                           tally("dec", S, 1, 1), tally("x", S, 1, 1))
        t_score, t_top, t_taken, t_self = (tally("score", G, 1, 4), tally("top", G, GT),
                                           tally("taken", G, GT), tally("self", G, GT))
        t_value, t_step = tally("value", G, 1, 2), m.sem("b_step")
        t_log, t_dist, t_infl, t_weight = tally("log", G), tally("dist", G), tally("infl", G), tally("weight", G, 1, 2)
        t_tr, t_wT, t_cx, t_rden, t_chead, t_cxT = (tally("tr", G, 1, 2), tally("wT", G, 1, 1), tally("cx", G, 1, 8),
                                                    tally("rden", G, 2), tally("chead", G, GT, 1), tally("cxT", G, 1, 2))
        b_score, b_v, b_tr, b_cx, b_cxT, b_nh, b_dec = [m.ps[0], m.ps[1]], m.ps[2], m.ps[3], m.ps[4], m.ps[5], m.ps[6], m.ps[7]

        preset = m.sem("b_preset")
        with nc.Block() as block:
            @block.gpsimd
            def _(pool):
                for i in range(2):
                    nc.gpsimd.memset(vwin[i][:, :, :, HALF:HALF + 1], 1.0).then_inc(preset, 1)
                pool.wait_ge(preset, 2)
                for i in range(2):
                    for hg in range(2):
                        sq = slice(HALF * (1 - hg), HALF * (2 - hg))
                        nc.gpsimd.tensor_scalar(lhs[hg][i][sq, :, :, :],
                                                m.hmask[sq, :].unsqueeze(1).unsqueeze(3).to_broadcast([HALF, NQT, HG, QT]),
                                                -1.0, None, ALU.mult).then_inc(preset, 1)
                        pool.wait_ge(preset, 2 * i + hg + 3)
                give_credit(pool, tallies)

            @block.vector
            def _(dve):
                nc.vector.tensor_scalar(metric2[:, :], metric[:, :], 2.0, None, ALU.mult)

        block = ctx.enter_context(nc.Block())

        def wait(eng, t, step, unit, j=None):
            eng.wait_ge(t.sem, t.done(step, unit, j))

        def column(a, b):
            return a[:, bass.ds(b, 1)]

        def queries(b, start=PAD, n=T):
            return qpad[:, bass.ds(b, 1), start:start + n].rearrange("p o t -> p (o t)")

        @block.gpsimd
        def _(pool):
            with pool.Fori(0, B // 2) as step:
                for i in range(2):
                    b = step * 2 + i
                    wait(pool, t_vps, step, i - 2)
                    nc.gpsimd.tensor_copy(xp[i][:, PAD:], z[:, bass.ds(b * T, T)]).then_inc(t_xp.sem, 1)
                    nc.gpsimd.tensor_copy(xp[i][:, 0:PAD], z[:, bass.ds(b * T, 1)].to_broadcast([P, PAD])).then_inc(t_xp.sem, 1)
                    wait(pool, t_q2m, step, i)
                    wait(pool, t_score, step, NG * (i - 1) - 1)
                    wait(pool, t_xp, step, i)
                    for hg in range(2):
                        own = slice(HALF * hg, HALF * (hg + 1))
                        nc.gpsimd.tensor_tensor(
                            lhs[hg][i][own, :, :, :],
                            q2m[i][own, :].rearrange("p (w q) -> p w q", q=QT).unsqueeze(2).to_broadcast([HALF, NQT, HG, QT]),
                            m.hmask[own, :].unsqueeze(1).unsqueeze(3).to_broadcast([HALF, NQT, HG, QT]),
                            ALU.mult).then_inc(t_lhs.sem, 1)
                    wait(pool, t_lhs, step, i)

        @block.tensor
        def _(pe):
            def scores(step, i, g):
                hg, w0 = g // (NG // 2), g % (NG // 2) * GT
                bank = b_score[g % 2]
                wait(pe, t_value, step, i * NG + g - 2)
                if g == 0:
                    wait(pe, t_keys, step, i)
                    wait(pe, t_lhs, step, i)
                for t in range(GT):
                    q0 = (w0 + t) * QT
                    nc.tensor.matmul(bank[:, t * KT:(t + 1) * KT], m.identb[:, :], m.band[:, :], start=True, stop=False)
                    mm = nc.tensor.matmul(bank[:, t * KT:(t + 1) * KT],
                                          lhs[hg][i][:, w0 + t, :, :].rearrange("p h q -> p (h q)"),
                                          keys[hg][i][:, q0:q0 + KT], start=False, stop=True)
                mm.then_inc(t_score.sem, 1)

            def values(step, i):
                wait(pe, t_xp, step, i)
                for half in range(2):
                    wait(pe, t_vw, step, i, half - 1)
                    for t in range(NQT // 2):
                        q0 = (half * (NQT // 2) + t) * QT
                        mm = nc.tensor.matmul(b_v[0:KT, t * P:(t + 1) * P], xp[i][:, q0:q0 + KT],
                                              w["encoder_value"], start=True, stop=True)
                    mm.then_inc(t_vps.sem, 1)

            def transposes(step, unit):
                wait(pe, t_weight, step, unit)
                wait(pe, t_wT, step, unit - 1)
                for t in range(GT):
                    mm = nc.tensor.transpose(b_tr[0:KT, t * P:(t + 1) * P], weight[unit % 2][:, t, :], m.ident[:, :])
                mm.then_inc(t_tr.sem, 1)

            def contexts(step, unit):
                i, g = divmod(unit, NG)
                hg, w0 = g // (NG // 2), g % (NG // 2) * GT
                wait(pe, t_wT, step, unit)
                wait(pe, t_chead, step, unit - 1)
                if g == 0:
                    wait(pe, t_vw, step, i)
                for t in range(GT):
                    mm = nc.tensor.matmul(b_cx[:, t * P:t * P + HALF + 1], weightT[unit % 2][:, t * P:(t + 1) * P],
                                          vwin[i][:, w0 + t, hg, :], start=True, stop=True)
                mm.then_inc(t_cx.sem, 1)

            def heads_together(step, unit):
                i, g = divmod(unit, NG)
                hg, w0 = g // (NG // 2), g % (NG // 2) * GT
                wait(pe, t_chead, step, unit)
                if g == 0:
                    wait(pe, t_ctx, step, i - 1)
                for t in range(GT):
                    q0 = (w0 + t) * QT
                    mm = nc.tensor.matmul(b_cxT[HALF * hg:HALF * (hg + 1), q0:q0 + QT], chead[unit % 2][:, t, :],
                                          m.qsel[:, :], start=True, stop=True)
                mm.then_inc(t_cxT.sem, 1)

            def sequence(step, i):
                values(step, i)
                wait(pe, t_qsq, step, i)
                wait(pe, t_heb, step, i - 1)
                nc.tensor.matmul(b_nh[:, 0:T], m.headsum[:, :], qsq[:, :], start=True, stop=True)
                nc.tensor.matmul(b_nh[:, T:2 * T], w["hebbian"], queries(step * 2 + i),
                                 start=True, stop=True).then_inc(t_nh.sem, 1)

            def decode(step, i):
                wait(pe, t_out, step, i)
                wait(pe, t_x, step, i - 1)
                nc.tensor.matmul(b_dec[:, 0:T], w["decoder"], outb[:, :], start=True, stop=True).then_inc(t_dec.sem, 1)

            with pe.Fori(0, B // 2) as step:
                scores(step, 0, 0)
                scores(step, 0, 1)
                sequence(step, 0)
                for unit in range(G):
                    if unit + 2 < G:
                        scores(step, *divmod(unit + 2, NG))
                    transposes(step, unit)
                    if unit:
                        heads_together(step, unit - 1)
                    contexts(step, unit)
                    if unit == NG - 1:
                        sequence(step, 1)
                    if unit == NG + 2:
                        decode(step, 0)
                heads_together(step, G - 1)
                decode(step, 1)

        @block.scalar
        def _(act):
            def sequence_inputs(step, i):
                b = step * 2 + i
                wait(act, t_lhs, step, i - 2)
                nc.scalar.copy(spare_act[:, 2 * i:2 * i + 1], m.eps[:, 0:1])
                nc.scalar.activation(q2m[i][:, :], queries(b), ACT.Copy, scale=column(metric2, b)).then_inc(t_q2m.sem, 1)
                wait(act, t_score, step, NG * (i - 1) - 1)
                wait(act, t_mk2, step, i)
                for hg in range(2):
                    own, sq = slice(HALF * hg, HALF * (hg + 1)), slice(HALF * (1 - hg), HALF * (2 - hg))
                    nc.scalar.copy(keys[hg][i][own, :], qpad[own, bass.ds(b, 1), :].rearrange("p o t -> p (o t)")
                                   ).then_inc(t_keys.sem, 1)
                    nc.scalar.copy(keys[hg][i][sq, :], mk2[i][own, :]).then_inc(t_keys.sem, 1)
                wait(act, t_nh, step, i - 1)
                nc.scalar.copy(spare_act[:, 2 * i + 1:2 * i + 2], m.eps[:, 0:1])
                nc.scalar.activation(qsq[:, :], queries(b), ACT.Square).then_inc(t_qsq.sem, 1)

            def value_windows(step, i, half):
                wait(act, t_vps, step, i, half)
                wait(act, t_cx, step, i * NG - NG - 1)
                w0 = half * (NQT // 2)
                nc.scalar.activation(vwin[i][:, w0:w0 + NQT // 2, :, 0:HALF],
                                     b_v[0:KT, :].rearrange("k (w g e) -> k w g e", w=NQT // 2, g=2),
                                     ACT.Relu).then_inc(t_vw.sem, 1)

            def copy_scores(step, unit):
                wait(act, t_score, step, unit)
                wait(act, t_weight, step, unit - 2)
                nc.scalar.copy(value[unit % 2][:, :, :], b_score[unit % 2][:, 0:GT * KT].rearrange("p (t k) -> p t k", t=GT)
                               ).then_inc(t_value.sem, 1)

            def distances(step, unit):
                d = dist[unit % 2]
                wait(act, t_weight, step, unit - 2)
                wait(act, t_value, step, unit)
                for t in range(GT):
                    wait(act, t_top, step, unit, t)
                    nc.scalar.activation(d[:, t, :], value[unit % 2][:, t, :], ACT.Identity,
                                         scale=-1.0, bias=top[0][unit % 2][:, t, 0:1]).then_inc(t_self.sem, 1)
                wait(act, t_self, step, unit)
                nc.scalar.activation(d[:, :, :], d[:, :, :], ACT.Ln, bias=m.eps[:, 2:3]).then_inc(t_log.sem, 1)
                wait(act, t_log, step, unit)
                nc.scalar.activation(d[:, :, :], d[:, :, :], ACT.Exp, scale=0.5).then_inc(t_dist.sem, 1)
                wait(act, t_dist, step, unit)
                nc.scalar.activation(d[:, :, :], d[:, :, :], ACT.Exp, scale=-1.0).then_inc(t_infl.sem, 1)

            def transposed(step, unit):
                wait(act, t_tr, step, unit)
                wait(act, t_cx, step, unit - 2)
                nc.scalar.copy(weightT[unit % 2][:, :], b_tr[0:KT, :]).then_inc(t_wT.sem, 1)

            def inverse_norms(step, i):
                wait(act, t_n2c, step, i, 0)
                wait(act, t_heb, step, i - 1)
                nc.scalar.activation(inv[:, :], n2c[:, :], ACT.Ln, scale=NORM_SCALE).then_inc(t_inv.sem, 1)
                wait(act, t_inv, step, i, 0)
                nc.scalar.activation(inv[:, :], inv[:, :], ACT.Exp, scale=-0.5, bias=m.eps[:, 3:4]).then_inc(t_inv.sem, 1)

            nc.scalar.preload_act_table_set(LOG_EXP)
            with act.Fori(0, B // 2) as step:
                sequence_inputs(step, 0)
                copy_scores(step, 0)
                copy_scores(step, 1)
                distances(step, 0)
                value_windows(step, 0, 0)
                value_windows(step, 0, 1)
                for unit in range(G):
                    if unit + 1 < G:
                        distances(step, unit + 1)
                    transposed(step, unit)
                    if unit == 0:
                        sequence_inputs(step, 1)
                    if unit + 2 < G:
                        copy_scores(step, unit + 2)
                    if unit == NG - 1:
                        value_windows(step, 1, 0)
                        value_windows(step, 1, 1)
                    if unit % NG == 1:
                        inverse_norms(step, unit // NG)

        @block.vector
        def _(dve):
            def squares(step, i):
                b = step * 2 + i
                wait(dve, t_keys, step, i - 2)
                all_q = qpad[:, bass.ds(b, 1), :].rearrange("p o t -> p (o t)")
                nc.vector.scalar_tensor_tensor(mk2[i][:, :], all_q, column(metric, b), all_q,
                                               ALU.mult, ALU.mult).then_inc(t_mk2.sem, 1)

            def carry(j):
                nc.vector.memset(spare[:, j:j + 1], 0.0)

            def select(step, i, g):
                unit, k = i * NG + g, g % 2
                base = unit * 2 * GT * (ROUNDS - 1)
                for r in range(ROUNDS):
                    src = value[k] if r == 0 else left[k]
                    if r == 0:
                        wait(dve, t_value, step, unit)
                        carry(3 * (g % 4) + 0)
                    for t in range(GT):
                        if r == 1 and t == 0:
                            wait(dve, t_taken, step, unit)
                            carry(3 * (g % 4) + 1)
                        elif r > 1:
                            dve.wait_ge(t_step, base + (2 * r - 3) * GT + t + 1)
                        ins = nc.vector.max(top[r][k][:, t, :], src[:, t, :])
                        ins.then_inc(t_top.sem, 1) if r == 0 else ins.then_inc(t_step, 1)
                    for t in range(GT):
                        if r == 0 and t == 0:
                            wait(dve, t_top, step, unit)
                            carry(3 * (g % 4) + 2)
                        elif r:
                            dve.wait_ge(t_step, base + (2 * r - 2) * GT + t + 1)
                        ins = nc.vector.match_replace(left[k][:, t, :], top[r][k][:, t, :], src[:, t, :], TAKEN)
                        ins.then_inc(t_taken.sem, 1) if r == 0 else ins.then_inc(t_step, 1)
                dve.wait_ge(t_step, base + 2 * GT * (ROUNDS - 1))
                wait(dve, t_infl, step, unit)
                wait(dve, t_tr, step, unit - 2)
                nc.vector.scalar_tensor_tensor(weight[k][:, :, :], left[k][:, :, :], TAKEN, dist[k][:, :, :],
                                               ALU.is_equal, ALU.mult).then_inc(t_weight.sem, 1)

            def normalise(step, unit):
                k = unit % 2
                cx = b_cx[:, :].rearrange("p (t e) -> p t e", t=GT)
                wait(dve, t_cx, step, unit)
                nc.vector.tensor_scalar(rden[k][:, :], cx[:, :, HALF], 1e-8, None, ALU.add).then_inc(t_rden.sem, 1)
                wait(dve, t_rden, step, unit, 0)
                nc.vector.reciprocal(rden[k][:, :], rden[k][:, :]).then_inc(t_rden.sem, 1)
                wait(dve, t_rden, step, unit)
                wait(dve, t_cxT, step, unit - 2)
                for t in range(GT):
                    nc.vector.scalar_tensor_tensor(chead[k][:, t, :], cx[:, t, 0:HALF], rden[k][:, t:t + 1], m.omask[:, :],
                                                   ALU.mult, ALU.mult).then_inc(t_chead.sem, 1)

            def norms(step, i):
                wait(dve, t_nh, step, i)
                nc.vector.tensor_scalar(n2c[:, :], b_nh[:, 0:T], 1e-24, None, ALU.max).then_inc(t_n2c.sem, 1)
                nc.vector.tensor_scalar(gate[:, :], b_nh[:, 0:T], GATE2, 0.1, ALU.is_gt, ALU.mult).then_inc(t_n2c.sem, 1)

            def hebbian(step, i):
                wait(dve, t_n2c, step, i)
                wait(dve, t_inv, step, i)
                nc.vector.tensor_tensor(gate[:, :], gate[:, :], inv[:, :], ALU.mult).then_inc(t_heb.sem, 1)
                wait(dve, t_heb, step, i, 0)
                nc.vector.tensor_tensor(heb[:, :], b_nh[:, T:2 * T], gate[:, :], ALU.mult).then_inc(t_heb.sem, 1)

            def finish(step, i):
                b = step * 2 + i
                wait(dve, t_cxT, step, i * NG + NG - 1)
                wait(dve, t_heb, step, i)
                nc.vector.tensor_tensor(ctxt[:, :], b_cxT[:, 0:T], heb[:, :], ALU.add).then_inc(t_ctx.sem, 1)
                wait(dve, t_ctx, step, i)
                wait(dve, t_dec, step, i - 1)
                nc.vector.tensor_tensor(outb[:, :], ctxt[:, :], queries(b), ALU.mult).then_inc(t_out.sem, 1)

            def residual(step, i):
                here = m.x[:, bass.ds((step * 2 + i) * T, T)]
                wait(dve, t_dec, step, i)
                nc.vector.tensor_tensor(here, here, b_dec[:, 0:T], ALU.add).then_inc(t_x.sem, 1)

            with dve.Fori(0, B // 2) as step:
                squares(step, 0)
                squares(step, 1)
                for unit in range(G):
                    i, g = divmod(unit, NG)
                    select(step, i, g)
                    if unit:
                        normalise(step, unit - 1)
                    if g == 0:
                        norms(step, i)
                    if unit == NG + 1:
                        finish(step, 0)
                    if g == 2:
                        hebbian(step, i)
                    if unit == G - 1:
                        residual(step, 0)
                normalise(step, G - 1)
                finish(step, 1)
                residual(step, 1)
                dve.wait_ge(t_step, G * 2 * GT * (ROUNDS - 1))
                dve.sem_clear(t_step)


def distance_layer(nc, m, dram):
    names = ("encoder_query", "encoder_value", "mn_w1", "mn_b1", "mn_w2", "mn_b2", "base_metric", "decoder",
             "hebbian_U", "hebbian_V")
    with ExitStack() as ctx:
        def sb(name, shape):
            return ctx.enter_context(nc.sbuf_tensor(name, shape, F32))

        w, loads = {"hebbian": sb("w_hebbian", [P, P])[:, :]}, []
        for name in names:
            a = dram["L0_attn_" + name]
            w[name] = sb("w_" + name, list(a.shape))[:, :]
            loads.append((w[name], a))
        z, qpad, metric = sb("a_z", [P, NT]), sb("a_qpad", [P, B, PAD + T]), sb("a_metric", [P, B])
        load_all(nc, m, "distance_layer", loads)
        layernorm(nc, m, "ln0", m.x, z)
        distance_queries(nc, m, w, z, qpad, metric)
        distance_attention(nc, m, w, z, qpad, metric)



UNROLL = 16
PAIRS = UNROLL // 2
OGRP = 8


def delta_inputs(nc, m, w, z, pT, kT, gT, fT, qT, vT):
    with ExitStack() as ctx:
        def sb(name, shape):
            return ctx.enter_context(nc.sbuf_tensor(name, shape, F32))

        def sem(name):
            return m.sem(name)

        kraw, beta, f = sb("d_kraw", [P, NT]), sb("d_beta", [P, NT]), sb("d_f", [P, NT])
        f1 = sb("d_f1", [HD, NT])
        ksq, rk, kn = sb("d_ksq", [P, NT]), sb("d_rk", [P, NT]), sb("d_kn", [P, NT])
        kf, kkf, bk = sb("d_kf", [P, NT]), sb("d_kkf", [P, NT]), sb("d_bk", [P, NT])
        qkv_done, silu_done, f1_done, f1_copied, f2_done, beta_done, sig_done = map(
            sem, ("d_qkv", "d_silu", "d_f1d", "d_f1c", "d_f2", "d_bd", "d_sig"))
        ksq_done, knorm_done, s_done, dch, kkf_done, rk_log, rk_done = map(
            sem, ("d_sq", "d_kno", "d_s", "d_ch", "d_kkfd", "d_rklog", "d_rkd"))
        block = ctx.enter_context(nc.Block())

        def tb(a, n):
            return a[:, cols(n)].rearrange("p (b t) -> p b t", b=BB)

        def bt(a, n):
            return a[:, 0:T, n * BB:(n + 1) * BB].rearrange("p t b -> p b t")

        @block.tensor
        def _(pe):
            for n in range(NBLK):
                for j, name in enumerate(("Wq", "Wk", "Wv")):
                    if 3 * n + j >= 6:
                        pe.wait_ge(silu_done, 3 * n + j - 5)
                    nc.tensor.matmul(m.ps[(3 * n + j) % 6][:, :], w[name], z[:, cols(n)],
                                     start=True, stop=True).then_inc(qkv_done, 1)
            for n in range(NBLK):
                if n >= 2:
                    pe.wait_ge(f1_copied, n - 1)
                nc.tensor.matmul(m.ps[6 + n % 2][0:HD, :], w["Wf1"], z[:, cols(n)],
                                 start=True, stop=True).then_inc(f1_done, 1)
            for n in range(NBLK):
                pe.wait_ge(silu_done, 3 * NBLK)
                pe.wait_ge(f1_copied, n + 1)
                if n >= 2:
                    pe.wait_ge(sig_done, 2 * (n - 1))
                nc.tensor.matmul(m.ps[n % 2][:, :], w["Wf2"], f1[:, cols(n)],
                                 start=True, stop=True).then_inc(f2_done, 1)
                nc.tensor.matmul(m.ps[2 + n % 2][:, :], w["Wbeta"], z[:, cols(n)],
                                 start=True, stop=True).then_inc(beta_done, 1)
            for n in range(NBLK):
                pe.wait_ge(ksq_done, n + 1)
                if n >= 1:
                    pe.wait_ge(dch, 7 * n)
                nc.tensor.matmul(m.ps[4][:, :], m.headsum[:, :], ksq[:, cols(n)],
                                 start=True, stop=True).then_inc(knorm_done, 1)
                pe.wait_ge(kkf_done, n + 1)
                nc.tensor.matmul(m.ps[5][:, :], m.headsum[:, :], kkf[:, cols(n)],
                                 start=True, stop=True).then_inc(s_done, 1)

        @block.scalar
        def _(act):
            for n in range(NBLK):
                for j, out in enumerate((bt(qT, n), tb(kraw, n), bt(vT, n))):
                    act.wait_ge(qkv_done, 3 * n + j + 1)
                    nc.scalar.activation(out, m.ps[(3 * n + j) % 6][:, :].rearrange(
                        "p (b t) -> p b t", b=BB), ACT.Silu).then_inc(silu_done, 1)
                act.wait_ge(silu_done, 3 * n + 2)
                nc.scalar.activation(ksq[:, cols(n)], kraw[:, cols(n)], ACT.Square).then_inc(ksq_done, 1)
            for n in range(NBLK):
                act.wait_ge(f1_done, n + 1)
                nc.scalar.copy(f1[:, cols(n)], m.ps[6 + n % 2][0:HD, :]).then_inc(f1_copied, 1)
            for n in range(NBLK):
                act.wait_ge(f2_done, n + 1)
                nc.scalar.activation(f[:, cols(n)], m.ps[n % 2][:, :], ACT.Sigmoid).then_inc(sig_done, 1)
                act.wait_ge(beta_done, n + 1)
                nc.scalar.activation(beta[:, cols(n)], m.ps[2 + n % 2][:, :], ACT.Sigmoid).then_inc(sig_done, 1)
            nc.scalar.preload_act_table_set(LOG_EXP)
            for n in range(NBLK):
                act.wait_ge(knorm_done, n + 1)
                nc.scalar.activation(rk[:, cols(n)], m.ps[4][:, :], ACT.Ln, bias=m.eps[:, 1:2]).then_inc(rk_log, 1)
                act.wait_ge(rk_log, n + 1)
                nc.scalar.activation(rk[:, cols(n)], rk[:, cols(n)], ACT.Exp, scale=-0.5).then_inc(rk_done, 1)

        @block.vector
        def _(dve):
            for n in range(NBLK):
                c, base = cols(n), 7 * n
                dve.wait_ge(rk_done, n + 1)
                nc.vector.tensor_tensor(kn[:, c], kraw[:, c], rk[:, c], ALU.mult).then_inc(dch, 1)
                dve.wait_ge(sig_done, 2 * (n + 1))
                dve.wait_ge(dch, base + 1)
                nc.vector.tensor_tensor(kf[:, c], kn[:, c], f[:, c], ALU.mult).then_inc(dch, 1)
                nc.vector.tensor_scalar(beta[:, c], beta[:, c], 2.0, None, ALU.mult).then_inc(dch, 1)
                dve.wait_ge(dch, base + 3)
                nc.vector.tensor_tensor(kkf[:, c], kn[:, c], kf[:, c], ALU.mult).then_inc(kkf_done, 1)
                nc.vector.scalar_tensor_tensor(bt(gT, n), tb(kf, n), -1.0, tb(beta, n),
                                               ALU.mult, ALU.mult).then_inc(dch, 1)
                nc.vector.tensor_tensor(bk[:, c], kn[:, c], beta[:, c], ALU.mult).then_inc(dch, 1)
                dve.wait_ge(s_done, n + 1)
                dve.wait_ge(dch, base + 5)
                nc.vector.tensor_tensor(bk[:, c], m.ps[5][:, :], bk[:, c], ALU.mult).then_inc(dch, 1)
                dve.wait_ge(dch, base + 6)
                nc.vector.tensor_tensor(bk[:, c], bk[:, c], kf[:, c], ALU.subtract).then_inc(dch, 1)
                dve.wait_ge(dch, base + 7)
                nc.vector.tensor_tensor(bt(pT, n), tb(bk, n), tb(beta, n), ALU.mult)
                nc.vector.tensor_copy(bt(kT, n), tb(kn, n))

        @block.gpsimd
        def _(pool):
            for n in range(NBLK):
                pool.wait_ge(sig_done, 2 * n + 1)
                nc.gpsimd.tensor_copy(bt(fT, n), tb(f, n))


def delta_pairs(nc, m, pre_p, pre_k, post_k, g, f, q, q_dot):
    HALFT = T // 2
    with ExitStack() as ctx:
        def sb(name):
            return ctx.enter_context(nc.sbuf_tensor(name, [P, HALFT, B], F32))

        prod = [sb(f"p_prod{j}") for j in range(4)]
        part = [sb(f"p_part{j}") for j in range(4)]
        prod_done, dot_done, step_done, copied, qdot_done = (m.sem("p_" + n) for n in (
            "prod", "dot", "step", "copied", "qdot"))
        block = ctx.enter_context(nc.Block())

        def even(a):
            return a[:, 0:T:2, :]

        def odd(a):
            return a[:, 1:T:2, :]

        def flat(a, n):
            return a[:, :, :].rearrange("p t b -> p (t b)")[:, cols(n)]

        def dot(j):
            return m.psum[:, j * 2 * BLK:(j + 1) * 2 * BLK].rearrange("p (t b) -> p t b", b=B)

        @block.tensor
        def _(pe):
            for j in range(4):
                pe.wait_ge(prod_done, j + 1)
                for n in range(2):
                    mm = nc.tensor.matmul(m.ps[2 * j + n][:, :], m.headsum[:, :], flat(prod[j], n), start=True, stop=True)
                mm.then_inc(dot_done, 1)

        @block.scalar
        def _(act):
            nc.scalar.copy(odd(post_k), odd(pre_k)).then_inc(copied, 1)

        @block.gpsimd
        def _(pool):
            nc.gpsimd.tensor_tensor(even(q_dot), even(q), even(pre_k), ALU.mult).then_inc(qdot_done, 1)
            nc.gpsimd.tensor_tensor(odd(q_dot), even(q), even(g), ALU.mult).then_inc(qdot_done, 1)

        @block.vector
        def _(dve):
            for j, (a1, a0) in enumerate(((pre_p, pre_k), (pre_p, g), (pre_k, pre_k), (pre_k, g))):
                nc.vector.tensor_tensor(prod[j][:, :, :], odd(a1), even(a0), ALU.mult).then_inc(prod_done, 1)
            nc.vector.tensor_tensor(part[0][:, :, :], odd(f), even(pre_k), ALU.mult).then_inc(step_done, 1)
            nc.vector.tensor_tensor(part[1][:, :, :], odd(f), even(g), ALU.mult).then_inc(step_done, 1)
            dve.wait_ge(prod_done, 4)
            nc.vector.tensor_tensor(odd(pre_p), odd(pre_p), even(f), ALU.mult)
            dve.wait_ge(copied, 1)
            nc.vector.tensor_tensor(odd(pre_k), odd(pre_k), even(f), ALU.mult)
            dve.wait_ge(step_done, 2)
            nc.vector.tensor_tensor(part[2][:, :, :], even(f), odd(f), ALU.mult).then_inc(step_done, 1)
            dve.wait_ge(step_done, 3)
            nc.vector.tensor_tensor(odd(f), even(f), even(q), ALU.mult).then_inc(step_done, 1)
            dve.wait_ge(step_done, 4)
            nc.vector.tensor_copy(even(f), part[2][:, :, :])
            count = 4
            dve.wait_ge(qdot_done, 2)
            for c, out in ((0, post_k), (1, g)):
                dve.wait_ge(dot_done, c + 3)
                nc.vector.tensor_tensor(prod[c][:, :, :], dot(c), odd(post_k), ALU.mult).then_inc(step_done, 1)
                nc.vector.tensor_tensor(prod[2 + c][:, :, :], dot(2 + c), odd(g), ALU.mult).then_inc(step_done, 1)
                dve.wait_ge(step_done, count + 2)
                nc.vector.tensor_tensor(part[2 + c][:, :, :], prod[c][:, :, :], prod[2 + c][:, :, :],
                                        ALU.add).then_inc(step_done, 1)
                dve.wait_ge(step_done, count + 3)
                nc.vector.tensor_tensor(even(out), part[c][:, :, :], part[2 + c][:, :, :], ALU.add)
                count += 3


def delta_scan(nc, m, pre_p, pre_k, post_k, g, f, q, q_dot, vT, ost):
    W = B * HD
    with ExitStack() as ctx:
        def ring(name, slots, n=2):
            return [ctx.enter_context(nc.sbuf_tensor(f"r_{name}{i}", [P, slots, B, HD], F32)) for i in range(n)]

        state, state_p, state_k = ring("state", 1), ring("statep", 2), ring("statek", 2)
        u_part, w_part, both = ring("upart", 2), ring("wpart", 2), ring("both", 2)
        decayed = ring("decayed", 2, 4)
        q_state, q_term, q_sum, v_spread = ring("qstate", 1), ring("qterm", 2), ring("qsum", 1), ring("vspread", 2)
        (s_state, s_statep, s_statek, s_upart, s_wpart, s_both, s_decayed, s_qstate, s_qterm, s_qsum,
         s_vspread, s_u, s_w, s_out, s_outcopied, s_preset) = (m.sem("r_" + n) for n in (
             "state", "statep", "statek", "upart", "wpart", "both", "decayed", "qstate", "qterm", "qsum",
             "vspread", "u", "w", "out", "outcopied", "preset"))
        sums = [m.psum[:, i * 2 * BLK:(i + 1) * 2 * BLK].rearrange("p (s c) -> p s c", s=2) for i in range(2)]
        o_ps = [m.ps[4], m.ps[5]]
        block = ctx.enter_context(nc.Block())

        def slot(a, j):
            return a[:, j, :, :].rearrange("p b j -> p (b j)")

        def pair(a):
            return a[:, :, :, :].rearrange("p s b j -> p (s b) j")

        def twice(a):
            return a[:, 0, :, :].unsqueeze(1).to_broadcast([P, 2, B, HD])

        def coef(a, r, first=0, n=2):
            return a[:, bass.ds(r * 2 + first, n), :].unsqueeze(3).to_broadcast([P, n, B, HD])

        def sum_pair(i, j):
            return sums[i][:, j, 0:2 * W].rearrange("p (s b j) -> p s b j", s=2, b=B)

        vmask2 = m.vmask[:, :].unsqueeze(1).to_broadcast([P, 2 * B, HD])

        def spread_v(r, i):
            nc.gpsimd.tensor_tensor(pair(v_spread[i]), vmask2,
                                    vT[:, bass.ds(r * 2, 2), :].rearrange("p s b -> p (s b)").unsqueeze(2).to_broadcast(
                                        [P, 2 * B, HD]), ALU.mult).then_inc(s_vspread, 1)

        @block.vector
        def _(dve):
            def ahead(r, i):
                p_coef = coef(pre_p, r)
                dve.wait_ge(s_state, r + 1)
                nc.vector.tensor_tensor(state_p[i][:, :, :, :], twice(state[i]), p_coef, ALU.mult).then_inc(s_statep, 1)
                nc.vector.tensor_tensor(state_k[i][:, :, :, :], twice(state[i]), coef(pre_k, r), ALU.mult).then_inc(s_statek, 1)

            nc.vector.memset(state[0][:, :, :, :], 0.0).then_inc(s_state, 1)
            nc.vector.memset(o_ps[1][:, :], 0.0).then_inc(s_outcopied, 1)
            nc.vector.memset(q_term[1][:, :, :, :], 0.0).then_inc(s_qterm, 1)
            ahead(0, 0)
            with dve.Fori(0, T // UNROLL) as step:
                for v in range(PAIRS):
                    i, r = v % 2, step * PAIRS + v
                    dve.wait_ge(s_decayed, r + 1)
                    dve.wait_ge(s_u, r + 1)
                    nc.vector.tensor_tensor(u_part[i][:, :, :, :], sum_pair(i, 0), coef(post_k, r), ALU.mult).then_inc(s_upart, 1)
                    dve.wait_ge(s_upart, r + 1)
                    nc.vector.tensor_tensor(u_part[i][:, 0, :, :], u_part[i][:, 0, :, :], decayed[v % 4][:, 0, :, :],
                                            ALU.add)
                    dve.wait_ge(s_w, r + 1)
                    nc.vector.tensor_tensor(w_part[i][:, :, :, :], sum_pair(i, 1), coef(g, r), ALU.mult).then_inc(s_wpart, 1)
                    dve.wait_ge(s_wpart, r + 1)
                    nc.vector.tensor_tensor(both[i][:, :, :, :], u_part[i][:, :, :, :], w_part[i][:, :, :, :],
                                            ALU.add).then_inc(s_both, 1)
                    dve.wait_ge(s_both, r + 1)
                    nc.vector.tensor_tensor(state[1 - i][:, 0, :, :], both[i][:, 0, :, :], both[i][:, 1, :, :],
                                            ALU.add).then_inc(s_state, 1)
                    ahead(r + 1, 1 - i)
                    nc.vector.tensor_tensor(q_term[i][:, :, :, :],
                                            sums[i][:, :, 0:W].rearrange("p s (b j) -> p s b j", b=B),
                                            coef(q_dot, r), ALU.mult).then_inc(s_qterm, 1)

        @block.gpsimd
        def _(pool):
            def decay(r, v, i):
                nc.gpsimd.tensor_tensor(decayed[v % 4][:, :, :, :], twice(state[i]), coef(f, r), ALU.mult).then_inc(s_decayed, 1)

            nc.gpsimd.memset(decayed[3][:, :, :, :], 0.0).then_inc(s_preset, 1)
            nc.gpsimd.memset(q_state[1][:, :, :, :], 0.0).then_inc(s_qstate, 1)
            nc.gpsimd.memset(q_sum[1][:, :, :, :], 0.0).then_inc(s_qsum, 1)
            spread_v(0, 0)
            pool.wait_ge(s_state, 1)
            decay(0, 0, 0)
            spread_v(1, 1)
            with pool.Fori(0, T // UNROLL) as step:
                for v in range(PAIRS):
                    i, r = v % 2, step * PAIRS + v
                    pool.wait_ge(s_state, r + 2)
                    decay(r + 1, v + 1, 1 - i)
                    nc.gpsimd.tensor_tensor(q_state[i][:, 0, :, :], state[1 - i][:, 0, :, :],
                                            q[:, bass.ds(r * 2 + 1, 1), :].rearrange("p o b -> p (o b)").unsqueeze(2)
                                            .to_broadcast([P, B, HD]), ALU.mult).then_inc(s_qstate, 1)
                    spread_v(r + 2, i)
                    pool.wait_ge(s_qterm, r + 2)
                    nc.gpsimd.tensor_tensor(q_sum[i][:, 0, :, :], q_term[i][:, 0, :, :], q_term[i][:, 1, :, :],
                                            ALU.add).then_inc(s_qsum, 1)

        @block.tensor
        def _(pe):
            def output(v):
                half, col = v % PAIRS // (OGRP // 2), v % (OGRP // 2) * 2 * NHEAD
                first = o_ps[half][:, col:col + NHEAD]
                nc.tensor.matmul(first, slot(decayed[v % 4], 1), m.headsel[:, :], start=True, stop=False)
                nc.tensor.matmul(first, slot(q_sum[v % 2], 0), m.headsel[:, :], start=False, stop=True)
                nc.tensor.matmul(o_ps[half][:, col + NHEAD:col + 2 * NHEAD], slot(q_state[v % 2], 0), m.headsel[:, :],
                                 start=True, stop=True).then_inc(s_out, 1)

            def values(i):
                nc.tensor.matmul(sums[i][:, 0, 0:2 * W], m.headsum[:, :], pair(v_spread[i]).rearrange("p s j -> p (s j)"),
                                 start=True, stop=False)

            pe.wait_ge(s_vspread, 1)
            values(0)
            pe.wait_ge(s_preset, 1)
            with pe.Fori(0, T // UNROLL) as step:
                for v in range(PAIRS):
                    i, r = v % 2, step * PAIRS + v
                    pe.wait_ge(s_statep, r + 1)
                    nc.tensor.matmul(sums[i][:, 0, 0:2 * W], m.headsum[:, :], pair(state_p[i]).rearrange("p s j -> p (s j)"),
                                     start=False, stop=True).then_inc(s_u, 1)
                    pe.wait_ge(s_statek, r + 1)
                    nc.tensor.matmul(sums[i][:, 1, 0:2 * W], m.headsum[:, :], pair(state_k[i]).rearrange("p s j -> p (s j)"),
                                     start=True, stop=True).then_inc(s_w, 1)
                    pe.wait_ge(s_vspread, r + 2)
                    pe.wait_ge(s_qterm, r + 1)
                    values(1 - i)
                    pe.wait_ge(s_qstate, r + 1)
                    pe.wait_ge(s_qsum, r + 1)
                    if v == 1:
                        pe.wait_ge(s_outcopied, step * 2 + 1)
                    if v == 1 + OGRP // 2:
                        pe.wait_ge(s_outcopied, step * 2 + 2)
                    output(v + PAIRS - 1)
            pe.wait_ge(s_statep, T // 2 + 1)
            nc.tensor.matmul(sums[0][:, 0, 0:2 * W], m.headsum[:, :], pair(state_p[0]).rearrange("p s j -> p (s j)"),
                             start=False, stop=True)
            pe.wait_ge(s_qstate, T // 2 + 1)
            pe.wait_ge(s_qsum, T // 2 + 1)
            output(PAIRS - 1)

        @block.scalar
        def _(act):
            def copy_out(half, t):
                nc.scalar.copy(ost[:, :, bass.ds(t, OGRP)],
                               o_ps[half][:, 0:OGRP * NHEAD].rearrange("p (t h) -> p h t", t=OGRP)).then_inc(s_outcopied, 1)

            with act.Fori(0, T // UNROLL) as step:
                act.wait_ge(s_out, step * PAIRS + 1)
                copy_out(1, step * UNROLL)
                act.wait_ge(s_out, step * PAIRS + (1 + OGRP // 2))
                copy_out(0, step * UNROLL + OGRP)
            act.wait_ge(s_out, T // 2 + 1)
            copy_out(1, T)


def delta_outputs(nc, m, w, z, ost, o_dram):
    with ExitStack() as ctx:
        def sb(name, shape):
            return ctx.enter_context(nc.sbuf_tensor(name, shape, F32))

        def sem(name):
            return m.sem(name)

        oT, sg, g1 = sb("e_oT", [P, NT]), sb("e_sg", [P, NT]), sb("e_g1", [HD, NT])
        ysq, ry = sb("e_ysq", [P, NT]), sb("e_ry", [P, NT])
        stored, loaded, g1_done, g1_copied, g2_done, sig_done, gated, squared, ms_done, dch, wo_done, ry_log, ry_done = map(
            sem, ("e_stored", "e_loaded", "e_g1d", "e_g1c", "e_g2", "e_sig", "e_gated", "e_sq", "e_ms", "e_dch",
                  "e_wo", "e_rylog", "e_ryd"))
        block = ctx.enter_context(nc.Block())

        @block.sync
        def _(sp):
            sp.dma_start(o_dram.rearrange("b j h t -> (b j) h t"), ost[:, :, OGRP:]).then_inc(stored, 16)
            sp.wait_ge(stored, 16)
            for h in range(NHEAD):
                sp.dma_start(oT[h * HD:(h + 1) * HD, :].rearrange("j (b t) -> j b t", b=B),
                             o_dram[:, :, h, :].rearrange("b j t -> j b t")).then_inc(loaded, 16)

        @block.tensor
        def _(pe):
            for n in range(NBLK):
                nc.tensor.matmul(m.ps[n][0:HD, :], w["Wog1"], z[:, cols(n)], start=True, stop=True).then_inc(g1_done, 1)
            for n in range(NBLK):
                pe.wait_ge(g1_copied, n + 1)
                nc.tensor.matmul(m.ps[4 + n][:, :], w["Wog2"], g1[:, cols(n)], start=True, stop=True).then_inc(g2_done, 1)
            for n in range(NBLK):
                pe.wait_ge(squared, n + 1)
                nc.tensor.matmul(m.ps[n][:, :], m.headavg[:, :], ysq[:, cols(n)], start=True, stop=True).then_inc(ms_done, 1)
            for n in range(NBLK):
                pe.wait_ge(dch, 2 * (n + 1))
                nc.tensor.matmul(m.ps[4 + n][:, :], w["Wo"], oT[:, cols(n)], start=True, stop=True).then_inc(wo_done, 1)

        @block.scalar
        def _(act):
            for n in range(NBLK):
                act.wait_ge(g1_done, n + 1)
                nc.scalar.copy(g1[:, cols(n)], m.ps[n][0:HD, :]).then_inc(g1_copied, 1)
            for n in range(NBLK):
                act.wait_ge(g2_done, n + 1)
                nc.scalar.activation(sg[:, cols(n)], m.ps[4 + n][:, :], ACT.Sigmoid).then_inc(sig_done, 1)
            nc.scalar.preload_act_table_set(LOG_EXP)
            for n in range(NBLK):
                act.wait_ge(gated, n + 1)
                nc.scalar.activation(ysq[:, cols(n)], oT[:, cols(n)], ACT.Square).then_inc(squared, 1)
            for n in range(NBLK):
                act.wait_ge(ms_done, n + 1)
                nc.scalar.activation(ry[:, cols(n)], m.ps[n][:, :], ACT.Ln, bias=m.eps[:, 1:2]).then_inc(ry_log, 1)
                act.wait_ge(ry_log, n + 1)
                nc.scalar.activation(ry[:, cols(n)], ry[:, cols(n)], ACT.Exp, scale=-0.5).then_inc(ry_done, 1)

        @block.vector
        def _(dve):
            dve.wait_ge(loaded, 16 * NHEAD)
            for n in range(NBLK):
                dve.wait_ge(sig_done, n + 1)
                nc.vector.tensor_tensor(oT[:, cols(n)], oT[:, cols(n)], sg[:, cols(n)], ALU.mult).then_inc(gated, 1)
            for n in range(NBLK):
                dve.wait_ge(gated, n + 1)
                dve.wait_ge(squared, n + 1)
                dve.wait_ge(ry_done, n + 1)
                nc.vector.tensor_tensor(oT[:, cols(n)], oT[:, cols(n)], ry[:, cols(n)], ALU.mult).then_inc(dch, 1)
                dve.wait_ge(dch, 2 * n + 1)
                nc.vector.tensor_scalar(oT[:, cols(n)], oT[:, cols(n)], w["norm_w"], None, ALU.mult).then_inc(dch, 1)
            for n in range(NBLK):
                dve.wait_ge(wo_done, n + 1)
                nc.vector.tensor_tensor(m.x[:, cols(n)], m.x[:, cols(n)], m.ps[4 + n][:, :], ALU.add)


def recurrence_layer(nc, m, dram):
    names = ("Wq", "Wk", "Wv", "Wf1", "Wf2", "Wbeta", "Wog1", "Wog2", "Wo", "norm_w")
    with ExitStack() as ctx:
        w, loads = {}, []
        for name in names:
            a = dram["L1_attn_" + name]
            buf = ctx.enter_context(nc.sbuf_tensor("w_" + name, list(a.shape), F32))
            w[name] = buf[:, :]
            loads.append((buf[:, :], a))
        z = ctx.enter_context(nc.sbuf_tensor("d_z", [P, NT], F32))
        pT, kT, gT, fT, qT, vT = (ctx.enter_context(nc.sbuf_tensor("d_" + n, [P, T + 4, B], F32))
                                  for n in ("pT", "kT", "gT", "fT", "qT", "vT"))
        load_all(nc, m, "recurrence_layer", loads)
        with nc.Block() as block:
            @block.gpsimd
            def _(pool):
                for a in (pT, kT, fT, vT):
                    nc.gpsimd.memset(a[:, T:, :], 0.0)
        layernorm(nc, m, "ln5", m.x, z)
        delta_inputs(nc, m, w, z, pT, kT, gT, fT, qT, vT)
        ost = ctx.enter_context(nc.sbuf_tensor("d_ost", [P, NHEAD, OGRP + T], F32))
        post_k, q_dot = (ctx.enter_context(nc.sbuf_tensor("d_" + n, [P, T, B], F32)) for n in ("post_k", "q_dot"))
        delta_pairs(nc, m, pT, kT, post_k, gT, fT, qT, q_dot)
        delta_scan(nc, m, pT, kT, post_k, gT, fT, qT, q_dot, vT, ost)
        delta_outputs(nc, m, w, z, ost, dram["o_scratch"])


NEXP = 8
TILES = NT // P


def route(nc, m, name, z, router, gates):
    with ExitStack() as ctx:
        def sb(s, shape):
            return ctx.enter_context(nc.sbuf_tensor(f"{name}_{s}", shape, F32))

        prob, order, best = sb("prob", [P, TILES, NEXP]), sb("order", [P, TILES, NEXP]), sb("best", [P, TILES, NEXP])
        pick1, pick2, rest = sb("pick1", [P, TILES, NEXP]), sb("pick2", [P, TILES, NEXP]), sb("rest", [P, TILES, NEXP])
        top, total, first = sb("top", [P, TILES]), sb("total", [P, TILES]), sb("first", [P, TILES])
        logits_done, shifted, exped, chain = (m.sem(f"{name}_{s}")
                                              for s in ("logits", "shifted", "exped", "chain"))
        block = ctx.enter_context(nc.Block())

        def wide(a):
            return a[:, :].unsqueeze(2).to_broadcast([P, TILES, NEXP])

        @block.tensor
        def _(pe):
            for t in range(TILES):
                mm = nc.tensor.matmul(m.ps[0][:, t * NEXP:(t + 1) * NEXP], z[:, cols(t, P)], router, start=True, stop=True)
            mm.then_inc(logits_done, 1)

        @block.scalar
        def _(act):
            act.wait_ge(shifted, 1)
            nc.scalar.activation(prob[:, :, :], prob[:, :, :], ACT.Exp).then_inc(exped, 1)

        @block.vector
        def _(dve):
            steps = [0]

            def then(ins):
                steps[0] += 1
                ins.then_inc(chain, 1)
                dve.wait_ge(chain, steps[0])

            logits = m.ps[0][:, 0:TILES * NEXP].rearrange("p (t e) -> p t e", t=TILES)
            weight = m.order[:, :].unsqueeze(1).to_broadcast([P, TILES, NEXP])
            dve.wait_ge(logits_done, 1)
            then(nc.vector.tensor_reduce(top[:, :], logits, AX.X, ALU.max))
            nc.vector.tensor_tensor(prob[:, :, :], logits, wide(top), ALU.subtract).then_inc(shifted, 1)
            dve.wait_ge(exped, 1)
            then(nc.vector.tensor_reduce(total[:, :], prob[:, :, :], AX.X, ALU.add))
            then(nc.vector.reciprocal(total[:, :], total[:, :]))
            then(nc.vector.tensor_tensor(prob[:, :, :], prob[:, :, :], wide(total), ALU.mult))

            def pick(source, out):
                then(nc.vector.tensor_reduce(top[:, :], source[:, :, :], AX.X, ALU.max))
                then(nc.vector.tensor_tensor(best[:, :, :], source[:, :, :], wide(top), ALU.is_equal))
                then(nc.vector.tensor_tensor(order[:, :, :], best[:, :, :], weight, ALU.mult))
                then(nc.vector.tensor_reduce(first[:, :], order[:, :, :], AX.X, ALU.max))
                then(nc.vector.tensor_tensor(out[:, :, :], order[:, :, :], wide(first), ALU.is_equal))

            pick(prob, pick1)
            then(nc.vector.scalar_tensor_tensor(rest[:, :, :], pick1[:, :, :], -2.0, prob[:, :, :], ALU.mult, ALU.add))
            pick(rest, pick2)
            then(nc.vector.tensor_tensor(pick1[:, :, :], pick1[:, :, :], pick2[:, :, :], ALU.add))
            then(nc.vector.tensor_tensor(gates[:, :, :], pick1[:, :, :], prob[:, :, :], ALU.mult))


def experts(nc, m, name, z, gates, up_dram, gate_dram, down_dram, width, gelu, shared=None):
    C = width // P
    S = 2 * NBLK * C
    with ExitStack() as ctx:
        def sb(s, shape, n=2):
            return [ctx.enter_context(nc.sbuf_tensor(f"{name}_{s}{i}", shape, F32)) for i in range(n)]

        tallies = []

        def tally(s, units, per=1, credit=0):
            tallies.append(Tally(m, f"{name}_{s}", units, per, credit))
            return tallies[-1]

        up, down = sb("up", [P, width]), sb("down", [P, C, P])
        first = sb("first", [P, width]) if not gelu else up
        gcol = sb("gcol", [P, TILES])
        silu, hidden, gate, gated = sb("silu", [P, BLK]), sb("hidden", [P, BLK]), sb("gate", [P, BLK]), sb("gated", [P, BLK])
        loads = 2 if gelu else 3
        t_w = [tally(f"w{i}", 1, 16 * loads) for i in range(2)]
        t_col = tally("col", 2)
        t_first, t_second, t_silu, t_hidden, t_down = (tally("first_ps", S), tally("second_ps", S), tally("silu_done", S, 1, 2),
                                                       tally("hidden_done", S, 1, 2), tally("down_done", S, 1, 2))
        t_gps, t_gate, t_gated, t_acc = (tally("gate_ps", 2 * NBLK, 1, 1), tally("gate_done", 2 * NBLK, 1, 2),
                                         tally("gated_done", 2 * NBLK, 1, 2), tally("acc", 2 * NBLK, 1, 2))
        b_first, b_second, b_y, b_gate = m.ps[0:2], m.ps[2:4], m.ps[4:6], m.ps[6:8]
        NPASS = NEXP // 2
        if shared:
            s_first, s_up, s_down = (sb(f"s_{j}", shape, 1)[0] for j, shape in
                                     (("first", [P, width // 2]), ("up", [P, width // 2]), ("down", [P, C // 2, P])))
            s_loaded = m.sem(name + "_sloaded")
        with nc.Block() as block:
            @block.gpsimd
            def _(pool):
                give_credit(pool, tallies)

        block = ctx.enter_context(nc.Block())

        def wait(eng, t, step, unit, j=None):
            eng.wait_ge(t.sem, t.done(step, unit, j))

        def load(sp, i, e):
            pick = (lambda a: a[e]) if isinstance(e, int) else (lambda a: a[bass.ds(e, 1)].rearrange("o a b -> (o a) b"))
            sp.dma_start(up[i][:, :], pick(up_dram)).then_inc(t_w[i].sem, 16)
            sp.dma_start(down[i][:, :, :], pick(down_dram).rearrange("(c p) h -> p c h", p=P)).then_inc(t_w[i].sem, 16)
            if not gelu:
                sp.dma_start(first[i][:, :], pick(gate_dram)).then_inc(t_w[i].sem, 16)

        @block.sync
        def _(sp):
            if shared:
                for dst, src in ((s_first[:, :], shared[0]), (s_up[:, :], shared[1]),
                                 (s_down[:, :, :], shared[2].rearrange("(c p) h -> p c h", p=P))):
                    sp.dma_start(dst, src).then_inc(s_loaded, 16)
            for i in range(2):
                load(sp, i, i)
            with sp.Fori(0, NPASS - 1) as step:
                for i in range(2):
                    wait(sp, t_down, step, (i + 1) * NBLK * C - 1)
                    load(sp, i, step * 2 + (i + 2))

        def steps(experts_of_pass, chunks):
            return [(i, n, c) for i in experts_of_pass for n in range(NBLK) for c in range(chunks)]

        def pe_pass(pe, step, chunks, weights, gated_by):
            seq = steps(range(len(weights)), chunks)

            def down_product(k):
                i, n, c = seq[k]
                wait(pe, t_hidden, step, k)
                if c == 0:
                    wait(pe, t_gated, step, i * NBLK + n - 2)
                nc.tensor.matmul(b_y[n % 2][:, :], weights[i][2][:, c, :], hidden[k % 2][:, :],
                                 start=(c == 0), stop=(c == chunks - 1)).then_inc(t_down.sem, 1)

            for k, (i, n, c) in enumerate(seq):
                w_first, w_up, _ = weights[i]
                if c == 0 and gated_by:
                    if n == 0:
                        wait(pe, t_col, step, i)
                        wait(pe, t_w[i], step, 0)
                    wait(pe, t_gate, step, i * NBLK + n - 2)
                    for t in range(BLK // P):
                        tile = n * (BLK // P) + t
                        mm = nc.tensor.matmul(b_gate[n % 2][:, cols(t, P)],
                                              gcol[i][:, tile:tile + 1].to_broadcast([P, P]), m.ident[:, :],
                                              start=True, stop=True)
                    mm.then_inc(t_gps.sem, 1)
                wait(pe, t_silu if not gelu else t_hidden, step, k - 2)
                nc.tensor.matmul(b_first[k % 2][:, :], w_first[:, cols(c, P)], z[:, cols(n)],
                                 start=True, stop=True).then_inc(t_first.sem, 1)
                if not gelu:
                    wait(pe, t_hidden, step, k - 2)
                    nc.tensor.matmul(b_second[k % 2][:, :], w_up[:, cols(c, P)], z[:, cols(n)],
                                     start=True, stop=True).then_inc(t_second.sem, 1)
                if k:
                    down_product(k - 1)
            down_product(len(seq) - 1)

        def act_pass(act, step, chunks, n_experts, gated_by):
            for k, (i, n, c) in enumerate(steps(range(n_experts), chunks)):
                if c == 0 and gated_by:
                    unit = i * NBLK + n
                    wait(act, t_gps, step, unit)
                    wait(act, t_gated, step, unit - 2)
                    nc.scalar.copy(gate[n % 2][:, :], b_gate[n % 2][:, :]).then_inc(t_gate.sem, 1)
                wait(act, t_first, step, k)
                if gelu:
                    wait(act, t_down, step, k - 2)
                    nc.scalar.activation(hidden[k % 2][:, :], b_first[k % 2][:, :], ACT.Gelu).then_inc(t_hidden.sem, 1)
                else:
                    wait(act, t_hidden, step, k - 2)
                    nc.scalar.activation(silu[k % 2][:, :], b_first[k % 2][:, :], ACT.Silu).then_inc(t_silu.sem, 1)

        def dve_pass(dve, step, chunks, n_experts, gated_by):
            seq = steps(range(n_experts), chunks)

            def gated_block(i, n):
                unit = i * NBLK + n
                wait(dve, t_down, step, unit * chunks + chunks - 1)
                wait(dve, t_acc, step, unit - 2)
                if gated_by:
                    wait(dve, t_gate, step, unit)
                    nc.vector.tensor_tensor(gated[n % 2][:, :], b_y[n % 2][:, :], gate[n % 2][:, :],
                                            ALU.mult).then_inc(t_gated.sem, 1)
                else:
                    nc.vector.tensor_scalar(gated[n % 2][:, :], b_y[n % 2][:, :], SHARED_SCALE, None,
                                            ALU.mult).then_inc(t_gated.sem, 1)

            for k, (i, n, c) in enumerate(seq):
                if not gelu:
                    wait(dve, t_second, step, k)
                    wait(dve, t_silu, step, k)
                    wait(dve, t_down, step, k - 2)
                    nc.vector.tensor_tensor(hidden[k % 2][:, :], b_second[k % 2][:, :], silu[k % 2][:, :],
                                            ALU.mult).then_inc(t_hidden.sem, 1)
                if k >= chunks + 1 and (k - 1) % chunks == 0:
                    gated_block(*seq[k - chunks - 1][:2])
            gated_block(*seq[-1][:2])

        def pool_pass(pool, step, n_experts, columns):
            if columns:
                wait(pool, t_gps, step, -1)
                for i in range(n_experts):
                    nc.gpsimd.tensor_copy(gcol[i][:, :], gates[:, :, bass.ds(step * 2 + i, 1)].rearrange("p t o -> p (t o)")
                                          ).then_inc(t_col.sem, 1)
            for i in range(n_experts):
                for n in range(NBLK):
                    unit = i * NBLK + n
                    wait(pool, t_gated, step, unit)
                    wait(pool, t_acc, step, unit - 1)
                    nc.gpsimd.tensor_tensor(m.x[:, cols(n)], m.x[:, cols(n)], gated[n % 2][:, :],
                                            ALU.add).then_inc(t_acc.sem, 1)

        pair = [(first[i], up[i], down[i]) for i in range(2)]

        @block.tensor
        def _(pe):
            with pe.Fori(0, NPASS) as step:
                pe_pass(pe, step, C, pair, True)
            if shared:
                pe.wait_ge(s_loaded, 48)
                pe_pass(pe, NPASS, C // 2, [(s_first, s_up, s_down)], False)

        @block.scalar
        def _(act):
            with act.Fori(0, NPASS) as step:
                act_pass(act, step, C, 2, True)
            if shared:
                act_pass(act, NPASS, C // 2, 1, False)

        @block.vector
        def _(dve):
            with dve.Fori(0, NPASS) as step:
                dve_pass(dve, step, C, 2, True)
            if shared:
                dve_pass(dve, NPASS, C // 2, 1, False)

        @block.gpsimd
        def _(pool):
            with pool.Fori(0, NPASS) as step:
                pool_pass(pool, step, 2, True)
            if shared:
                pool_pass(pool, NPASS, 1, False)


SHARED_SCALE = 0.5


def mixture_layer(nc, m, dram):
    d = {k: dram["L1_ffn_" + k] for k in ("Wr", "Wg", "Wu", "Wd", "Sg", "Su", "Sd")}
    with ExitStack() as ctx:
        z = ctx.enter_context(nc.sbuf_tensor("f_z", [P, NT], F32))
        router = ctx.enter_context(nc.sbuf_tensor("f_router", [P, NEXP], F32))
        gates = ctx.enter_context(nc.sbuf_tensor("f_gates", [P, TILES, NEXP], F32))
        load_all(nc, m, "mixture_layer", [(router[:, :], d["Wr"])])
        layernorm(nc, m, "ln6", m.x, z)
        route(nc, m, "f_route", z, router[:, :], gates)
        experts(nc, m, "f", z, gates, d["Wu"], d["Wg"], d["Wd"], d["Wg"].shape[2], False, (d["Sg"], d["Su"], d["Sd"]))


AHD = 8


def sequence_attention(nc, m, w, z):
    with ExitStack() as ctx:
        def sb(s, shape):
            return ctx.enter_context(nc.sbuf_tensor("g_" + s, shape, F32))

        def sem(s):
            return m.sem("g_" + s)

        hn = sb("hn", [P, NT])
        q, k, v, attended = sb("q", [P, B, T]), sb("k", [P, B, T]), sb("v", [P, B, T]), sb("attended", [P, B, T])
        prod = [sb(f"prod{i}", [P, B, T]) for i in range(2)]
        prob = [sb(f"prob{i}", [P, B, T]) for i in range(2)]
        top, total = sb("top", [P, T]), sb("total", [P, T])
        layernorm(nc, m, "ln2", z, hn, w["ln1_w"], w["ln1_b"])
        qkv_done, qkv_copied, prods, scored, shifted, exped, weighted, chain, added, attn_done, proj_done = map(
            sem, ("qkv", "qkvc", "prods", "scored", "shifted", "exped", "weighted", "chain", "added", "attn", "proj"))
        block = ctx.enter_context(nc.Block())

        def flat(a):
            return a[:, :, :].rearrange("p b t -> p (b t)")

        def banks(s, n):
            half = 4 * (s % 2)
            return m.psum[:, half * BLK:half * BLK + n * T].rearrange("p (b t) -> p b t", b=n)

        @block.tensor
        def _(pe):
            for j in range(3):
                for n in range(NBLK):
                    u = j * NBLK + n
                    if u >= 8:
                        pe.wait_ge(qkv_copied, u - 7)
                    nc.tensor.matmul(m.ps[u % 8][:, :], w["in_proj_w"][:, cols(j, P)], hn[:, cols(n)],
                                     start=True, stop=True).then_inc(qkv_done, 1)
            for s in range(B):
                pe.wait_ge(prods, s + 1)
                if s < 2:
                    pe.wait_ge(qkv_copied, 3 * NBLK)
                else:
                    pe.wait_ge(shifted, s - 1)
                for c in range(0, s + 1, BB):
                    n = min(BB, s + 1 - c) * T
                    mm = nc.tensor.matmul(m.psum[:, (4 * (s % 2)) * BLK + c * T:(4 * (s % 2)) * BLK + c * T + n],
                                          m.headscale[:, :], flat(prod[s % 2])[:, c * T:c * T + n], start=True, stop=True)
                mm.then_inc(scored, 1)
            for n in range(NBLK):
                pe.wait_ge(attn_done, (n + 1) * BB)
                if n == 0:
                    pe.wait_ge(shifted, B)
                nc.tensor.matmul(m.ps[n][:, :], w["out_proj_w"], flat(attended)[:, cols(n)],
                                 start=True, stop=True).then_inc(proj_done, 1)

        @block.scalar
        def _(act):
            for j, out in enumerate((q, k, v)):
                for n in range(NBLK):
                    u = j * NBLK + n
                    act.wait_ge(qkv_done, u + 1)
                    nc.scalar.activation(flat(out)[:, cols(n)], m.ps[u % 8][:, :], ACT.Identity,
                                         bias=w["in_proj_b"][:, j:j + 1]).then_inc(qkv_copied, 1)
            for s in range(B):
                act.wait_ge(shifted, s + 1)
                nc.scalar.activation(prob[s % 2][:, 0:s + 1, :], prob[s % 2][:, 0:s + 1, :], ACT.Exp).then_inc(exped, 1)

        @block.gpsimd
        def _(pool):
            for s in range(B):
                pool.wait_ge(exped, s + 1)
                pool.wait_ge(scored, s + 1)
                nc.gpsimd.tensor_tensor(prod[s % 2][:, 0:s + 1, :], prob[s % 2][:, 0:s + 1, :], v[:, 0:s + 1, :],
                                        ALU.mult).then_inc(weighted, 1)

        @block.vector
        def _(dve):
            steps = [0]

            def then(ins):
                steps[0] += 1
                ins.then_inc(chain, 1)
                dve.wait_ge(chain, steps[0])

            def products(s):
                if s >= 2:
                    dve.wait_ge(weighted, s - 1)
                    dve.wait_ge(attn_done, s - 1)
                nc.vector.tensor_tensor(prod[s % 2][:, 0:s + 1, :], k[:, 0:s + 1, :],
                                        q[:, s:s + 1, :].to_broadcast([P, s + 1, T]), ALU.mult).then_inc(prods, 1)

            dve.wait_ge(qkv_copied, 3 * NBLK)
            products(0)
            for s in range(B):
                n = s + 1
                dve.wait_ge(scored, n)
                then(nc.vector.tensor_reduce(top[:, :], banks(s, n).rearrange("p b t -> p t b"), AX.X, ALU.max))
                nc.vector.tensor_tensor(prob[s % 2][:, 0:n, :], banks(s, n),
                                        top[:, :].unsqueeze(1).to_broadcast([P, n, T]), ALU.subtract).then_inc(shifted, 1)
                if s + 1 < B:
                    products(s + 1)
                dve.wait_ge(exped, n)
                then(nc.vector.tensor_reduce(total[:, :], prob[s % 2][:, 0:n, :].rearrange("p b t -> p t b"), AX.X, ALU.add))
                then(nc.vector.reciprocal(total[:, :], total[:, :]))
                dve.wait_ge(weighted, n)
                then(nc.vector.tensor_reduce(attended[:, s, :], prod[s % 2][:, 0:n, :].rearrange("p b t -> p t b"),
                                             AX.X, ALU.add))
                nc.vector.tensor_tensor(attended[:, s, :], attended[:, s, :], total[:, :], ALU.mult).then_inc(attn_done, 1)
            for n in range(NBLK):
                dve.wait_ge(proj_done, n + 1)
                nc.vector.scalar_tensor_tensor(z[:, cols(n)], m.ps[n][:, :], w["out_proj_b"], z[:, cols(n)],
                                               ALU.add, ALU.add).then_inc(added, 1)
            dve.wait_ge(added, NBLK)


def sequence_layer(nc, m, dram):
    names = ("ln1_w", "ln1_b", "in_proj_w", "in_proj_b", "out_proj_w", "out_proj_b", "ln2_w", "ln2_b", "router_w")
    with ExitStack() as ctx:
        w, loads = {}, []
        for name in names:
            a = dram["L0_ffn_" + name]
            w[name] = ctx.enter_context(nc.sbuf_tensor("w_" + name, list(a.shape), F32))[:, :]
            loads.append((w[name], a))
        z = ctx.enter_context(nc.sbuf_tensor("g_z", [P, NT], F32))
        gates = ctx.enter_context(nc.sbuf_tensor("g_gates", [P, TILES, NEXP], F32))
        load_all(nc, m, "sequence_layer", loads)
        layernorm(nc, m, "ln1", m.x, z)
        sequence_attention(nc, m, w, z)
        with nc.Block() as block:
            @block.gpsimd
            def _(pool):
                nc.gpsimd.tensor_tensor(m.x[:, :], m.x[:, :], z[:, :], ALU.add)
        with nc.sbuf_tensor("g_hn2", [P, NT], F32) as hn2:
            layernorm(nc, m, "ln3", z, hn2, w["ln2_w"], w["ln2_b"])
            route(nc, m, "g_route", hn2, w["router_w"], gates)
            experts(nc, m, "h", hn2, gates, dram["L0_ffn_w1"], None, dram["L0_ffn_w2"], dram["L0_ffn_w1"].shape[2], True)


LAYERS = (distance_layer, sequence_layer, recurrence_layer, mixture_layer)

CONSTS = ("avg", "headsum", "headavg", "headsel", "vmask", "ident", "band", "hmask", "omask", "qsel", "headscale", "order")


def program(nc, dram, stages):
    with ExitStack() as ctx:
        m = Mem(nc)
        m.x = ctx.enter_context(nc.sbuf_tensor("x", [P, NT], F32))
        m.scratch = ctx.enter_context(nc.sbuf_tensor("scratch", [P, 2], F32))
        m.psum = ctx.enter_context(nc.psum_tensor("banks", [P, 8 * BLK], F32))
        m.ps = [m.psum[:, cols(i)] for i in range(8)]
        loads, bufs = [(m.x, dram["x"])], []
        for name in CONSTS:
            a = dram[name]
            bufs.append(ctx.enter_context(nc.sbuf_tensor("c_" + name, list(a.shape), a.dtype)))
            loads.append((bufs[-1], a))
        (m.avg, m.headsum, m.headavg, m.headsel, m.vmask, m.ident, m.band32, m.hmask, m.omask, m.qsel, m.headscale,
         m.order) = bufs
        m.identb = ctx.enter_context(nc.sbuf_tensor("identb", [P, P], BF16))
        m.band = ctx.enter_context(nc.sbuf_tensor("band", [P, KT], BF16))
        m.eps = ctx.enter_context(nc.sbuf_tensor("eps", [P, 5], F32))
        loaded = m.sem("loaded")
        with nc.Block() as block:
            @block.gpsimd
            def _(pool):
                for i, eps in enumerate((1e-5, 1e-6, 1e-8, 0.5 * math.log(NORM_SCALE), 1.0)):
                    nc.gpsimd.memset(m.eps[:, i:i + 1], eps)

            @block.sync
            def _(sp):
                for buf, a in loads:
                    sp.dma_start(buf[:, :], a).then_inc(loaded, 16)
                sp.wait_ge(loaded, 16 * len(loads))
        with nc.Block() as block:
            @block.vector
            def _(dve):
                nc.vector.tensor_copy(m.identb[:, :], m.ident[:, :])
                nc.vector.tensor_copy(m.band[:, :], m.band32[:, :])
        for stage in stages:
            stage(nc, m, dram)
            m.release()
        stored = m.sem("stored")
        with nc.Block() as block:
            @block.sync
            def _(sp):
                sp.dma_start(dram["out"], m.x[:, :]).then_inc(stored, 16)
                sp.wait_ge(stored, 16)




def constants():
    part = np.arange(P)
    head = part // HD
    same = head[:, None] == head[None, :]
    key, query = np.arange(KT), part % QT
    inside = (key[None, :] > query[:, None]) & (key[None, :] <= query[:, None] + WIN)
    f = np.float32
    return {
        "avg": np.full((P, P), 1.0 / P, f),
        "headsum": same.astype(f),
        "headavg": same.astype(f) / f(HD),
        "headsel": (head[:, None] == np.arange(NHEAD)[None, :]).astype(f),
        "vmask": (part[:, None] % HD == np.arange(HD)[None, :]).astype(f),
        "ident": np.eye(P, dtype=f),
        "band": np.where(inside, 0.0, OUTSIDE).astype(f),
        "hmask": (head[:, None] % HG == np.arange(HG)[None, :]).astype(f),
        "omask": (part[:, None] // QT == np.arange(HALF)[None, :] // HD).astype(f),
        "headscale": ((part[:, None] // AHD == part[None, :] // AHD) / np.sqrt(AHD)).astype(f),
        "order": np.tile(np.arange(NEXP, 0, -1), (P, 1)).astype(f),
        "qsel": (query[:, None] == np.arange(QT)[None, :]).astype(f),
    }


def host_layout(inputs):
    a = {k: np.asarray(v) for k, v in inputs.items()}
    out = {"x": a["L0_attn_x"].reshape(NT, P).T}
    for name in ("encoder_query", "encoder_value"):
        out["L0_attn_" + name] = a["L0_attn_" + name].transpose(1, 0, 2).reshape(P, P)
    for name in ("mn_w1", "mn_w2", "decoder"):
        out["L0_attn_" + name] = a["L0_attn_" + name]
    for name in ("mn_b1", "mn_b2", "base_metric"):
        out["L0_attn_" + name] = a["L0_attn_" + name].reshape(-1, 1)
    u, v = a["L0_attn_hebbian_U"], a["L0_attn_hebbian_V"]
    rank = u.shape[2]
    for name in ("hebbian_U", "hebbian_V"):
        out["L0_attn_" + name] = np.zeros((NHEAD * rank, P), u.dtype)
    for h in range(NHEAD):
        rows, channels = slice(h * rank, (h + 1) * rank), slice(h * HD, (h + 1) * HD)
        out["L0_attn_hebbian_U"][rows, channels] = u[h].T
        out["L0_attn_hebbian_V"][rows, channels] = v[h]
    for name in ("ln1_w", "ln1_b", "out_proj_b", "ln2_w", "ln2_b"):
        out["L0_ffn_" + name] = a["L0_ffn_" + name].reshape(P, 1)
    out["L0_ffn_in_proj_b"] = a["L0_ffn_in_proj_b"].reshape(3, P).T
    for name in ("in_proj_w", "out_proj_w", "router_w"):
        out["L0_ffn_" + name] = a["L0_ffn_" + name].T
    for name in ("w1", "w2"):
        out["L0_ffn_" + name] = a["L0_ffn_" + name]
    for name in ("Wq", "Wk", "Wv", "Wf1", "Wf2", "Wog1", "Wog2", "Wo"):
        out["L1_attn_" + name] = a["L1_attn_" + name]
    out["L1_attn_Wbeta"] = np.repeat(a["L1_attn_Wbeta"], HD, axis=1)
    out["L1_attn_norm_w"] = a["L1_attn_norm_w"].reshape(P, 1)
    for name in ("Wr", "Wg", "Wu", "Wd", "Sg", "Su", "Sd"):
        out["L1_ffn_" + name] = a["L1_ffn_" + name]
    return {k: np.ascontiguousarray(v) for k, v in out.items()}


def kernel(**inputs):
    from concourse import bacc
    from concourse.bass_utils import run_bass_kernel_spmd

    nc = bacc.Bacc("TRN2", target_bir_lowering=False, num_devices=1)
    arrays = {**host_layout(inputs), **constants()}
    dram = {name: nc.dram_tensor("in_" + name, a.shape, mybir.dt.from_np(a.dtype), kind="ExternalInput").ap()
            for name, a in arrays.items()}
    dram["out"] = nc.dram_tensor("out", [P, NT], F32, kind="ExternalOutput").ap()
    dram["o_scratch"] = nc.dram_tensor("o_scratch", [B, HD, NHEAD, T], F32, kind="Internal").ap()
    program(nc, dram, LAYERS)
    r = run_bass_kernel_spmd(nc, [{"in_" + name: a for name, a in arrays.items()}], core_ids=[0])
    return np.ascontiguousarray(r.results[0]["out"].T).reshape(B, T, P)
```

```python
import math
from contextlib import ExitStack

import concourse.bass as bass
import numpy as np
from concourse import mybir

F32 = mybir.dt.float32
BF16 = mybir.dt.bfloat16
ALU = mybir.AluOpType
ACT = mybir.ActivationFunctionType
AX = mybir.AxisListType

P = 128
B, T = 8, 256
NT = B * T
BLK = 512
NBLK = NT // BLK
BB = BLK // T
HD = 16
NHEAD = P // HD
LN_EPS = 1e-5


LOG_EXP = "natural_log_exp_and_others"


class Mem:

    def __init__(self, nc):
        self.nc, self.semaphores = nc, []

    def sem(self, name):
        self.semaphores.append(self.nc.alloc_semaphore(name))
        return self.semaphores[-1]

    def release(self):
        self.nc.clear_and_free_semaphores(self.semaphores)
        self.nc.all_engine_barrier()
        self.semaphores = []


def cols(n, width=BLK):
    return slice(n * width, (n + 1) * width)


def load_all(block, loads, loaded):
    @block.sync
    def _(sp):
        for dst, src in loads:
            sp.dma_start(dst, src).then_inc(loaded, 16)
        sp.wait_ge(loaded, 16 * len(loads))


def layernorm(nc, m, name, src, dst, weight=None, bias=None, pool_work=None):
    with ExitStack() as ctx:
        sq = ctx.enter_context(nc.sbuf_tensor(f"{name}_squares", [P, NT], F32))
        rstd = ctx.enter_context(nc.sbuf_tensor(f"{name}_rstd", [P, NT], F32))
        centred, squared, var_done, logged, rstd_done, normed, scaled = (
            m.sem(f"{name}_{s}")
            for s in ("centred", "squared", "var", "log", "rstd", "normed", "scaled"))
        block = ctx.enter_context(nc.Block())

        if pool_work is not None:
            @block.gpsimd
            def _(pool):
                pool_work(pool)

        @block.tensor
        def _(pe):
            for n in range(NBLK):
                nc.tensor.matmul(m.ps[n][:, :], m.centre[:, :], src[:, cols(n)],
                                 start=True, stop=True).then_inc(centred, 1)
            for n in range(NBLK):
                pe.wait_ge(squared, n + 1)
                nc.tensor.matmul(m.ps[NBLK + n][:, :], m.avg[:, :], sq[:, cols(n)],
                                 start=True, stop=True).then_inc(var_done, 1)

        @block.scalar
        def _(act):
            nc.scalar.preload_act_table_set(LOG_EXP)
            for n in range(NBLK):
                act.wait_ge(centred, n + 1)
                nc.scalar.activation(sq[:, cols(n)], m.ps[n][:, :], ACT.Square).then_inc(squared, 1)
            for n in range(NBLK):
                act.wait_ge(var_done, n + 1)
                nc.scalar.activation(rstd[:, cols(n)], m.ps[NBLK + n][:, :], ACT.Ln,
                                     bias=m.eps[:, 0:1]).then_inc(logged, 1)
                act.wait_ge(logged, n + 1)
                nc.scalar.activation(rstd[:, cols(n)], rstd[:, cols(n)], ACT.Exp, scale=-0.5).then_inc(rstd_done, 1)

        @block.vector
        def _(dve):
            for n in range(NBLK):
                dve.wait_ge(rstd_done, n + 1)
                nc.vector.tensor_tensor(dst[:, cols(n)], m.ps[n][:, :], rstd[:, cols(n)],
                                        ALU.mult).then_inc(normed, 1)
                if weight is not None:
                    dve.wait_ge(normed, n + 1)
                    nc.vector.tensor_scalar(dst[:, cols(n)], dst[:, cols(n)], weight, bias,
                                            ALU.mult, ALU.add).then_inc(scaled, 1)


PAD = 64
WIN = 64
TOPK = 32
QT = 32
KT = QT + WIN
HG = 4
NQT = T // QT
GT = 4
NG = NQT * (NHEAD // HG) // GT
HALF = HG * HD
SEQ_PASS = 4
ROUNDS = TOPK // 8
TAKEN = -3.0e38
OUTSIDE = -1.0e15
GATE2 = float(0.2) ** 2
NORM_SCALE = 2.0 ** 30


class Tally:

    def __init__(self, m, name, units, per=1, credit=0):
        self.sem = m.sem(name)
        self.units, self.per, self.credit = units, per, credit * per

    def done(self, step, unit, j=None):
        j = self.per - 1 if j is None else j
        return step * (self.units * self.per) + (unit * self.per + self.credit + j + 1)


def give_credit(pool, tallies):
    for t in tallies:
        if t.credit:
            pool.sem_inc(t.sem, t.credit)


def distance_queries(nc, m, w, z, qpad, metric):
    with ExitStack() as ctx:
        def sb(name, shape):
            return ctx.enter_context(nc.sbuf_tensor(name, shape, F32))

        def sem(name):
            return m.sem(name)

        total, every8, sig = sb("a_total", [P, B]), sb("a_every8", [P, B]), sb("a_sig", [P, B])
        hidden, arg, size, tail = sb("a_hidden", [P // 2, B]), sb("a_arg", [P, B]), sb("a_size", [P, B]), sb("a_tail", [P, B])
        base01 = sb("a_base01", [P, 1])
        q_done, relu_done, sums, sig_done, hid_done, gelu_done, mod_done, arg_done, size_done, act_done, based = map(
            sem, ("a_q", "a_relu", "a_sums", "a_sigd", "a_hid", "a_gelu", "a_mod", "a_argd", "a_sized", "a_act", "a_based"))
        hm_done, hm_copied = sem("a_hm"), sem("a_hmc")
        block = ctx.enter_context(nc.Block())

        @block.tensor
        def _(pe):
            for n in range(NBLK):
                nc.tensor.matmul(m.ps[n][:, :], w["encoder_query"], z[:, cols(n)], start=True, stop=True).then_inc(q_done, 1)
            nc.tensor.matmul(m.ps[5][:, 0:P], w["hebbian_U"], w["hebbian_V"], start=True, stop=True).then_inc(hm_done, 1)
            pe.wait_ge(sig_done, 1)
            nc.tensor.matmul(m.ps[4][0:P // 2, 0:B], w["mn_w1"], sig[:, :], start=True, stop=True).then_inc(hid_done, 1)
            pe.wait_ge(gelu_done, 1)
            nc.tensor.matmul(m.ps[6][:, 0:B], w["mn_w2"], hidden[:, :], start=True, stop=True).then_inc(mod_done, 1)

        @block.scalar
        def _(act):
            for n in range(NBLK):
                act.wait_ge(q_done, n + 1)
                nc.scalar.activation(qpad[:, n * BB:(n + 1) * BB, PAD:], m.ps[n][:, :].rearrange("p (b t) -> p b t", b=BB),
                                     ACT.Relu).then_inc(relu_done, 1)
            act.wait_ge(hm_done, 1)
            nc.scalar.copy(w["hebbian"], m.ps[5][:, 0:P]).then_inc(hm_copied, 1)
            act.wait_ge(hid_done, 1)
            nc.scalar.activation(hidden[:, :], m.ps[4][0:P // 2, 0:B], ACT.Gelu, bias=w["mn_b1"]).then_inc(gelu_done, 1)
            nc.scalar.preload_act_table_set(LOG_EXP)
            act.wait_ge(size_done, 1)
            nc.scalar.activation(tail[:, :], size[:, :], ACT.Exp, scale=-1.0).then_inc(act_done, 1)
            act.wait_ge(act_done, 1)
            nc.scalar.activation(tail[:, :], tail[:, :], ACT.Ln, bias=m.eps[:, 4:5]).then_inc(act_done, 1)

        @block.gpsimd
        def _(pool):
            for n in range(NBLK):
                pool.wait_ge(relu_done, n + 1)
                for b in range(n * BB, (n + 1) * BB):
                    nc.gpsimd.tensor_copy(qpad[:, b, 0:PAD], qpad[:, b, PAD:PAD + 1].to_broadcast([P, PAD]))

        @block.vector
        def _(dve):
            for n in range(NBLK):
                bs = slice(n * BB, (n + 1) * BB)
                dve.wait_ge(relu_done, n + 1)
                nc.vector.tensor_reduce(total[:, bs], qpad[:, bs, PAD:], AX.X, ALU.add).then_inc(sums, 1)
                nc.vector.tensor_reduce(every8[:, bs], qpad[:, bs, PAD:PAD + T:8], AX.X, ALU.add).then_inc(sums, 1)
            dve.wait_ge(sums, 2 * NBLK)
            nc.vector.tensor_scalar(every8[:, :], every8[:, :], 0.5 * 8 / T, None, ALU.mult).then_inc(sums, 1)
            dve.wait_ge(sums, 2 * NBLK + 1)
            nc.vector.scalar_tensor_tensor(sig[:, :], total[:, :], 1.0 / T, every8[:, :], ALU.mult, ALU.add).then_inc(sig_done, 1)
            nc.vector.scalar_tensor_tensor(base01[:, :], w["mn_b2"], 0.1, w["base_metric"], ALU.mult, ALU.add).then_inc(based, 1)
            dve.wait_ge(mod_done, 1)
            dve.wait_ge(based, 1)
            nc.vector.tensor_scalar(arg[:, :], m.ps[6][:, 0:B], 0.1, base01[:, :], ALU.mult, ALU.add).then_inc(arg_done, 1)
            dve.wait_ge(arg_done, 1)
            nc.vector.scalar_tensor_tensor(size[:, :], arg[:, :], -1.0, arg[:, :], ALU.mult, ALU.max).then_inc(size_done, 1)
            dve.wait_ge(act_done, 2)
            nc.vector.scalar_tensor_tensor(metric[:, :], arg[:, :], 0.0, tail[:, :], ALU.max, ALU.add).then_inc(arg_done, 1)
            dve.wait_ge(arg_done, 2)


def distance_attention(nc, m, w, z, qpad, metric):
    with ExitStack() as ctx:
        def sb(name, shape, n=2):
            return [ctx.enter_context(nc.sbuf_tensor(f"{name}{i}", shape, F32)) for i in range(n)]

        def tally(name, per=1, credit=0):
            return Tally(m.sem("b_" + name), per, credit)

        xp = sb("b_xp", [P, PAD + T])
        q2m, mk2 = sb("b_q2m", [P, T]), sb("b_mk2", [P, PAD + T])
        keys = [sb(f"b_keys{i}", [P, PAD + T]) for i in range(2)]
        lhs = [sb(f"b_lhs{i}", [P, NQT, HG, QT]) for i in range(2)]
        vwin = sb("b_vwin", [KT, NQT, NHEAD // HG, HALF + 1])
        qsq, n2c, inv, gate, heb, ctxt, outb = (sb("b_" + s, [P, T], 1)[0] for s in (
            "qsq", "n2c", "inv", "gate", "heb", "ctxt", "outb"))
        metric2 = sb("b_metric2", [P, B], 1)[0]
        top = [sb(f"b_top{r}_", [P, GT, 8]) for r in range(ROUNDS)]
        left, weight, dist = sb("b_left", [P, GT, KT]), sb("b_weight", [P, GT, KT]), sb("b_dist", [P, GT, KT])
        value, (spare, spare_act) = sb("b_value", [P, GT, KT]), sb("b_spare", [P, 12])
        weightT = sb("b_weightT", [KT, GT * P])
        rden, chead = sb("b_rden", [P, GT]), sb("b_chead", [P, GT, HALF])

        tallies = []

        def tally(name, units, per=1, credit=0):
            tallies.append(Tally(m, "b_" + name, units, per, credit))
            return tallies[-1]

        S, G = SEQ_PASS, SEQ_PASS * NG
        t_xp, t_q2m, t_mk2 = tally("xp", S, 2), tally("q2m", S), tally("mk2", S)
        t_keys, t_lhs, t_vps, t_vw = tally("keys", S, 4, 2), tally("lhs", S, 2, 2), tally("vps", S, 2, 2), tally("vw", S, 2, 1)
        t_qsq, t_nh, t_n2c, t_inv = tally("qsq", S), tally("nh", S, 1, 1), tally("n2c", S, 2), tally("inv", S, 2)
        t_heb, t_ctx, t_out, t_dec, t_x = (tally("heb", S, 2, 1), tally("ctx", S, 1, 1), tally("out", S),
                                           tally("dec", S, 1, 1), tally("x", S, 1, 1))
        t_score, t_top, t_taken, t_self = (tally("score", G, 1, NG + 1), tally("top", G, GT),
                                           tally("taken", G, GT), tally("self", G, GT))
        t_value, t_step = tally("value", G, 1, 2), m.sem("b_step")
        t_log, t_dist, t_infl, t_weight = tally("log", G), tally("dist", G), tally("infl", G), tally("weight", G, 1, 2)
        t_tr, t_wT, t_cx, t_rden, t_chead, t_cxT = (tally("tr", G, 1, 2), tally("wT", G, 1, 1), tally("cx", G, 1, 8),
                                                    tally("rden", G, 2), tally("chead", G, GT, 1), tally("cxT", G, 1, 2))
        b_score, b_v, b_tr, b_cx, b_cxT, b_nh, b_dec = [m.ps[0], m.ps[1]], m.ps[2], m.ps[3], m.ps[4], m.ps[5], m.ps[6], m.ps[7]

        def head_rows(hg):
            sq = slice(HALF * (1 - hg), HALF * (2 - hg))
            return sq, m.hmask[sq, :].unsqueeze(1).unsqueeze(3).to_broadcast([HALF, NQT, HG, QT])

        with nc.Block() as block:
            @block.gpsimd
            def _(pool):
                for i in range(2):
                    nc.gpsimd.memset(vwin[i][:, :, :, HALF:HALF + 1], 1.0)
                give_credit(pool, tallies)

            @block.scalar
            def _(act):
                sq, heads = head_rows(1)
                for i in range(2):
                    nc.scalar.activation(lhs[1][i][sq, :, :, :], heads, ACT.Copy, scale=-1.0)

            @block.vector
            def _(dve):
                nc.vector.tensor_scalar(metric2[:, :], metric[:, :], 2.0, None, ALU.mult)
                sq, heads = head_rows(0)
                for i in range(2):
                    nc.vector.tensor_scalar(lhs[0][i][sq, :, :, :], heads, -1.0, None, ALU.mult)

        block = ctx.enter_context(nc.Block())

        load_all(block, [(buf[:, :], a) for buf, a in m.later], m.sem("b_later"))

        def wait(eng, t, step, unit, j=None):
            eng.wait_ge(t.sem, t.done(step, unit, j))

        def column(a, b):
            return a[:, bass.ds(b, 1)]

        def queries(b, start=PAD, n=T):
            return qpad[:, bass.ds(b, 1), start:start + n].rearrange("p o t -> p (o t)")

        @block.gpsimd
        def _(pool):
            with pool.Fori(0, B // S) as step:
                for i in range(S):
                    b, k = step * S + i, i % 2
                    wait(pool, t_vps, step, i - 2)
                    nc.gpsimd.tensor_copy(xp[k][:, PAD:], z[:, bass.ds(b * T, T)]).then_inc(t_xp.sem, 1)
                    nc.gpsimd.tensor_copy(xp[k][:, 0:PAD], z[:, bass.ds(b * T, 1)].to_broadcast([P, PAD])).then_inc(t_xp.sem, 1)
                    wait(pool, t_q2m, step, i)
                    wait(pool, t_score, step, NG * (i - 1) - 1)
                    wait(pool, t_xp, step, i)
                    for hg in range(2):
                        own = slice(HALF * hg, HALF * (hg + 1))
                        nc.gpsimd.tensor_tensor(
                            lhs[hg][k][own, :, :, :],
                            q2m[k][own, :].rearrange("p (w q) -> p w q", q=QT).unsqueeze(2).to_broadcast([HALF, NQT, HG, QT]),
                            m.hmask[own, :].unsqueeze(1).unsqueeze(3).to_broadcast([HALF, NQT, HG, QT]),
                            ALU.mult).then_inc(t_lhs.sem, 1)
                    wait(pool, t_lhs, step, i)

        @block.tensor
        def _(pe):
            def scores(step, i, g):
                hg, w0 = g // (NG // 2), g % (NG // 2) * GT
                bank = b_score[g % 2]
                wait(pe, t_value, step, i * NG + g - 2)
                if g == 0:
                    wait(pe, t_keys, step, i)
                    wait(pe, t_lhs, step, i)
                for t in range(GT):
                    q0 = (w0 + t) * QT
                    nc.tensor.matmul(bank[:, t * KT:(t + 1) * KT], m.identb[:, :], m.band[:, :], start=True, stop=False)
                    mm = nc.tensor.matmul(bank[:, t * KT:(t + 1) * KT],
                                          lhs[hg][i % 2][:, w0 + t, :, :].rearrange("p h q -> p (h q)"),
                                          keys[hg][i % 2][:, q0:q0 + KT], start=False, stop=True)
                mm.then_inc(t_score.sem, 1)

            def values(step, i):
                wait(pe, t_xp, step, i)
                for half in range(2):
                    wait(pe, t_vw, step, i, half - 1)
                    for t in range(NQT // 2):
                        q0 = (half * (NQT // 2) + t) * QT
                        mm = nc.tensor.matmul(b_v[0:KT, t * P:(t + 1) * P], xp[i % 2][:, q0:q0 + KT],
                                              w["encoder_value"], start=True, stop=True)
                    mm.then_inc(t_vps.sem, 1)

            def transposes(step, unit):
                wait(pe, t_weight, step, unit)
                wait(pe, t_wT, step, unit - 1)
                for t in range(GT):
                    mm = nc.tensor.transpose(b_tr[0:KT, t * P:(t + 1) * P], weight[unit % 2][:, t, :], m.ident[:, :])
                mm.then_inc(t_tr.sem, 1)

            def contexts(step, unit):
                i, g = divmod(unit, NG)
                hg, w0 = g // (NG // 2), g % (NG // 2) * GT
                wait(pe, t_wT, step, unit)
                wait(pe, t_chead, step, unit - 1)
                if g == 0:
                    wait(pe, t_vw, step, i)
                for t in range(GT):
                    mm = nc.tensor.matmul(b_cx[:, t * P:t * P + HALF + 1], weightT[unit % 2][:, t * P:(t + 1) * P],
                                          vwin[i % 2][:, w0 + t, hg, :], start=True, stop=True)
                mm.then_inc(t_cx.sem, 1)

            def heads_together(step, unit):
                i, g = divmod(unit, NG)
                hg, w0 = g // (NG // 2), g % (NG // 2) * GT
                wait(pe, t_chead, step, unit)
                if g == 0:
                    wait(pe, t_ctx, step, i - 1)
                for t in range(GT):
                    q0 = (w0 + t) * QT
                    mm = nc.tensor.matmul(b_cxT[HALF * hg:HALF * (hg + 1), q0:q0 + QT], chead[unit % 2][:, t, :],
                                          m.qsel[:, :], start=True, stop=True)
                mm.then_inc(t_cxT.sem, 1)

            def sequence(step, i):
                values(step, i)
                wait(pe, t_qsq, step, i)
                wait(pe, t_heb, step, i - 1)
                nc.tensor.matmul(b_nh[:, 0:T], m.headsum[:, :], qsq[:, :], start=True, stop=True)
                nc.tensor.matmul(b_nh[:, T:2 * T], w["hebbian"], queries(step * S + i),
                                 start=True, stop=True).then_inc(t_nh.sem, 1)

            def decode(step, i):
                wait(pe, t_out, step, i)
                wait(pe, t_x, step, i - 1)
                nc.tensor.matmul(b_dec[:, 0:T], w["decoder"], outb[:, :], start=True, stop=True).then_inc(t_dec.sem, 1)

            with pe.Fori(0, B // S) as step:
                scores(step, 0, 0)
                scores(step, 0, 1)
                sequence(step, 0)
                for unit in range(G):
                    if unit + 2 < G:
                        scores(step, *divmod(unit + 2, NG))
                    transposes(step, unit)
                    if unit:
                        heads_together(step, unit - 1)
                    contexts(step, unit)
                    i, g = divmod(unit, NG)
                    if g == NG - 1 and i + 1 < S:
                        sequence(step, i + 1)
                    if g == 2 and i:
                        decode(step, i - 1)
                heads_together(step, G - 1)
                decode(step, S - 1)

        @block.scalar
        def _(act):
            def sequence_inputs(step, i):
                b = step * S + i
                wait(act, t_lhs, step, i - 2)
                nc.scalar.copy(spare_act[:, 2 * i:2 * i + 1], m.eps[:, 0:1])
                nc.scalar.activation(q2m[i % 2][:, :], queries(b), ACT.Copy, scale=column(metric2, b)).then_inc(t_q2m.sem, 1)
                wait(act, t_score, step, NG * (i - 1) - 1)
                wait(act, t_mk2, step, i)
                for hg in range(2):
                    own, sq = slice(HALF * hg, HALF * (hg + 1)), slice(HALF * (1 - hg), HALF * (2 - hg))
                    nc.scalar.copy(keys[hg][i % 2][own, :], qpad[own, bass.ds(b, 1), :].rearrange("p o t -> p (o t)")
                                   ).then_inc(t_keys.sem, 1)
                    nc.scalar.copy(keys[hg][i % 2][sq, :], mk2[i % 2][own, :]).then_inc(t_keys.sem, 1)
                wait(act, t_nh, step, i - 1)
                nc.scalar.copy(spare_act[:, 2 * i + 1:2 * i + 2], m.eps[:, 0:1])
                nc.scalar.activation(qsq[:, :], queries(b), ACT.Square).then_inc(t_qsq.sem, 1)

            def value_windows(step, i, half):
                wait(act, t_vps, step, i, half)
                wait(act, t_cx, step, i * NG - NG - 1)
                w0 = half * (NQT // 2)
                nc.scalar.activation(vwin[i % 2][:, w0:w0 + NQT // 2, :, 0:HALF],
                                     b_v[0:KT, :].rearrange("k (w g e) -> k w g e", w=NQT // 2, g=2),
                                     ACT.Relu).then_inc(t_vw.sem, 1)

            def copy_scores(step, unit):
                wait(act, t_score, step, unit)
                wait(act, t_weight, step, unit - 2)
                nc.scalar.copy(value[unit % 2][:, :, :], b_score[unit % 2][:, 0:GT * KT].rearrange("p (t k) -> p t k", t=GT)
                               ).then_inc(t_value.sem, 1)

            def distances(step, unit):
                d = dist[unit % 2]
                wait(act, t_weight, step, unit - 2)
                wait(act, t_value, step, unit)
                for t in range(GT):
                    wait(act, t_top, step, unit, t)
                    nc.scalar.activation(d[:, t, :], value[unit % 2][:, t, :], ACT.Identity,
                                         scale=-1.0, bias=top[0][unit % 2][:, t, 0:1]).then_inc(t_self.sem, 1)
                wait(act, t_self, step, unit)
                nc.scalar.activation(d[:, :, :], d[:, :, :], ACT.Ln, bias=m.eps[:, 2:3]).then_inc(t_log.sem, 1)
                wait(act, t_log, step, unit)
                nc.scalar.activation(d[:, :, :], d[:, :, :], ACT.Exp, scale=0.5).then_inc(t_dist.sem, 1)
                wait(act, t_dist, step, unit)
                nc.scalar.activation(d[:, :, :], d[:, :, :], ACT.Exp, scale=-1.0).then_inc(t_infl.sem, 1)

            def transposed(step, unit):
                wait(act, t_tr, step, unit)
                wait(act, t_cx, step, unit - 2)
                nc.scalar.copy(weightT[unit % 2][:, :], b_tr[0:KT, :]).then_inc(t_wT.sem, 1)

            def inverse_norms(step, i):
                wait(act, t_n2c, step, i, 0)
                wait(act, t_heb, step, i - 1)
                nc.scalar.activation(inv[:, :], n2c[:, :], ACT.Ln, scale=NORM_SCALE).then_inc(t_inv.sem, 1)
                wait(act, t_inv, step, i, 0)
                nc.scalar.activation(inv[:, :], inv[:, :], ACT.Exp, scale=-0.5, bias=m.eps[:, 3:4]).then_inc(t_inv.sem, 1)

            nc.scalar.preload_act_table_set(LOG_EXP)
            with act.Fori(0, B // S) as step:
                sequence_inputs(step, 0)
                copy_scores(step, 0)
                copy_scores(step, 1)
                distances(step, 0)
                value_windows(step, 0, 0)
                value_windows(step, 0, 1)
                for unit in range(G):
                    if unit + 1 < G:
                        distances(step, unit + 1)
                    transposed(step, unit)
                    i, g = divmod(unit, NG)
                    if g == 0 and i + 1 < S:
                        sequence_inputs(step, i + 1)
                    if unit + 2 < G:
                        copy_scores(step, unit + 2)
                    if g == NG - 1 and i + 1 < S:
                        value_windows(step, i + 1, 0)
                        value_windows(step, i + 1, 1)
                    if g == 1:
                        inverse_norms(step, i)

        @block.vector
        def _(dve):
            def squares(step, i):
                b = step * S + i
                wait(dve, t_keys, step, i - 2)
                all_q = qpad[:, bass.ds(b, 1), :].rearrange("p o t -> p (o t)")
                nc.vector.scalar_tensor_tensor(mk2[i % 2][:, :], all_q, column(metric, b), all_q,
                                               ALU.mult, ALU.mult).then_inc(t_mk2.sem, 1)

            def carry(j):
                nc.vector.memset(spare[:, j:j + 1], 0.0)

            def select(step, i, g):
                unit, k = i * NG + g, g % 2
                base = unit * 2 * GT * (ROUNDS - 1)
                for r in range(ROUNDS):
                    src = value[k] if r == 0 else left[k]
                    if r == 0:
                        wait(dve, t_value, step, unit)
                        carry(3 * (g % 4) + 0)
                    for t in range(GT):
                        if r == 1 and t == 0:
                            wait(dve, t_taken, step, unit)
                            carry(3 * (g % 4) + 1)
                        elif r > 1:
                            dve.wait_ge(t_step, base + (2 * r - 3) * GT + t + 1)
                        ins = nc.vector.max(top[r][k][:, t, :], src[:, t, :])
                        ins.then_inc(t_top.sem, 1) if r == 0 else ins.then_inc(t_step, 1)
                    for t in range(GT):
                        if r == 0 and t == 0:
                            wait(dve, t_top, step, unit)
                            carry(3 * (g % 4) + 2)
                        elif r:
                            dve.wait_ge(t_step, base + (2 * r - 2) * GT + t + 1)
                        ins = nc.vector.match_replace(left[k][:, t, :], top[r][k][:, t, :], src[:, t, :], TAKEN)
                        ins.then_inc(t_taken.sem, 1) if r == 0 else ins.then_inc(t_step, 1)
                dve.wait_ge(t_step, base + 2 * GT * (ROUNDS - 1))
                wait(dve, t_infl, step, unit)
                wait(dve, t_tr, step, unit - 2)
                nc.vector.scalar_tensor_tensor(weight[k][:, :, :], left[k][:, :, :], TAKEN, dist[k][:, :, :],
                                               ALU.is_equal, ALU.mult).then_inc(t_weight.sem, 1)

            def normalise(step, unit):
                k = unit % 2
                cx = b_cx[:, :].rearrange("p (t e) -> p t e", t=GT)
                wait(dve, t_cx, step, unit)
                nc.vector.tensor_scalar(rden[k][:, :], cx[:, :, HALF], 1e-8, None, ALU.add).then_inc(t_rden.sem, 1)
                wait(dve, t_rden, step, unit, 0)
                nc.vector.reciprocal(rden[k][:, :], rden[k][:, :]).then_inc(t_rden.sem, 1)
                wait(dve, t_rden, step, unit)
                wait(dve, t_cxT, step, unit - 2)
                for t in range(GT):
                    nc.vector.scalar_tensor_tensor(chead[k][:, t, :], cx[:, t, 0:HALF], rden[k][:, t:t + 1], m.omask[:, :],
                                                   ALU.mult, ALU.mult).then_inc(t_chead.sem, 1)

            def norms(step, i):
                wait(dve, t_nh, step, i)
                nc.vector.tensor_scalar(n2c[:, :], b_nh[:, 0:T], 1e-24, None, ALU.max).then_inc(t_n2c.sem, 1)
                nc.vector.tensor_scalar(gate[:, :], b_nh[:, 0:T], GATE2, 0.1, ALU.is_gt, ALU.mult).then_inc(t_n2c.sem, 1)

            def hebbian(step, i):
                wait(dve, t_n2c, step, i)
                wait(dve, t_inv, step, i)
                nc.vector.tensor_tensor(gate[:, :], gate[:, :], inv[:, :], ALU.mult).then_inc(t_heb.sem, 1)
                wait(dve, t_heb, step, i, 0)
                nc.vector.tensor_tensor(heb[:, :], b_nh[:, T:2 * T], gate[:, :], ALU.mult).then_inc(t_heb.sem, 1)

            def finish(step, i):
                b = step * S + i
                wait(dve, t_cxT, step, i * NG + NG - 1)
                wait(dve, t_heb, step, i)
                nc.vector.tensor_tensor(ctxt[:, :], b_cxT[:, 0:T], heb[:, :], ALU.add).then_inc(t_ctx.sem, 1)
                wait(dve, t_ctx, step, i)
                wait(dve, t_dec, step, i - 1)
                nc.vector.tensor_tensor(outb[:, :], ctxt[:, :], queries(b), ALU.mult).then_inc(t_out.sem, 1)

            def residual(step, i):
                here = m.x[:, bass.ds((step * S + i) * T, T)]
                wait(dve, t_dec, step, i)
                nc.vector.tensor_tensor(here, here, b_dec[:, 0:T], ALU.add).then_inc(t_x.sem, 1)

            with dve.Fori(0, B // S) as step:
                squares(step, 0)
                for unit in range(G):
                    i, g = divmod(unit, NG)
                    if g == 0 and i + 1 < S:
                        squares(step, i + 1)
                    select(step, i, g)
                    if unit:
                        normalise(step, unit - 1)
                    if g == 1 and i:
                        finish(step, i - 1)
                    if g == 1:
                        norms(step, i)
                    if g == 2:
                        hebbian(step, i)
                    if g == NG - 1 and i:
                        residual(step, i - 1)
                normalise(step, G - 1)
                finish(step, S - 1)
                residual(step, S - 1)
                dve.wait_ge(t_step, G * 2 * GT * (ROUNDS - 1))
                dve.sem_clear(t_step)


def distance_layer(nc, m, dram):
    with ExitStack() as ctx:
        def sb(name, shape):
            return ctx.enter_context(nc.sbuf_tensor(name, shape, F32))

        w = dict(m.weights["L0_attn_"], hebbian=sb("w_hebbian", [P, P])[:, :])
        z, qpad, metric = sb("a_z", [P, NT]), sb("a_qpad", [P, B, PAD + T]), sb("a_metric", [P, B])
        layernorm(nc, m, "ln0", m.x, z)
        distance_queries(nc, m, w, z, qpad, metric)
        distance_attention(nc, m, w, z, qpad, metric)



UNROLL = 16
PAIRS = UNROLL // 2
OGRP = 8


def delta_inputs(nc, m, w, z, pT, kT, gT, fT, qT, vT):
    with ExitStack() as ctx:
        def sb(name, shape):
            return ctx.enter_context(nc.sbuf_tensor(name, shape, F32))

        def sem(name):
            return m.sem(name)

        kraw, beta, f = sb("d_kraw", [P, NT]), sb("d_beta", [P, NT]), sb("d_f", [P, NT])
        f1 = sb("d_f1", [HD, NT])
        ksq, rk, kn = sb("d_ksq", [P, NT]), sb("d_rk", [P, NT]), sb("d_kn", [P, NT])
        kf, kkf, bk = sb("d_kf", [P, NT]), sb("d_kkf", [P, NT]), sb("d_bk", [P, NT])
        qkv_done, silu_done, f1_done, f1_copied, f2_done, beta_done, sig_done = map(
            sem, ("d_qkv", "d_silu", "d_f1d", "d_f1c", "d_f2", "d_bd", "d_sig"))
        ksq_done, knorm_done, s_done, dch, kkf_done, rk_log, rk_done, normed, decays, scaled = map(
            sem, ("d_sq", "d_kno", "d_s", "d_ch", "d_kkfd", "d_rklog", "d_rkd", "d_normed", "d_decays", "d_scaled"))
        block = ctx.enter_context(nc.Block())

        def tb(a, n):
            return a[:, cols(n)].rearrange("p (b t) -> p b t", b=BB)

        def bt(a, n):
            return a[:, 0:T, n * BB:(n + 1) * BB].rearrange("p t b -> p b t")

        @block.tensor
        def _(pe):
            for n in range(NBLK):
                for j, name in enumerate(("Wq", "Wk", "Wv")):
                    if 3 * n + j >= 6:
                        pe.wait_ge(silu_done, 3 * n + j - 5)
                    nc.tensor.matmul(m.ps[(3 * n + j) % 6][:, :], w[name], z[:, cols(n)],
                                     start=True, stop=True).then_inc(qkv_done, 1)
            for n in range(NBLK):
                if n >= 2:
                    pe.wait_ge(f1_copied, n - 1)
                nc.tensor.matmul(m.ps[6 + n % 2][0:HD, :], w["Wf1"], z[:, cols(n)],
                                 start=True, stop=True).then_inc(f1_done, 1)
            for n in range(NBLK):
                pe.wait_ge(silu_done, 3 * NBLK)
                pe.wait_ge(f1_copied, n + 1)
                if n >= 2:
                    pe.wait_ge(sig_done, 2 * (n - 1))
                nc.tensor.matmul(m.ps[n % 2][:, :], w["Wf2"], f1[:, cols(n)],
                                 start=True, stop=True).then_inc(f2_done, 1)
                nc.tensor.matmul(m.ps[2 + n % 2][:, :], w["Wbeta"], z[:, cols(n)],
                                 start=True, stop=True).then_inc(beta_done, 1)
            for n in range(NBLK):
                pe.wait_ge(ksq_done, n + 1)
                pe.wait_ge(sig_done, 2 * NBLK)
                nc.tensor.matmul(m.ps[n][:, :], m.headsum[:, :], ksq[:, cols(n)],
                                 start=True, stop=True).then_inc(knorm_done, 1)
            for n in range(NBLK):
                pe.wait_ge(kkf_done, n + 1)
                nc.tensor.matmul(m.ps[NBLK + n][:, :], m.headsum[:, :], kkf[:, cols(n)],
                                 start=True, stop=True).then_inc(s_done, 1)

        @block.scalar
        def _(act):
            for n in range(NBLK):
                for j, out in enumerate((bt(qT, n), tb(kraw, n), bt(vT, n))):
                    act.wait_ge(qkv_done, 3 * n + j + 1)
                    nc.scalar.activation(out, m.ps[(3 * n + j) % 6][:, :].rearrange(
                        "p (b t) -> p b t", b=BB), ACT.Silu).then_inc(silu_done, 1)
                act.wait_ge(silu_done, 3 * n + 2)
                nc.scalar.activation(ksq[:, cols(n)], kraw[:, cols(n)], ACT.Square).then_inc(ksq_done, 1)
            for n in range(NBLK):
                act.wait_ge(f1_done, n + 1)
                nc.scalar.copy(f1[:, cols(n)], m.ps[6 + n % 2][0:HD, :]).then_inc(f1_copied, 1)
            for n in range(NBLK):
                act.wait_ge(f2_done, n + 1)
                nc.scalar.activation(f[:, cols(n)], m.ps[n % 2][:, :], ACT.Sigmoid).then_inc(sig_done, 1)
                act.wait_ge(beta_done, n + 1)
                nc.scalar.activation(beta[:, cols(n)], m.ps[2 + n % 2][:, :], ACT.Sigmoid).then_inc(sig_done, 1)
            nc.scalar.preload_act_table_set(LOG_EXP)
            for n in range(NBLK):
                act.wait_ge(knorm_done, n + 1)
                nc.scalar.activation(rk[:, cols(n)], m.ps[n][:, :], ACT.Ln, bias=m.eps[:, 1:2]).then_inc(rk_log, 1)
                act.wait_ge(rk_log, n + 1)
                nc.scalar.activation(rk[:, cols(n)], rk[:, cols(n)], ACT.Exp, scale=-0.5).then_inc(rk_done, 1)

        @block.vector
        def _(dve):
            dve.wait_ge(sig_done, 2 * NBLK)
            for n in range(NBLK):
                c = cols(n)
                dve.wait_ge(rk_done, n + 1)
                nc.vector.tensor_tensor(kn[:, c], kraw[:, c], rk[:, c], ALU.mult).then_inc(normed, 1)
                dve.wait_ge(normed, n + 1)
                nc.vector.tensor_tensor(kf[:, c], kn[:, c], f[:, c], ALU.mult).then_inc(decays, 1)
                dve.wait_ge(decays, n + 1)
                nc.vector.tensor_tensor(kkf[:, c], kn[:, c], kf[:, c], ALU.mult).then_inc(kkf_done, 1)
                nc.vector.scalar_tensor_tensor(bk[:, c], kn[:, c], 2.0, beta[:, c], ALU.mult, ALU.mult).then_inc(scaled, 1)
            for n in range(NBLK):
                c, base = cols(n), 2 * n
                nc.vector.scalar_tensor_tensor(bt(gT, n), tb(kf, n), -2.0, tb(beta, n), ALU.mult, ALU.mult)
                dve.wait_ge(s_done, n + 1)
                dve.wait_ge(scaled, n + 1)
                nc.vector.tensor_tensor(bk[:, c], m.ps[NBLK + n][:, :], bk[:, c], ALU.mult).then_inc(dch, 1)
                dve.wait_ge(dch, base + 1)
                nc.vector.tensor_tensor(bk[:, c], bk[:, c], kf[:, c], ALU.subtract).then_inc(dch, 1)
                dve.wait_ge(dch, base + 2)
                nc.vector.scalar_tensor_tensor(bt(pT, n), tb(bk, n), 2.0, tb(beta, n), ALU.mult, ALU.mult)

        @block.gpsimd
        def _(pool):
            for n in range(NBLK):
                pool.wait_ge(sig_done, 2 * n + 1)
                nc.gpsimd.tensor_copy(bt(fT, n), tb(f, n))
            for n in range(NBLK):
                pool.wait_ge(normed, n + 1)
                nc.gpsimd.tensor_copy(bt(kT, n), tb(kn, n))


def delta_pairs(nc, m, pre_p, pre_k, post_k, g, f, q, q_dot):
    HALFT = T // 2
    with ExitStack() as ctx:
        def sb(name):
            return ctx.enter_context(nc.sbuf_tensor(name, [P, HALFT, B], F32))

        prod = [sb(f"p_prod{j}") for j in range(4)]
        part = [sb(f"p_part{j}") for j in range(4)]
        prod_done, dot_done, step_done, copied, f_done, qdot_done = (m.sem("p_" + n) for n in (
            "prod", "dot", "step", "copied", "f", "qdot"))
        block = ctx.enter_context(nc.Block())

        def even(a):
            return a[:, 0:T:2, :]

        def odd(a):
            return a[:, 1:T:2, :]

        def flat(a, n):
            return a[:, :, :].rearrange("p t b -> p (t b)")[:, cols(n)]

        def dot(j):
            return m.psum[:, j * 2 * BLK:(j + 1) * 2 * BLK].rearrange("p (t b) -> p t b", b=B)

        @block.tensor
        def _(pe):
            for j in range(4):
                pe.wait_ge(prod_done, j + 1)
                for n in range(2):
                    mm = nc.tensor.matmul(m.ps[2 * j + n][:, :], m.headsum[:, :], flat(prod[j], n), start=True, stop=True)
                mm.then_inc(dot_done, 1)

        @block.scalar
        def _(act):
            nc.scalar.copy(odd(post_k), odd(pre_k)).then_inc(copied, 1)
            act.wait_ge(step_done, 2)
            nc.scalar.copy(even(f), part[2][:, :, :]).then_inc(f_done, 1)

        @block.gpsimd
        def _(pool):
            nc.gpsimd.tensor_tensor(part[0][:, :, :], odd(f), even(pre_k), ALU.mult).then_inc(qdot_done, 1)
            nc.gpsimd.tensor_tensor(part[1][:, :, :], odd(f), even(g), ALU.mult).then_inc(qdot_done, 1)
            nc.gpsimd.tensor_tensor(even(q_dot), even(q), even(pre_k), ALU.mult).then_inc(qdot_done, 1)
            nc.gpsimd.tensor_tensor(odd(q_dot), even(q), even(g), ALU.mult).then_inc(qdot_done, 1)

        @block.vector
        def _(dve):
            for j, (a1, a0) in enumerate(((pre_p, pre_k), (pre_p, g), (pre_k, pre_k), (pre_k, g))):
                nc.vector.tensor_tensor(prod[j][:, :, :], odd(a1), even(a0), ALU.mult).then_inc(prod_done, 1)
            dve.wait_ge(prod_done, 4)
            nc.vector.tensor_tensor(odd(pre_p), odd(pre_p), even(f), ALU.mult)
            dve.wait_ge(copied, 1)
            nc.vector.tensor_tensor(odd(pre_k), odd(pre_k), even(f), ALU.mult)
            nc.vector.tensor_tensor(part[2][:, :, :], even(f), odd(f), ALU.mult).then_inc(step_done, 1)
            dve.wait_ge(step_done, 1)
            dve.wait_ge(qdot_done, 4)
            nc.vector.tensor_tensor(odd(f), even(f), even(q), ALU.mult).then_inc(step_done, 1)
            count = 2
            for c, out in ((0, post_k), (1, g)):
                dve.wait_ge(dot_done, c + 3)
                nc.vector.tensor_tensor(prod[c][:, :, :], dot(c), odd(post_k), ALU.mult).then_inc(step_done, 1)
                nc.vector.tensor_tensor(prod[2 + c][:, :, :], dot(2 + c), odd(g), ALU.mult).then_inc(step_done, 1)
                dve.wait_ge(step_done, count + 2)
                if c == 0:
                    dve.wait_ge(f_done, 1)
                nc.vector.tensor_tensor(part[2 + c][:, :, :], prod[c][:, :, :], prod[2 + c][:, :, :],
                                        ALU.add).then_inc(step_done, 1)
                dve.wait_ge(step_done, count + 3)
                nc.vector.tensor_tensor(even(out), part[c][:, :, :], part[2 + c][:, :, :], ALU.add)
                count += 3


def delta_scan(nc, m, pre_p, pre_k, post_k, g, f, q, q_dot, vT, ost):
    W = B * HD
    with ExitStack() as ctx:
        def ring(name, slots, n=2):
            return [ctx.enter_context(nc.sbuf_tensor(f"r_{name}{i}", [P, slots, B, HD], F32)) for i in range(n)]

        state, state_p, state_k = ring("state", 1), ring("statep", 2), ring("statek", 2)
        terms = ring("terms", 6, 4)
        q_state, q_term, q_sum, v_spread = ring("qstate", 1), ring("qterm", 2), ring("qsum", 1), ring("vspread", 2)
        (s_state, s_statep, s_statek, s_terms, s_decayed, s_qstate, s_qterm, s_qsum,
         s_vspread, s_u, s_w, s_out, s_outcopied, s_preset) = (m.sem("r_" + n) for n in (
             "state", "statep", "statek", "terms", "decayed", "qstate", "qterm", "qsum",
             "vspread", "u", "w", "out", "outcopied", "preset"))
        sums = [m.psum[:, i * 2 * BLK:(i + 1) * 2 * BLK].rearrange("p (s c) -> p s c", s=2) for i in range(2)]
        o_ps = [m.ps[4], m.ps[5]]
        block = ctx.enter_context(nc.Block())

        def slot(a, j):
            return a[:, j, :, :].rearrange("p b j -> p (b j)")

        def pair(a):
            return a[:, :, :, :].rearrange("p s b j -> p (s b) j")

        def twice(a):
            return a[:, 0, :, :].unsqueeze(1).to_broadcast([P, 2, B, HD])

        def coef(a, r, first=0, n=2):
            return a[:, bass.ds(r * 2 + first, n), :].unsqueeze(3).to_broadcast([P, n, B, HD])

        def sum_pair(i, j):
            return sums[i][:, j, 0:2 * W].rearrange("p (s b j) -> p s b j", s=2, b=B)

        vmask2 = m.vmask[:, :].unsqueeze(1).to_broadcast([P, 2 * B, HD])

        def spread_v(r, i):
            nc.gpsimd.tensor_tensor(pair(v_spread[i]), vmask2,
                                    vT[:, bass.ds(r * 2, 2), :].rearrange("p s b -> p (s b)").unsqueeze(2).to_broadcast(
                                        [P, 2 * B, HD]), ALU.mult).then_inc(s_vspread, 1)

        @block.vector
        def _(dve):
            def ahead(r, i):
                p_coef = coef(pre_p, r)
                dve.wait_ge(s_state, r + 1)
                nc.vector.tensor_tensor(state_p[i][:, :, :, :], twice(state[i]), p_coef, ALU.mult).then_inc(s_statep, 1)
                nc.vector.tensor_tensor(state_k[i][:, :, :, :], twice(state[i]), coef(pre_k, r), ALU.mult).then_inc(s_statek, 1)

            nc.vector.memset(state[0][:, :, :, :], 0.0).then_inc(s_state, 1)
            nc.vector.memset(o_ps[1][:, :], 0.0).then_inc(s_outcopied, 1)
            nc.vector.memset(q_term[1][:, :, :, :], 0.0).then_inc(s_qterm, 1)
            ahead(0, 0)
            with dve.Fori(0, T // UNROLL) as step:
                for v in range(PAIRS):
                    i, r = v % 2, step * PAIRS + v
                    dve.wait_ge(s_decayed, r + 1)
                    dve.wait_ge(s_u, r + 1)
                    nc.vector.tensor_tensor(terms[v % 4][:, 0:2, :, :], sum_pair(i, 0), coef(post_k, r), ALU.mult)
                    dve.wait_ge(s_w, r + 1)
                    nc.vector.tensor_tensor(terms[v % 4][:, 2:4, :, :], sum_pair(i, 1), coef(g, r), ALU.mult).then_inc(s_terms, 1)
                    dve.wait_ge(s_terms, r + 1)
                    nc.vector.tensor_reduce(slot(state[1 - i], 0),
                                            terms[v % 4][:, 0:5, :, :].rearrange("p s b j -> p (b j) s"),
                                            AX.X, ALU.add).then_inc(s_state, 1)
                    ahead(r + 1, 1 - i)
                    nc.vector.tensor_tensor(q_term[i][:, :, :, :],
                                            sums[i][:, :, 0:W].rearrange("p s (b j) -> p s b j", b=B),
                                            coef(q_dot, r), ALU.mult).then_inc(s_qterm, 1)

        @block.gpsimd
        def _(pool):
            def decay(r, v, i):
                nc.gpsimd.tensor_tensor(terms[v % 4][:, 4:6, :, :], twice(state[i]), coef(f, r), ALU.mult).then_inc(s_decayed, 1)

            nc.gpsimd.memset(terms[3][:, 5, :, :], 0.0).then_inc(s_preset, 1)
            nc.gpsimd.memset(q_state[1][:, :, :, :], 0.0).then_inc(s_qstate, 1)
            nc.gpsimd.memset(q_sum[1][:, :, :, :], 0.0).then_inc(s_qsum, 1)
            spread_v(0, 0)
            pool.wait_ge(s_state, 1)
            decay(0, 0, 0)
            spread_v(1, 1)
            with pool.Fori(0, T // UNROLL) as step:
                for v in range(PAIRS):
                    i, r = v % 2, step * PAIRS + v
                    pool.wait_ge(s_state, r + 2)
                    decay(r + 1, v + 1, 1 - i)
                    nc.gpsimd.tensor_tensor(q_state[i][:, 0, :, :], state[1 - i][:, 0, :, :],
                                            q[:, bass.ds(r * 2 + 1, 1), :].rearrange("p o b -> p (o b)").unsqueeze(2)
                                            .to_broadcast([P, B, HD]), ALU.mult).then_inc(s_qstate, 1)
                    spread_v(r + 2, i)
                    pool.wait_ge(s_qterm, r + 2)
                    nc.gpsimd.tensor_tensor(q_sum[i][:, 0, :, :], q_term[i][:, 0, :, :], q_term[i][:, 1, :, :],
                                            ALU.add).then_inc(s_qsum, 1)

        @block.tensor
        def _(pe):
            def output(v):
                half, col = v % PAIRS // (OGRP // 2), v % (OGRP // 2) * 2 * NHEAD
                first = o_ps[half][:, col:col + NHEAD]
                nc.tensor.matmul(first, slot(terms[v % 4], 5), m.headsel[:, :], start=True, stop=False)
                nc.tensor.matmul(first, slot(q_sum[v % 2], 0), m.headsel[:, :], start=False, stop=True)
                nc.tensor.matmul(o_ps[half][:, col + NHEAD:col + 2 * NHEAD], slot(q_state[v % 2], 0), m.headsel[:, :],
                                 start=True, stop=True).then_inc(s_out, 1)

            def values(i):
                nc.tensor.matmul(sums[i][:, 0, 0:2 * W], m.headsum[:, :], pair(v_spread[i]).rearrange("p s j -> p (s j)"),
                                 start=True, stop=False)

            pe.wait_ge(s_vspread, 1)
            values(0)
            pe.wait_ge(s_preset, 1)
            with pe.Fori(0, T // UNROLL) as step:
                for v in range(PAIRS):
                    i, r = v % 2, step * PAIRS + v
                    pe.wait_ge(s_statep, r + 1)
                    nc.tensor.matmul(sums[i][:, 0, 0:2 * W], m.headsum[:, :], pair(state_p[i]).rearrange("p s j -> p (s j)"),
                                     start=False, stop=True).then_inc(s_u, 1)
                    pe.wait_ge(s_statek, r + 1)
                    nc.tensor.matmul(sums[i][:, 1, 0:2 * W], m.headsum[:, :], pair(state_k[i]).rearrange("p s j -> p (s j)"),
                                     start=True, stop=True).then_inc(s_w, 1)
                    pe.wait_ge(s_vspread, r + 2)
                    pe.wait_ge(s_qterm, r + 1)
                    values(1 - i)
                    pe.wait_ge(s_qstate, r + 1)
                    pe.wait_ge(s_qsum, r + 1)
                    if v == 1:
                        pe.wait_ge(s_outcopied, step * 2 + 1)
                    if v == 1 + OGRP // 2:
                        pe.wait_ge(s_outcopied, step * 2 + 2)
                    output(v + PAIRS - 1)
            pe.wait_ge(s_statep, T // 2 + 1)
            nc.tensor.matmul(sums[0][:, 0, 0:2 * W], m.headsum[:, :], pair(state_p[0]).rearrange("p s j -> p (s j)"),
                             start=False, stop=True)
            pe.wait_ge(s_qstate, T // 2 + 1)
            pe.wait_ge(s_qsum, T // 2 + 1)
            output(PAIRS - 1)

        @block.scalar
        def _(act):
            def copy_out(half, t):
                nc.scalar.copy(ost[:, :, bass.ds(t, OGRP)],
                               o_ps[half][:, 0:OGRP * NHEAD].rearrange("p (t h) -> p h t", t=OGRP)).then_inc(s_outcopied, 1)

            with act.Fori(0, T // UNROLL) as step:
                act.wait_ge(s_out, step * PAIRS + 1)
                copy_out(1, step * UNROLL)
                act.wait_ge(s_out, step * PAIRS + (1 + OGRP // 2))
                copy_out(0, step * UNROLL + OGRP)
            act.wait_ge(s_out, T // 2 + 1)
            copy_out(1, T)


def delta_outputs(nc, m, w, z, ost, o_dram):
    with ExitStack() as ctx:
        def sb(name, shape):
            return ctx.enter_context(nc.sbuf_tensor(name, shape, F32))

        def sem(name):
            return m.sem(name)

        oT, sg, g1 = sb("e_oT", [P, NT]), sb("e_sg", [P, NT]), sb("e_g1", [HD, NT])
        ysq, ry = sb("e_ysq", [P, NT]), sb("e_ry", [P, NT])
        stored, loaded, g1_done, g1_copied, g2_done, sig_done, gated, squared, ms_done, dch, wo_done, ry_log, ry_done = map(
            sem, ("e_stored", "e_loaded", "e_g1d", "e_g1c", "e_g2", "e_sig", "e_gated", "e_sq", "e_ms", "e_dch",
                  "e_wo", "e_rylog", "e_ryd"))
        block = ctx.enter_context(nc.Block())

        @block.sync
        def _(sp):
            sp.dma_start(o_dram.rearrange("b j h t -> (b j) h t"), ost[:, :, OGRP:]).then_inc(stored, 16)
            sp.wait_ge(stored, 16)
            for h in range(NHEAD):
                sp.dma_start(oT[h * HD:(h + 1) * HD, :].rearrange("j (b t) -> j b t", b=B),
                             o_dram[:, :, h, :].rearrange("b j t -> j b t")).then_inc(loaded, 16)

        @block.tensor
        def _(pe):
            for n in range(NBLK):
                nc.tensor.matmul(m.ps[n][0:HD, :], w["Wog1"], z[:, cols(n)], start=True, stop=True).then_inc(g1_done, 1)
            for n in range(NBLK):
                pe.wait_ge(g1_copied, n + 1)
                nc.tensor.matmul(m.ps[4 + n][:, :], w["Wog2"], g1[:, cols(n)], start=True, stop=True).then_inc(g2_done, 1)
            for n in range(NBLK):
                pe.wait_ge(squared, n + 1)
                nc.tensor.matmul(m.ps[n][:, :], m.headavg[:, :], ysq[:, cols(n)], start=True, stop=True).then_inc(ms_done, 1)
            for n in range(NBLK):
                pe.wait_ge(dch, 2 * (n + 1))
                nc.tensor.matmul(m.ps[4 + n][:, :], w["Wo"], oT[:, cols(n)], start=True, stop=True).then_inc(wo_done, 1)

        @block.scalar
        def _(act):
            for n in range(NBLK):
                act.wait_ge(g1_done, n + 1)
                nc.scalar.copy(g1[:, cols(n)], m.ps[n][0:HD, :]).then_inc(g1_copied, 1)
            for n in range(NBLK):
                act.wait_ge(g2_done, n + 1)
                nc.scalar.activation(sg[:, cols(n)], m.ps[4 + n][:, :], ACT.Sigmoid).then_inc(sig_done, 1)
            nc.scalar.preload_act_table_set(LOG_EXP)
            for n in range(NBLK):
                act.wait_ge(gated, n + 1)
                nc.scalar.activation(ysq[:, cols(n)], oT[:, cols(n)], ACT.Square).then_inc(squared, 1)
            for n in range(NBLK):
                act.wait_ge(ms_done, n + 1)
                nc.scalar.activation(ry[:, cols(n)], m.ps[n][:, :], ACT.Ln, bias=m.eps[:, 1:2]).then_inc(ry_log, 1)
                act.wait_ge(ry_log, n + 1)
                nc.scalar.activation(ry[:, cols(n)], ry[:, cols(n)], ACT.Exp, scale=-0.5).then_inc(ry_done, 1)

        @block.vector
        def _(dve):
            dve.wait_ge(loaded, 16 * NHEAD)
            for n in range(NBLK):
                dve.wait_ge(sig_done, n + 1)
                nc.vector.tensor_tensor(oT[:, cols(n)], oT[:, cols(n)], sg[:, cols(n)], ALU.mult).then_inc(gated, 1)
            for n in range(NBLK):
                dve.wait_ge(gated, n + 1)
                dve.wait_ge(squared, n + 1)
                dve.wait_ge(ry_done, n + 1)
                nc.vector.tensor_tensor(oT[:, cols(n)], oT[:, cols(n)], ry[:, cols(n)], ALU.mult).then_inc(dch, 1)
                dve.wait_ge(dch, 2 * n + 1)
                nc.vector.tensor_scalar(oT[:, cols(n)], oT[:, cols(n)], w["norm_w"], None, ALU.mult).then_inc(dch, 1)
            for n in range(NBLK):
                dve.wait_ge(wo_done, n + 1)
                nc.vector.tensor_tensor(m.x[:, cols(n)], m.x[:, cols(n)], m.ps[4 + n][:, :], ALU.add)


def recurrence_layer(nc, m, dram):
    with ExitStack() as ctx:
        w = m.weights["L1_attn_"]
        z = ctx.enter_context(nc.sbuf_tensor("d_z", [P, NT], F32))
        pT, kT, gT, fT, qT, vT = (ctx.enter_context(nc.sbuf_tensor("d_" + n, [P, T + 4, B], F32))
                                  for n in ("pT", "kT", "gT", "fT", "qT", "vT"))

        def clear_ahead(pool):
            for a in (pT, kT, fT, vT):
                nc.gpsimd.memset(a[:, T:, :], 0.0)

        layernorm(nc, m, "ln5", m.x, z, pool_work=clear_ahead)
        delta_inputs(nc, m, w, z, pT, kT, gT, fT, qT, vT)
        ost = ctx.enter_context(nc.sbuf_tensor("d_ost", [P, NHEAD, OGRP + T], F32))
        post_k, q_dot = (ctx.enter_context(nc.sbuf_tensor("d_" + n, [P, T, B], F32)) for n in ("post_k", "q_dot"))
        delta_pairs(nc, m, pT, kT, post_k, gT, fT, qT, q_dot)
        delta_scan(nc, m, pT, kT, post_k, gT, fT, qT, q_dot, vT, ost)
        delta_outputs(nc, m, w, z, ost, dram["o_scratch"])


NEXP = 8
PARTS = 3
EXP_PASS = 4
TILES = NT // P


class ExpertWeights:

    def __init__(self, nc, ctx, m, name, up_dram, gate_dram, down_dram, width, shared=None):
        self.width, self.chunks, self.gelu, self.shared_dram = width, width // P, gate_dram is None, shared
        self.dram = (up_dram, down_dram, gate_dram)

        def sb(s, shape, n=2):
            return [ctx.enter_context(nc.sbuf_tensor(f"{name}_{s}{i}", shape, F32)) for i in range(n)]

        self.up, self.down = sb("up", [P, width]), sb("down", [P, self.chunks, P])
        self.first = self.up if self.gelu else sb("first", [P, width])
        self.loaded = [Tally(m, f"{name}_w{i}", EXP_PASS // 2, 16 * (2 if self.gelu else 3)) for i in range(2)]
        if shared:
            self.shared = [sb(f"s_{j}", shape, 1)[0] for j, shape in (
                ("first", [P, width // 2]), ("up", [P, width // 2]), ("down", [P, self.chunks // 2, P]))]
            self.shared_loaded = m.sem(name + "_sloaded")

    def load(self, sp, i, e):
        up_dram, down_dram, gate_dram = self.dram
        sp.dma_start(self.up[i][:, :], up_dram[e]).then_inc(self.loaded[i].sem, 16)
        if not self.gelu:
            sp.dma_start(self.first[i][:, :], gate_dram[e]).then_inc(self.loaded[i].sem, 16)
        sp.dma_start(self.down[i][:, :, :], down_dram[e].rearrange("(c p) h -> p c h", p=P)).then_inc(self.loaded[i].sem, 16)

    def load_first(self, sp):
        for i in range(2):
            self.load(sp, i, i)
        if self.shared_dram:
            first, up, down = self.shared_dram
            for dst, src in ((self.shared[0][:, :], first), (self.shared[1][:, :], up),
                             (self.shared[2][:, :, :], down.rearrange("(c p) h -> p c h", p=P))):
                sp.dma_start(dst, src).then_inc(self.shared_loaded, 16)


def route(nc, m, name, z, router, gatesT, weights):
    with ExitStack() as ctx:
        def sb(s, shape):
            return ctx.enter_context(nc.sbuf_tensor(f"{name}_{s}", shape, F32))

        prob, order, best = sb("prob", [P, TILES, NEXP]), sb("order", [P, TILES, NEXP]), sb("best", [P, TILES, NEXP])
        pick1, pick2, rest = sb("pick1", [P, TILES, NEXP]), sb("pick2", [P, TILES, NEXP]), sb("rest", [P, TILES, NEXP])
        top, total, first = sb("top", [P, TILES]), sb("total", [P, TILES]), sb("first", [P, TILES])
        parts = ctx.enter_context(nc.sbuf_tensor(f"{name}_parts", [P, TILES, PARTS, NEXP], BF16))
        logits_done, shifted, exped, chain, split_done, turned, turned_copied = (m.sem(f"{name}_{s}") for s in (
            "logits", "shifted", "exped", "chain", "split", "turned", "turnedc"))
        block = ctx.enter_context(nc.Block())

        @block.sync
        def _(sp):
            weights.load_first(sp)

        def wide(a):
            return a[:, :].unsqueeze(2).to_broadcast([P, TILES, NEXP])

        @block.tensor
        def _(pe):
            for t in range(TILES):
                mm = nc.tensor.matmul(m.ps[0][:, t * NEXP:(t + 1) * NEXP], z[:, cols(t, P)], router, start=True, stop=True)
            mm.then_inc(logits_done, 1)
            pe.wait_ge(split_done, 1)
            for n in range(NBLK):
                for t in range(BLK // P):
                    tile = n * (BLK // P) + t
                    mm = nc.tensor.matmul(m.ps[1 + n][0:PARTS * NEXP, cols(t, P)],
                                          parts[:, tile, :, :].rearrange("p a e -> p (a e)"), m.identb[:, :],
                                          start=True, stop=True)
                mm.then_inc(turned, 1)

        @block.scalar
        def _(act):
            act.wait_ge(shifted, 1)
            nc.scalar.activation(prob[:, :, :], prob[:, :, :], ACT.Exp).then_inc(exped, 1)
            for n in range(NBLK):
                act.wait_ge(turned, n + 1)
                nc.scalar.copy(gatesT[:, cols(n)], m.ps[1 + n][0:PARTS * NEXP, :]).then_inc(turned_copied, 1)

        @block.vector
        def _(dve):
            steps = [0]

            def then(ins):
                steps[0] += 1
                ins.then_inc(chain, 1)
                dve.wait_ge(chain, steps[0])

            logits = m.ps[0][:, 0:TILES * NEXP].rearrange("p (t e) -> p t e", t=TILES)
            weight = m.order[:, :].unsqueeze(1).to_broadcast([P, TILES, NEXP])
            dve.wait_ge(logits_done, 1)
            then(nc.vector.tensor_reduce(top[:, :], logits, AX.X, ALU.max))
            nc.vector.tensor_tensor(prob[:, :, :], logits, wide(top), ALU.subtract).then_inc(shifted, 1)
            dve.wait_ge(exped, 1)
            then(nc.vector.tensor_reduce(total[:, :], prob[:, :, :], AX.X, ALU.add))
            then(nc.vector.reciprocal(total[:, :], total[:, :]))
            then(nc.vector.tensor_tensor(prob[:, :, :], prob[:, :, :], wide(total), ALU.mult))

            def pick(source, out):
                then(nc.vector.tensor_reduce(top[:, :], source[:, :, :], AX.X, ALU.max))
                then(nc.vector.tensor_tensor(best[:, :, :], source[:, :, :], wide(top), ALU.is_equal))
                then(nc.vector.tensor_tensor(order[:, :, :], best[:, :, :], weight, ALU.mult))
                then(nc.vector.tensor_reduce(first[:, :], order[:, :, :], AX.X, ALU.max))
                then(nc.vector.tensor_tensor(out[:, :, :], order[:, :, :], wide(first), ALU.is_equal))

            pick(prob, pick1)
            then(nc.vector.scalar_tensor_tensor(rest[:, :, :], pick1[:, :, :], -2.0, prob[:, :, :], ALU.mult, ALU.add))
            pick(rest, pick2)
            then(nc.vector.tensor_tensor(pick1[:, :, :], pick1[:, :, :], pick2[:, :, :], ALU.add))
            then(nc.vector.tensor_tensor(rest[:, :, :], pick1[:, :, :], prob[:, :, :], ALU.mult))
            for part in range(PARTS):
                last = part == PARTS - 1
                ins = nc.vector.tensor_copy(parts[:, :, part, :], rest[:, :, :])
                if last:
                    ins.then_inc(split_done, 1)
                else:
                    then(ins)
                    then(nc.vector.tensor_tensor(rest[:, :, :], rest[:, :, :], parts[:, :, part, :], ALU.subtract))


def experts(nc, m, name, z, gatesT, w):
    C, gelu, shared = w.chunks, w.gelu, w.shared_dram is not None
    S = EXP_PASS * NBLK * C
    with ExitStack() as ctx:
        def sb(s, shape, n=2):
            return [ctx.enter_context(nc.sbuf_tensor(f"{name}_{s}{i}", shape, F32)) for i in range(n)]

        tallies = []

        def tally(s, units, per=1, credit=0):
            tallies.append(Tally(m, f"{name}_{s}", units, per, credit))
            return tallies[-1]

        chosen = [ctx.enter_context(nc.sbuf_tensor(f"{name}_chosen{i}", [PARTS * NEXP, P], BF16)) for i in range(EXP_PASS)]
        silu, hidden, gate, gated = sb("silu", [P, BLK]), sb("hidden", [P, BLK]), sb("gate", [P, BLK]), sb("gated", [P, BLK])
        t_w = w.loaded
        t_col = tally("col", EXP_PASS)
        t_first, t_second, t_silu, t_hidden, t_down = (tally("first_ps", S), tally("second_ps", S), tally("silu_done", S, 1, 2),
                                                       tally("hidden_done", S, 1, 2), tally("down_done", S, 1, 2))
        t_gps, t_gate, t_gated, t_acc = (tally("gate_ps", EXP_PASS * NBLK, 1, 1), tally("gate_done", EXP_PASS * NBLK, 1, 2),
                                         tally("gated_done", EXP_PASS * NBLK, 1, 2), tally("acc", EXP_PASS * NBLK, 1, 2))
        b_first, b_second, b_y, b_gate = m.ps[0:2], m.ps[2:4], m.ps[4:6], m.ps[6:8]
        NPASS = NEXP // EXP_PASS
        with nc.Block() as block:
            @block.gpsimd
            def _(pool):
                give_credit(pool, tallies)

        block = ctx.enter_context(nc.Block())

        def wait(eng, t, step, unit, j=None):
            eng.wait_ge(t.sem, t.done(step, unit, j))

        @block.sync
        def _(sp):
            for e in range(2, NEXP):
                step, i = divmod(e - 2, EXP_PASS)
                wait(sp, t_down, step, (i + 1) * NBLK * C - 1)
                w.load(sp, e % 2, e)

        def steps(experts_of_pass, chunks):
            return [(i, n, c) for i in experts_of_pass for n in range(NBLK) for c in range(chunks)]

        def pe_pass(pe, step, chunks, weights, gated_by):
            seq = steps(range(len(weights)), chunks)

            def down_product(k):
                i, n, c = seq[k]
                wait(pe, t_hidden, step, k)
                if c == 0:
                    wait(pe, t_gated, step, i * NBLK + n - 2)
                nc.tensor.matmul(b_y[n % 2][:, :], weights[i][2][:, c, :], hidden[k % 2][:, :],
                                 start=(c == 0), stop=(c == chunks - 1)).then_inc(t_down.sem, 1)

            for k, (i, n, c) in enumerate(seq):
                w_first, w_up, _ = weights[i]
                if c == 0 and gated_by:
                    if n == 0:
                        wait(pe, t_col, step, i)
                        wait(pe, t_w[i % 2], step, i // 2)
                    wait(pe, t_gate, step, i * NBLK + n - 2)
                    nc.tensor.matmul(b_gate[n % 2][:, :], chosen[i][:, :], gatesT[:, cols(n)],
                                     start=True, stop=True).then_inc(t_gps.sem, 1)
                wait(pe, t_silu if not gelu else t_hidden, step, k - 2)
                nc.tensor.matmul(b_first[k % 2][:, :], w_first[:, cols(c, P)], z[:, cols(n)],
                                 start=True, stop=True).then_inc(t_first.sem, 1)
                if not gelu:
                    wait(pe, t_hidden, step, k - 2)
                    nc.tensor.matmul(b_second[k % 2][:, :], w_up[:, cols(c, P)], z[:, cols(n)],
                                     start=True, stop=True).then_inc(t_second.sem, 1)
                if k:
                    down_product(k - 1)
            down_product(len(seq) - 1)

        def act_pass(act, step, chunks, n_experts, gated_by):
            for k, (i, n, c) in enumerate(steps(range(n_experts), chunks)):
                if c == 0 and gated_by:
                    unit = i * NBLK + n
                    wait(act, t_gps, step, unit)
                    wait(act, t_gated, step, unit - 2)
                    nc.scalar.copy(gate[n % 2][:, :], b_gate[n % 2][:, :]).then_inc(t_gate.sem, 1)
                wait(act, t_first, step, k)
                if gelu:
                    wait(act, t_down, step, k - 2)
                    nc.scalar.activation(hidden[k % 2][:, :], b_first[k % 2][:, :], ACT.Gelu).then_inc(t_hidden.sem, 1)
                else:
                    wait(act, t_hidden, step, k - 2)
                    nc.scalar.activation(silu[k % 2][:, :], b_first[k % 2][:, :], ACT.Silu).then_inc(t_silu.sem, 1)

        def dve_pass(dve, step, chunks, n_experts, gated_by):
            seq = steps(range(n_experts), chunks)

            def gated_block(i, n):
                unit = i * NBLK + n
                wait(dve, t_down, step, unit * chunks + chunks - 1)
                wait(dve, t_acc, step, unit - 2)
                if gated_by:
                    wait(dve, t_gate, step, unit)
                    nc.vector.tensor_tensor(gated[n % 2][:, :], b_y[n % 2][:, :], gate[n % 2][:, :],
                                            ALU.mult).then_inc(t_gated.sem, 1)
                else:
                    nc.vector.tensor_scalar(gated[n % 2][:, :], b_y[n % 2][:, :], SHARED_SCALE, None,
                                            ALU.mult).then_inc(t_gated.sem, 1)

            for k, (i, n, c) in enumerate(seq):
                if not gelu:
                    wait(dve, t_second, step, k)
                    wait(dve, t_silu, step, k)
                    wait(dve, t_down, step, k - 2)
                    nc.vector.tensor_tensor(hidden[k % 2][:, :], b_second[k % 2][:, :], silu[k % 2][:, :],
                                            ALU.mult).then_inc(t_hidden.sem, 1)
                if k >= chunks + 1 and (k - 1) % chunks == 0:
                    gated_block(*seq[k - chunks - 1][:2])
            gated_block(*seq[-1][:2])

        def pool_pass(pool, step, n_experts, columns):
            if columns:
                wait(pool, t_gps, step, -1)
                for i in range(n_experts):
                    nc.gpsimd.tensor_copy(chosen[i][:, :], m.rows[:, bass.ds((step * EXP_PASS + i) * P, P)]).then_inc(t_col.sem, 1)
            for i in range(n_experts):
                for n in range(NBLK):
                    unit = i * NBLK + n
                    wait(pool, t_gated, step, unit)
                    wait(pool, t_acc, step, unit - 1)
                    nc.gpsimd.tensor_tensor(m.x[:, cols(n)], m.x[:, cols(n)], gated[n % 2][:, :],
                                            ALU.add).then_inc(t_acc.sem, 1)

        in_pass = [(w.first[i % 2], w.up[i % 2], w.down[i % 2]) for i in range(EXP_PASS)]

        @block.tensor
        def _(pe):
            with pe.Fori(0, NPASS) as step:
                pe_pass(pe, step, C, in_pass, True)
            if shared:
                pe.wait_ge(w.shared_loaded, 16 * len(w.shared))
                pe_pass(pe, NPASS, C // 2, [w.shared], False)

        @block.scalar
        def _(act):
            nc.scalar.preload_act_table_set("gelu_and_others" if gelu else "silu_and_others")
            with act.Fori(0, NPASS) as step:
                act_pass(act, step, C, EXP_PASS, True)
            if shared:
                act_pass(act, NPASS, C // 2, 1, False)

        @block.vector
        def _(dve):
            with dve.Fori(0, NPASS) as step:
                dve_pass(dve, step, C, EXP_PASS, True)
            if shared:
                dve_pass(dve, NPASS, C // 2, 1, False)

        @block.gpsimd
        def _(pool):
            with pool.Fori(0, NPASS) as step:
                pool_pass(pool, step, EXP_PASS, True)
            if shared:
                pool_pass(pool, NPASS, 1, False)


SHARED_SCALE = 0.5


def mixture_layer(nc, m, dram):
    d = {k: dram["L1_ffn_" + k] for k in ("Wr", "Wg", "Wu", "Wd", "Sg", "Su", "Sd")}
    with ExitStack() as ctx:
        z = ctx.enter_context(nc.sbuf_tensor("f_z", [P, NT], F32))
        gates = ctx.enter_context(nc.sbuf_tensor("f_gates", [PARTS * NEXP, NT], BF16))
        layernorm(nc, m, "ln6", m.x, z)
        w = ExpertWeights(nc, ctx, m, "f", d["Wu"], d["Wg"], d["Wd"], d["Wg"].shape[2], (d["Sg"], d["Su"], d["Sd"]))
        route(nc, m, "f_route", z, m.weights["L1_ffn_"]["Wr"], gates, w)
        experts(nc, m, "f", z, gates, w)


AHD = 8


def sequence_attention(nc, m, w, z):
    with ExitStack() as ctx:
        def sb(s, shape):
            return ctx.enter_context(nc.sbuf_tensor("g_" + s, shape, F32))

        def sem(s):
            return m.sem("g_" + s)

        hn = sb("hn", [P, NT])
        q, k, v, attended = sb("q", [P, B, T]), sb("k", [P, B, T]), sb("v", [P, B, T]), sb("attended", [P, B, T])
        prod = [sb(f"prod{i}", [P, B, T]) for i in range(2)]
        prob, prob_v = ([sb(f"{name}{i}", [P, B, T]) for i in range(2)] for name in ("prob", "probv"))
        top, total = ([sb(f"{name}{i}", [P, T]) for i in range(2)] for name in ("top", "total"))
        layernorm(nc, m, "ln2", z, hn, w["ln1_w"], w["ln1_b"])
        qkv_done, qkv_copied, prods, scored, shifted, exped, weighted, chain, added, attn_done, proj_done, totalled, logged, inverted = map(
            sem, ("qkv", "qkvc", "prods", "scored", "shifted", "exped", "weighted", "chain", "added", "attn", "proj", "totalled", "logged",
                  "inverted"))
        block = ctx.enter_context(nc.Block())

        def flat(a):
            return a[:, :, :].rearrange("p b t -> p (b t)")

        def banks(s, n):
            half = 4 * (s % 2)
            return m.psum[:, half * BLK:half * BLK + n * T].rearrange("p (b t) -> p b t", b=n)

        @block.tensor
        def _(pe):
            for j in range(3):
                for n in range(NBLK):
                    u = j * NBLK + n
                    if u >= 8:
                        pe.wait_ge(qkv_copied, u - 7)
                    nc.tensor.matmul(m.ps[u % 8][:, :], w["in_proj_w"][:, cols(j, P)], hn[:, cols(n)],
                                     start=True, stop=True).then_inc(qkv_done, 1)
            for s in range(B):
                pe.wait_ge(prods, s + 1)
                if s < 2:
                    pe.wait_ge(qkv_copied, 3 * NBLK)
                else:
                    pe.wait_ge(shifted, s - 1)
                for c in range(0, s + 1, BB):
                    n = min(BB, s + 1 - c) * T
                    mm = nc.tensor.matmul(m.psum[:, (4 * (s % 2)) * BLK + c * T:(4 * (s % 2)) * BLK + c * T + n],
                                          m.headscale[:, :], flat(prod[s % 2])[:, c * T:c * T + n], start=True, stop=True)
                mm.then_inc(scored, 1)
            for n in range(NBLK):
                pe.wait_ge(attn_done, (n + 1) * BB)
                if n == 0:
                    pe.wait_ge(shifted, B)
                nc.tensor.matmul(m.ps[n][:, :], w["out_proj_w"], flat(attended)[:, cols(n)],
                                 start=True, stop=True).then_inc(proj_done, 1)

        @block.scalar
        def _(act):
            for j, out in enumerate((q, k, v)):
                for n in range(NBLK):
                    u = j * NBLK + n
                    act.wait_ge(qkv_done, u + 1)
                    nc.scalar.activation(flat(out)[:, cols(n)], m.ps[u % 8][:, :], ACT.Identity,
                                         bias=w["in_proj_b"][:, j:j + 1]).then_inc(qkv_copied, 1)
            nc.scalar.preload_act_table_set(LOG_EXP)
            def invert(s):
                sums = total[s % 2]
                act.wait_ge(totalled, s + 1)
                nc.scalar.activation(sums[:, :], sums[:, :], ACT.Ln).then_inc(logged, 1)
                act.wait_ge(logged, s + 1)
                nc.scalar.activation(sums[:, :], sums[:, :], ACT.Exp, scale=-1.0).then_inc(inverted, 1)

            for s in range(B):
                act.wait_ge(shifted, s + 1)
                nc.scalar.activation(prob[s % 2][:, 0:s + 1, :], prob[s % 2][:, 0:s + 1, :], ACT.Exp).then_inc(exped, 1)
                if s:
                    invert(s - 1)
            invert(B - 1)

        @block.gpsimd
        def _(pool):
            def products(s):
                if s >= 2:
                    pool.wait_ge(scored, s - 1)
                nc.gpsimd.tensor_tensor(prod[s % 2][:, 0:s + 1, :], k[:, 0:s + 1, :],
                                        q[:, s:s + 1, :].to_broadcast([P, s + 1, T]), ALU.mult).then_inc(prods, 1)

            pool.wait_ge(qkv_copied, 3 * NBLK)
            products(0)
            for s in range(B):
                if s + 1 < B:
                    products(s + 1)
                pool.wait_ge(exped, s + 1)
                if s >= 2:
                    pool.wait_ge(attn_done, s - 1)
                nc.gpsimd.tensor_tensor(prob_v[s % 2][:, 0:s + 1, :], prob[s % 2][:, 0:s + 1, :], v[:, 0:s + 1, :],
                                        ALU.mult).then_inc(weighted, 1)

        @block.vector
        def _(dve):
            steps = [0]

            def then(ins):
                steps[0] += 1
                ins.then_inc(chain, 1)
                dve.wait_ge(chain, steps[0])

            def shift(s):
                n = s + 1
                dve.wait_ge(scored, n)
                if s >= 2:
                    dve.wait_ge(weighted, s - 1)
                then(nc.vector.tensor_reduce(top[s % 2][:, :], banks(s, n).rearrange("p b t -> p t b"), AX.X, ALU.max))
                nc.vector.tensor_tensor(prob[s % 2][:, 0:n, :], banks(s, n),
                                        top[s % 2][:, :].unsqueeze(1).to_broadcast([P, n, T]), ALU.subtract).then_inc(shifted, 1)

            shift(0)
            for s in range(B):
                n = s + 1
                if n < B:
                    shift(n)
                dve.wait_ge(exped, n)
                nc.vector.tensor_reduce(total[s % 2][:, :], prob[s % 2][:, 0:n, :].rearrange("p b t -> p t b"),
                                        AX.X, ALU.add).then_inc(totalled, 1)
                dve.wait_ge(weighted, n)
                then(nc.vector.tensor_reduce(attended[:, s, :], prob_v[s % 2][:, 0:n, :].rearrange("p b t -> p t b"),
                                             AX.X, ALU.add))
                dve.wait_ge(inverted, n)
                nc.vector.tensor_tensor(attended[:, s, :], attended[:, s, :], total[s % 2][:, :], ALU.mult).then_inc(attn_done, 1)
            for n in range(NBLK):
                dve.wait_ge(proj_done, n + 1)
                nc.vector.scalar_tensor_tensor(z[:, cols(n)], m.ps[n][:, :], w["out_proj_b"], z[:, cols(n)],
                                               ALU.add, ALU.add).then_inc(added, 1)
            dve.wait_ge(added, NBLK)


def sequence_layer(nc, m, dram):
    with ExitStack() as ctx:
        w = m.weights["L0_ffn_"]
        z = ctx.enter_context(nc.sbuf_tensor("g_z", [P, NT], F32))
        gates = ctx.enter_context(nc.sbuf_tensor("g_gates", [PARTS * NEXP, NT], BF16))
        layernorm(nc, m, "ln1", m.x, z)
        sequence_attention(nc, m, w, z)

        def add_attended(pool):
            nc.gpsimd.tensor_tensor(m.x[:, :], m.x[:, :], z[:, :], ALU.add)

        hn2 = ctx.enter_context(nc.sbuf_tensor("g_hn2", [P, NT], F32))
        layernorm(nc, m, "ln3", z, hn2, w["ln2_w"], w["ln2_b"], add_attended)
        w1 = dram["L0_ffn_w1"]
        expert_weights = ExpertWeights(nc, ctx, m, "h", w1, None, dram["L0_ffn_w2"], w1.shape[2])
        route(nc, m, "g_route", hn2, w["router_w"], gates, expert_weights)
        experts(nc, m, "h", hn2, gates, expert_weights)


LAYERS = (distance_layer, sequence_layer, recurrence_layer, mixture_layer)

WEIGHTS = {
    "L0_attn_": ("encoder_query", "encoder_value", "mn_w1", "mn_b1", "mn_w2", "mn_b2", "base_metric", "decoder",
                 "hebbian_U", "hebbian_V"),
    "L0_ffn_": ("ln1_w", "ln1_b", "in_proj_w", "in_proj_b", "out_proj_w", "out_proj_b", "ln2_w", "ln2_b", "router_w"),
    "L1_attn_": ("Wq", "Wk", "Wv", "Wf1", "Wf2", "Wbeta", "Wog1", "Wog2", "Wo", "norm_w"),
    "L1_ffn_": ("Wr",),
}

CONSTS = ("centre", "avg", "headsum", "headavg", "headsel", "vmask", "ident", "band", "hmask", "omask", "qsel", "headscale", "order", "rows")


def program(nc, dram, stages):
    with ExitStack() as ctx:
        m = Mem(nc)
        m.x = ctx.enter_context(nc.sbuf_tensor("x", [P, NT], F32))
        m.psum = ctx.enter_context(nc.psum_tensor("banks", [P, 8 * BLK], F32))
        m.ps = [m.psum[:, cols(i)] for i in range(8)]
        loads, bufs, m.weights, m.later = [(m.x, dram["x"])], [], {}, []
        for name in CONSTS:
            a = dram[name]
            bufs.append(ctx.enter_context(nc.sbuf_tensor("c_" + name, list(a.shape), a.dtype)))
            loads.append((bufs[-1], a))
        for prefix, names in WEIGHTS.items():
            m.weights[prefix] = {}
            for name in names:
                a = dram[prefix + name]
                buf = ctx.enter_context(nc.sbuf_tensor("w_" + prefix + name, list(a.shape), F32))
                m.weights[prefix][name] = buf[:, :]
                first = prefix == "L0_attn_" or stages[0] is not distance_layer
                (loads if first else m.later).append((buf, a))
        (m.centre, m.avg, m.headsum, m.headavg, m.headsel, m.vmask, m.ident, m.band32, m.hmask, m.omask, m.qsel, m.headscale,
         m.order, m.rows) = bufs
        m.identb = ctx.enter_context(nc.sbuf_tensor("identb", [P, P], BF16))
        m.band = ctx.enter_context(nc.sbuf_tensor("band", [P, KT], BF16))
        m.eps = ctx.enter_context(nc.sbuf_tensor("eps", [P, 5], F32))
        loaded = m.sem("loaded")
        with nc.Block() as block:
            @block.gpsimd
            def _(pool):
                for i, eps in enumerate((1e-5, 1e-6, 1e-8, 0.5 * math.log(NORM_SCALE), 1.0)):
                    nc.gpsimd.memset(m.eps[:, i:i + 1], eps)

            load_all(block, [(buf[:, :], a) for buf, a in loads], loaded)
        with nc.Block() as block:
            @block.vector
            def _(dve):
                nc.vector.tensor_copy(m.identb[:, :], m.ident[:, :])
                nc.vector.tensor_copy(m.band[:, :], m.band32[:, :])
        for stage in stages:
            stage(nc, m, dram)
            m.release()
        stored = m.sem("stored")
        with nc.Block() as block:
            @block.sync
            def _(sp):
                sp.dma_start(dram["out"], m.x[:, :]).then_inc(stored, 16)
                sp.wait_ge(stored, 16)




def constants():
    part = np.arange(P)
    head = part // HD
    same = head[:, None] == head[None, :]
    key, query = np.arange(KT), part % QT
    inside = (key[None, :] > query[:, None]) & (key[None, :] <= query[:, None] + WIN)
    f = np.float32
    return {
        "centre": (np.eye(P) - 1.0 / P).astype(f),
        "avg": np.full((P, P), 1.0 / P, f),
        "headsum": same.astype(f),
        "headavg": same.astype(f) / f(HD),
        "headsel": (head[:, None] == np.arange(NHEAD)[None, :]).astype(f),
        "vmask": (part[:, None] % HD == np.arange(HD)[None, :]).astype(f),
        "ident": np.eye(P, dtype=f),
        "band": np.where(inside, 0.0, OUTSIDE).astype(f),
        "hmask": (head[:, None] % HG == np.arange(HG)[None, :]).astype(f),
        "omask": (part[:, None] // QT == np.arange(HALF)[None, :] // HD).astype(f),
        "headscale": ((part[:, None] // AHD == part[None, :] // AHD) / np.sqrt(AHD)).astype(f),
        "order": np.tile(np.arange(NEXP, 0, -1), (P, 1)).astype(f),
        "rows": (np.arange(3 * NEXP)[:, None] % NEXP == np.repeat(np.arange(NEXP), P)[None, :]).astype(f),
        "qsel": (query[:, None] == np.arange(QT)[None, :]).astype(f),
    }


def host_layout(inputs):
    a = {k: np.asarray(v) for k, v in inputs.items()}
    out = {"x": a["L0_attn_x"].reshape(NT, P).T}
    for name in ("encoder_query", "encoder_value"):
        out["L0_attn_" + name] = a["L0_attn_" + name].transpose(1, 0, 2).reshape(P, P)
    for name in ("mn_w1", "mn_w2", "decoder"):
        out["L0_attn_" + name] = a["L0_attn_" + name]
    for name in ("mn_b1", "mn_b2", "base_metric"):
        out["L0_attn_" + name] = a["L0_attn_" + name].reshape(-1, 1)
    u, v = a["L0_attn_hebbian_U"], a["L0_attn_hebbian_V"]
    rank = u.shape[2]
    for name in ("hebbian_U", "hebbian_V"):
        out["L0_attn_" + name] = np.zeros((NHEAD * rank, P), u.dtype)
    for h in range(NHEAD):
        rows, channels = slice(h * rank, (h + 1) * rank), slice(h * HD, (h + 1) * HD)
        out["L0_attn_hebbian_U"][rows, channels] = u[h].T
        out["L0_attn_hebbian_V"][rows, channels] = v[h]
    for name in ("ln1_w", "ln1_b", "out_proj_b", "ln2_w", "ln2_b"):
        out["L0_ffn_" + name] = a["L0_ffn_" + name].reshape(P, 1)
    out["L0_ffn_in_proj_b"] = a["L0_ffn_in_proj_b"].reshape(3, P).T
    for name in ("in_proj_w", "out_proj_w", "router_w"):
        out["L0_ffn_" + name] = a["L0_ffn_" + name].T
    for name in ("w1", "w2"):
        out["L0_ffn_" + name] = a["L0_ffn_" + name]
    for name in ("Wq", "Wk", "Wv", "Wf1", "Wf2", "Wog1", "Wog2", "Wo"):
        out["L1_attn_" + name] = a["L1_attn_" + name]
    out["L1_attn_Wbeta"] = np.repeat(a["L1_attn_Wbeta"], HD, axis=1)
    out["L1_attn_norm_w"] = a["L1_attn_norm_w"].reshape(P, 1)
    for name in ("Wr", "Wg", "Wu", "Wd", "Sg", "Su", "Sd"):
        out["L1_ffn_" + name] = a["L1_ffn_" + name]
    return {k: np.ascontiguousarray(v) for k, v in out.items()}


def kernel(**inputs):
    from concourse import bacc
    from concourse.bass_utils import run_bass_kernel_spmd

    nc = bacc.Bacc("TRN2", target_bir_lowering=False, num_devices=1)
    arrays = {**host_layout(inputs), **constants()}
    dram = {name: nc.dram_tensor("in_" + name, a.shape, mybir.dt.from_np(a.dtype), kind="ExternalInput").ap()
            for name, a in arrays.items()}
    dram["out"] = nc.dram_tensor("out", [P, NT], F32, kind="ExternalOutput").ap()
    dram["o_scratch"] = nc.dram_tensor("o_scratch", [B, HD, NHEAD, T], F32, kind="Internal").ap()
    program(nc, dram, LAYERS)
    r = run_bass_kernel_spmd(nc, [{"in_" + name: a for name, a in arrays.items()}], core_ids=[0])
    return np.ascontiguousarray(r.results[0]["out"].T).reshape(B, T, P)
```
